# Optimizing a Trainium2 kernel written in Bass

```python
import numpy as np
import jax
import jax.numpy as jnp

def _softmax(x, axis=-1):
    return jax.nn.softmax(x, axis=axis)

def _gelu(x):
    return jax.nn.gelu(x, approximate=True)

def _silu(x):
    return jax.nn.silu(x)

def _sigmoid(x):
    return jax.nn.sigmoid(x)

def _layernorm(x, axis=-1, eps=1e-05):
    m = jnp.mean(x, axis=axis, keepdims=True)
    v = jnp.var(x, axis=axis, keepdims=True)
    return (x - m) / jnp.sqrt(v + eps)

def _scatter_add(tgt, idx, src, axis=0):
    return tgt.at[idx].add(src)

def _segment_sum(src, seg, n):
    return jax.ops.segment_sum(src, seg, n)
kernel_name = 'mk_flamingo_gated_d1_seqx_r2_6286e2'

def setup_inputs(seed: int=0):
    np.random.seed(seed)
    _w = jnp.asarray

    def _rec_inputs():
        import jax
        import jax.numpy as jnp
        _rk = jax.random.key(seed)
        x = -0.000125 + 0.9999 * jax.random.normal(jax.random.fold_in(_rk, 1), (8, 224, 512), jnp.float32)
        _lenS = 224 - jax.random.randint(jax.random.fold_in(_rk, 7), (8,), 0, max(1, 224 // 4) + 1, jnp.int32)
        _lenS2 = 750 - jax.random.randint(jax.random.fold_in(_rk, 8), (8,), 0, max(1, 750 // 4) + 1, jnp.int32)
        _ctx_768P = jax.random.normal(jax.random.fold_in(_rk, 11), (8, 16, 384), jnp.float32)
        _ctx_768c = jax.random.dirichlet(jax.random.fold_in(_rk, 511), 0.3 * jnp.ones((16,), jnp.float32), (8, 750))
        _ctx_768t = jnp.einsum('bsk,bkd->bsd', _ctx_768c, _ctx_768P)
        _ctx_768t = _ctx_768t * jax.lax.rsqrt(jnp.mean(jnp.square(_ctx_768t)) + 1e-12) * 0.953939
        ctx_768 = 0.00272024 + 0.999456 * (_ctx_768t + 0.3 * jax.random.normal(jax.random.fold_in(_rk, 611), (8, 750, 384), jnp.float32))
        _g = jax.random.normal(jax.random.fold_in(_rk, 9001), (2, 1), jnp.float32)
        _g = jnp.sign(_g) * jnp.maximum(jnp.abs(_g), 1.0) + (_g == 0) * 1.0
        g_xattn = _g[0]
        g_ffn = _g[1]
        return (x, ctx_768, g_xattn, g_ffn)
    x, ctx_768, g_xattn, g_ffn = _rec_inputs()

    def _L0_xattn_setup():
        import jax, jax.numpy as jnp
        import numpy as np
        HEADS = 16
        DIM_HEAD = 64
        SCALE = DIM_HEAD ** (-0.5)
        QUERY_DIM = 512
        CONTEXT_DIM = 384
        INNER_DIM = HEADS * DIM_HEAD
        key = jax.random.key(seed)
        ks = jax.random.split(key, 7)
        B, Nq, Nk = (8, 2048, 77)
        x = jax.random.normal(ks[0], (B, Nq, QUERY_DIM), dtype=jnp.float32)
        context = jax.random.normal(ks[1], (B, Nk, CONTEXT_DIM), dtype=jnp.float32)
        Wq = jax.random.normal(ks[2], (QUERY_DIM, INNER_DIM), dtype=jnp.float32) * QUERY_DIM ** (-0.5)
        Wk = jax.random.normal(ks[3], (CONTEXT_DIM, INNER_DIM), dtype=jnp.float32) * CONTEXT_DIM ** (-0.5)
        Wv = jax.random.normal(ks[4], (CONTEXT_DIM, INNER_DIM), dtype=jnp.float32) * CONTEXT_DIM ** (-0.5)
        Wo = jax.random.normal(ks[5], (INNER_DIM, QUERY_DIM), dtype=jnp.float32) * INNER_DIM ** (-0.5)
        bo = jnp.zeros((QUERY_DIM,), dtype=jnp.float32)
        return {'x': x, 'context': context, 'Wq': Wq, 'Wk': Wk, 'Wv': Wv, 'Wo': Wo, 'bo': bo}
    _L0_xattn_all = _L0_xattn_setup()
    _L0_xattn_in = {k: v for k, v in _L0_xattn_all.items() if k in ('Wq', 'Wk', 'Wv', 'Wo', 'bo')}
    del _L0_xattn_all

    def _L0_ffn_setup():
        import jax, jax.numpy as jnp
        import numpy as np

        def _bitlinear(x, w_latent):
            scale = jax.lax.stop_gradient(jnp.clip(jnp.mean(jnp.abs(w_latent), axis=1, keepdims=True), 1e-05, None))
            tern = jnp.clip(jnp.round(w_latent / scale), -1.0, 1.0)
            w = w_latent + jax.lax.stop_gradient(tern - w_latent)
            return x @ (w * scale).T
        key = jax.random.key(seed)
        ks = jax.random.split(key, 6)
        dim, hidden, rank = (512, 2048, 16)
        B, S = (4, 2048)
        x = jax.random.normal(ks[0], (B, S, dim), dtype=jnp.float32)
        w_fc = 0.02 * jax.random.normal(ks[1], (hidden, dim), dtype=jnp.float32)
        w_proj = 0.02 * jax.random.normal(ks[2], (dim, hidden), dtype=jnp.float32)
        u = 0.02 * jax.random.normal(ks[3], (hidden, rank), dtype=jnp.float32)
        v = 0.02 * jax.random.normal(ks[4], (rank, dim), dtype=jnp.float32)
        fast_b = jax.random.normal(ks[5], (rank, rank), dtype=jnp.float32)
        gate = jnp.float32(0.05)
        return {'x': x, 'fast_b': fast_b, 'w_fc': w_fc, 'w_proj': w_proj, 'u': u, 'v': v, 'gate': gate}
    _L0_ffn_all = _L0_ffn_setup()
    _L0_ffn_in = {k: v for k, v in _L0_ffn_all.items() if k in ('fast_b', 'w_fc', 'w_proj', 'u', 'v', 'gate')}
    del _L0_ffn_all
    return {'x': x, 'ctx_768': ctx_768, 'g_xattn': g_xattn, 'g_ffn': g_ffn, 'L0_xattn_Wq': _L0_xattn_in['Wq'], 'L0_xattn_Wk': _L0_xattn_in['Wk'], 'L0_xattn_Wv': _L0_xattn_in['Wv'], 'L0_xattn_Wo': _L0_xattn_in['Wo'], 'L0_xattn_bo': _L0_xattn_in['bo'], 'L0_ffn_fast_b': _L0_ffn_in['fast_b'], 'L0_ffn_w_fc': _L0_ffn_in['w_fc'], 'L0_ffn_w_proj': _L0_ffn_in['w_proj'], 'L0_ffn_u': _L0_ffn_in['u'], 'L0_ffn_v': _L0_ffn_in['v'], 'L0_ffn_gate': _L0_ffn_in['gate']}

def reference(x, ctx_768, g_xattn, g_ffn, L0_xattn_Wq, L0_xattn_Wk, L0_xattn_Wv, L0_xattn_Wo, L0_xattn_bo, L0_ffn_fast_b, L0_ffn_w_fc, L0_ffn_w_proj, L0_ffn_u, L0_ffn_v, L0_ffn_gate):
    import jax
    import jax.numpy as jnp

    def _L0_xattn_ref(x, context, Wq, Wk, Wv, Wo, bo):
        import jax, jax.numpy as jnp
        import numpy as np
        HEADS = 16
        DIM_HEAD = 64
        SCALE = DIM_HEAD ** (-0.5)
        QUERY_DIM = 512
        CONTEXT_DIM = 384
        INNER_DIM = HEADS * DIM_HEAD
        B, Nq, _ = x.shape
        Nk = context.shape[1]
        q = x @ Wq
        k = context @ Wk
        v = context @ Wv
        q = q.reshape(B, Nq, HEADS, DIM_HEAD).transpose(0, 2, 1, 3)
        k = k.reshape(B, Nk, HEADS, DIM_HEAD).transpose(0, 2, 1, 3)
        v = v.reshape(B, Nk, HEADS, DIM_HEAD).transpose(0, 2, 1, 3)
        sim = jnp.einsum('bhid,bhjd->bhij', q, k) * SCALE
        attn = jax.nn.softmax(sim, axis=-1)
        out = jnp.einsum('bhij,bhjd->bhid', attn, v)
        out = out.transpose(0, 2, 1, 3).reshape(B, Nq, INNER_DIM)
        return out @ Wo + bo

    def _L0_ffn_ref(x, fast_b, w_fc, w_proj, u, v, gate):
        import jax, jax.numpy as jnp
        import numpy as np

        def _bitlinear(x, w_latent):
            scale = jax.lax.stop_gradient(jnp.clip(jnp.mean(jnp.abs(w_latent), axis=1, keepdims=True), 1e-05, None))
            tern = jnp.clip(jnp.round(w_latent / scale), -1.0, 1.0)
            w = w_latent + jax.lax.stop_gradient(tern - w_latent)
            return x @ (w * scale).T
        h = _bitlinear(x, w_fc) + gate * (x @ v.T @ fast_b.T @ u.T)
        r = jnp.maximum(h, 0.0)
        return _bitlinear(r * r, w_proj)
    x = x + jnp.tanh(g_xattn[0]) * _L0_xattn_ref(_layernorm(x, axis=-1), ctx_768, L0_xattn_Wq, L0_xattn_Wk, L0_xattn_Wv, L0_xattn_Wo, L0_xattn_bo)
    x = x + jnp.tanh(g_ffn[0]) * _L0_ffn_ref(_layernorm(x, axis=-1), L0_ffn_fast_b, L0_ffn_w_fc, L0_ffn_w_proj, L0_ffn_u, L0_ffn_v, L0_ffn_gate)
    return x

_drawn_inputs = setup_inputs


def setup_inputs(seed=0):
    import zlib

    import numpy as np

    out = dict(_drawn_inputs(seed))
    spreads = {'L0_xattn_bo': (0.0, 0.1)}
    factors = {'L0_ffn_fast_b': 8.0, 'L0_ffn_u': 8.0, 'L0_ffn_v': 8.0}
    for name, (base, spread) in spreads.items():
        noise = np.random.default_rng([zlib.crc32(name.encode()), seed]).standard_normal(out[name].shape)
        drawn = base * np.exp(spread * noise) if base else spread * noise
        out[name] = jnp.asarray(drawn.astype(out[name].dtype))
    for name, factor in factors.items():
        out[name] = (out[name] * factor).astype(out[name].dtype)
    return out
```

```python
from contextlib import ExitStack

import numpy as np

import concourse.bass as bass
from concourse import mybir

F32 = mybir.dt.float32
F16 = mybir.dt.float16
BF16 = mybir.dt.bfloat16
I32 = mybir.dt.int32
ALU = mybir.AluOpType
ACT = mybir.ActivationFunctionType
AX = mybir.AxisListType
ABSMAX = bass.bass_isa.ReduceOp.absmax


P = 128
B, NQ, D = 8, 224, 512
NK, DC = 750, 384
H, DH, HID, R = 16, 64, 2048, 16
INNER = H * DH
T = B * NQ
QT = NQ // 2
KT, NKT = 125, NK // 125
KH = NK // 2
GH = H // 2
DCH, CCH, ICH, HCH = D // P, DC // P, INNER // P, HID // P
TT, ST = 2 * NQ, 4
SUB = TT // ST
NTILES = T // TT
COPIES = P // R
EPS = 1e-5
Z_PART = [0, 0, 0, 1, 1, 1, 2, 2]
U_PART = [0, 1, 2, 0, 1, 2, 0, 1]

X_EXP = 11
Q_EXP, KV_EXP, P_EXP = -20, -24, 14
INV_SQRT_MAGIC = 0x5F3759DF

C_WQ, C_WK, C_WV, C_WO, C_FB = range(5)


def pow2_scale(dve, own, amax, field, scale, inverse, exponent_sum=268):
    v = bass_vector(dve)
    own(v.tensor_scalar(field, amax.bitcast(I32), 23, None, ALU.logical_shift_right))
    own(v.tensor_scalar(field, field, -1.0, float(exponent_sum), ALU.mult, ALU.add))
    own(v.tensor_scalar(field, field, 253.0, 1.0, ALU.min, ALU.max))
    own(v.tensor_scalar(scale.bitcast(I32), field, 23, None, ALU.logical_shift_left))
    own(v.tensor_scalar(field, field, -1.0, 254.0, ALU.mult, ALU.add))
    own(v.tensor_scalar(inverse.bitcast(I32), field, 23, None, ALU.logical_shift_left))


POW2_STEPS = 6


def bass_vector(dve):
    return dve


class Own:

    def __init__(self, eng, sem, start=0):
        self.eng, self.sem, self.start, self.n = eng, sem, start, 0

    def __call__(self, instruction):
        self.n += 1
        instruction.then_inc(self.sem, 1)
        self.eng.wait_ge(self.sem, self.start + self.n)


def layer_norm(v, own, x, stats, mean_var, work, y_bits, out):
    for s in range(ST):
        last = v.bn_stats(stats[:, s, :], x[:, s, :])
    own(last)
    for s in range(ST):
        last = v.bn_aggr(mean_var[:, s, :], stats[:, s, :])
    own(last)
    var, sq = work[:, 0, :], work[:, 1, :]
    y = y_bits.bitcast(F32)
    own(v.tensor_scalar(var, mean_var[:, :, 1], EPS, None, ALU.add))
    own(v.tensor_scalar(y_bits, var.bitcast(I32), 1, None, ALU.logical_shift_right))
    own(v.tensor_scalar(y_bits, y_bits, -1.0, float(INV_SQRT_MAGIC), ALU.mult, ALU.add))
    for _ in range(3):
        own(v.tensor_tensor(sq, y, y, ALU.mult))
        own(v.tensor_tensor(sq, sq, var, ALU.mult))
        own(v.tensor_scalar(sq, sq, -0.5, 1.5, ALU.mult, ALU.add))
        own(v.tensor_tensor(y, y, sq, ALU.mult))
    for s in range(ST):
        last = v.tensor_scalar(out[:, s, :], x[:, s, :], mean_var[:, s, 0:1], y[:, s:s + 1],
                               ALU.subtract, ALU.mult)
    return last


NORM_STEPS = 5 + 12


def flamingo_block(nc, x, ctx_t, g_xattn, g_ffn, wq, wk, wv, wo, bo, fast_b_t, w_fc, w_proj, u, v_low, gate, out):
    x_tiles = x.rearrange("(i s p) d -> i p s d", s=ST, p=SUB)
    out_tiles = out.rearrange("(i s p) d -> i p s d", s=ST, p=SUB)
    ctx_v = ctx_t.rearrange("b (c p) k -> b p c k", p=P)
    q_dram = [nc.dram_tensor(f"q_{n}", (B, INNER, NQ), F16, kind="Internal").ap() for n in ("high", "low")]
    o_dram = nc.dram_tensor("attn_out", (B, INNER, NQ), F32, kind="Internal").ap()

    with ExitStack() as keep:
        def sb(name, shape, dt, ctx=keep):
            return ctx.enter_context(nc.sbuf_tensor(name, shape, dt))

        def sem(name, ctx=keep):
            return ctx.enter_context(nc.semaphore(name))

        ps = keep.enter_context(nc.psum_tensor("ps", [P, 8, 512], F32))

        ident = sb("ident", [P, P], F32)
        ident16 = sb("ident16", [P, P], F16)
        ident_b = sb("ident_b", [P, P], BF16)
        ones = sb("ones", [P, P], F32)
        masks = sb("masks", [P, 3], F32)
        scal = sb("scal", [P, 3], F32)
        tanh_g = sb("tanh_g", [P, 2], F32)
        bo_bc = sb("bo_bc", [P, D], F32)
        proj_bc = sb("proj_bc", [P, D], F32)
        fc_scale = sb("fc_scale", [P, HCH], F32)
        relu_scale = sb("relu_scale", [P, HCH], F32)
        fc_t = sb("fc_t", [P, DCH, HID], F16)
        proj_t = sb("proj_t", [P, HCH, D], F16)
        u_t = sb("u_t", [P, HID], BF16)
        w_scale = sb("w_scale", [P, 5], F32)
        w_inv = sb("w_inv", [P, 5], F32)
        wo_s = sb("wo_s", [P, 2, ICH, D], F16)
        fb_s = sb("fb_s", [P, 2, DCH, P], F16)
        score_w = sb("score_w", [P, 1], F32)
        out_w = sb("out_w", [P, 1], F32)
        z_scale = sb("z_scale", [P, 1], F32)
        attn_w = sb("attn_w", [P, 1], F32)

        with ExitStack() as c:
            fc32 = sb("fc32", [P, HCH, D], F32, c)
            pj32 = sb("pj32", [P, DCH, HID], F32, c)
            u32 = sb("u32", [P, HCH, R], F32, c)
            fc_n = sb("fc_n", [P, HCH, D], F16, c)
            pj_n = sb("pj_n", [P, DCH, HID], F16, c)
            mag = sb("mag", [P, 20], F32, c)
            thr = sb("thr", [P, 20], F32, c)
            neg_thr = sb("neg_thr", [P, 20], F32, c)
            pj_scale = sb("pj_scale", [P, DCH], F32, c)
            diag = sb("diag", [P, DCH, P], F32, c)
            u_f = sb("u_f", [P, HCH, R], F32, c)
            u_r = sb("u_r", [P, HCH, R], F32, c)
            u_parts = [sb(f"u_part{n}", [P, HCH, R], BF16, c) for n in range(3)]
            u_rep = sb("u_rep", [P, HCH, COPIES, R], BF16, c)
            rden = sb("rden", [P, HCH], F32, c)

            s_fc, s_pj, s_small, s_bo = (sem(n, c) for n in ("fc_in", "pj_in", "small_in", "bo_in"))
            s_const = sem("const_made", c)
            s_ident = sem("ident_copied", c)
            s_mag, s_tern, s_tanh = sem("row_sum", c), sem("ternary_made", c), sem("tanh_done", c)
            s_own, s_mask = sem("dve_own", c), sem("mask_made", c)
            s_urep, s_diag = sem("u_copies", c), sem("diag_made", c)
            s_full, s_copied = sem("tp_full", c), sem("tp_copied", c)
            s_bc, s_done = sem("proj_bc_full", c), sem("dve_const", c)

            block = c.enter_context(nc.Block())

            @block.sync
            def _(sp):
                sp.dma_start(fc32[:], w_fc.rearrange("(j p) d -> p j d", p=P)).then_inc(s_fc, 16)
                sp.dma_start(pj32[:], w_proj.rearrange("(j p) h -> p j h", p=P)).then_inc(s_pj, 16)

            @block.gpsimd
            def _(pool):
                g = nc.gpsimd
                g.memset(ident[:], 0.0).then_inc(s_const, 1)
                g.memset(masks[:], 1.0).then_inc(s_const, 1)
                g.memset(ones[:], 1.0).then_inc(s_const, 1)
                pool.wait_ge(s_const, 3)
                g.affine_select(out=ident[:], in_=ident[:], compare_op=ALU.not_equal, fill=1.0, base=0,
                                pattern=[[-1, P]], channel_multiplier=1).then_inc(s_const, 1)
                for n, first in ((1, R * Z_PART.index(1)), (2, R * Z_PART.index(2))):
                    g.affine_select(out=masks[:, n:n + 1], in_=masks[:, n:n + 1], compare_op=ALU.is_ge, fill=0.0,
                                    base=-first, pattern=[[0, 1]], channel_multiplier=1).then_inc(s_const, 1)

            @block.scalar
            def _(act):
                a = nc.scalar
                for n, g in enumerate((g_xattn, g_ffn, gate)):
                    act.dma_start(scal[:, n:n + 1], g.to_broadcast([P, 1])).then_inc(s_small, 16)
                act.dma_start(bo_bc[:], bo.to_broadcast([P, D])).then_inc(s_bo, 16)
                act.dma_start(u32[:], u.rearrange("(j p) r -> p j r", p=P)).then_inc(s_small, 16)
                act.wait_ge(s_small, 64)
                a.activation(tanh_g[:], scal[:, 0:2], ACT.Tanh).then_inc(s_tanh, 1)
                act.wait_ge(s_fc, 16)
                for j in range(HCH):
                    a.activation(fc_n[:, j, :], fc32[:, j, :], ACT.Abs, accum_out=mag[:, j:j + 1]).then_inc(s_mag, 1)
                act.wait_ge(s_pj, 16)
                for j in range(DCH):
                    a.activation(pj_n[:, j, :], pj32[:, j, :], ACT.Abs,
                                 accum_out=mag[:, HCH + j:HCH + j + 1]).then_inc(s_mag, 1)
                for n in range(16):
                    act.wait_ge(s_full, n + 1)
                    bank = ps[:, n % 8, :].bitcast(F16)
                    if n < 8:
                        d, half = n % 4, n // 4
                        dst = fc_t[:, d, half * 1024:half * 1024 + 1024]
                    else:
                        dst = proj_t[:, 2 * (n - 8):2 * (n - 8) + 2, :]
                    a.activation(dst, bank, ACT.Copy).then_inc(s_copied, 1)
                for n in range(2):
                    act.wait_ge(s_full, 17 + n)
                    a.activation(u_t[:, n * 1024:n * 1024 + 1024], ps[:, n, :].bitcast(BF16),
                                 ACT.Copy).then_inc(s_copied, 1)

            @block.vector
            def _(dve):
                v = nc.vector
                own = Own(dve, s_own)
                dve.wait_ge(s_const, 6)
                v.tensor_copy(ident16[:], ident[:]).then_inc(s_ident, 1)
                v.tensor_copy(ident_b[:], ident[:]).then_inc(s_ident, 1)
                own(v.tensor_scalar(masks[:, 0:1], masks[:, 1:2], -1.0, 1.0, ALU.mult, ALU.add))
                own(v.tensor_tensor(masks[:, 1:2], masks[:, 1:2], masks[:, 2:3], ALU.subtract))
                dve.wait_ge(s_bo, 16)
                dve.wait_ge(s_tanh, 1)
                v.tensor_scalar(bo_bc[:], bo_bc[:], tanh_g[:, 0:1], None, ALU.mult)

                def thresholds(cols, scale, width, sums):
                    dve.wait_ge(s_mag, sums)
                    own(v.tensor_scalar(scale, mag[:, cols], 1.0 / width, 1e-5, ALU.mult, ALU.max))
                    v.tensor_scalar(thr[:, cols], scale, 0.5, None, ALU.mult)
                    own(v.tensor_scalar(neg_thr[:, cols], scale, -0.5, None, ALU.mult))

                thresholds(slice(0, HCH), fc_scale[:], D, HCH)
                for j in range(HCH):
                    own(v.tensor_scalar(fc_n[:, j, :], fc32[:, j, :], thr[:, j:j + 1], 1.0, ALU.is_gt, ALU.subtract))
                    v.scalar_tensor_tensor(out=fc_n[:, j, :], in0=fc32[:, j, :], scalar=neg_thr[:, j:j + 1],
                                           in1=fc_n[:, j, :], op0=ALU.is_ge, op1=ALU.add).then_inc(s_tern, 1)
                thresholds(slice(HCH, HCH + DCH), pj_scale[:], HID, HCH + DCH)
                for j in range(DCH):
                    c0 = HCH + j
                    own(v.tensor_scalar(pj_n[:, j, :], pj32[:, j, :], thr[:, c0:c0 + 1], 1.0, ALU.is_gt, ALU.subtract))
                    v.scalar_tensor_tensor(out=pj_n[:, j, :], in0=pj32[:, j, :], scalar=neg_thr[:, c0:c0 + 1],
                                           in1=pj_n[:, j, :], op0=ALU.is_ge, op1=ALU.add).then_inc(s_tern, 1)
                own(v.tensor_scalar(pj_scale[:], pj_scale[:], tanh_g[:, 1:2], None, ALU.mult))
                for j in range(DCH):
                    last = v.tensor_scalar(diag[:, j, :], ident[:], pj_scale[:, j:j + 1], None, ALU.mult)
                last.then_inc(s_diag, 1)
                v.tensor_scalar(relu_scale[:], fc_scale[:], 2.0 ** -X_EXP, None, ALU.mult)
                own(v.reciprocal(rden[:], fc_scale[:]))
                own(v.tensor_scalar(rden[:], rden[:], scal[:, 2:3], 2.0 ** X_EXP, ALU.mult, ALU.mult))
                for j in range(HCH):
                    last = v.tensor_scalar(u_f[:, j, :], u32[:, j, :], rden[:, j:j + 1], None, ALU.mult)
                own(last)
                own(v.tensor_copy(u_parts[0][:], u_f[:]))
                own(v.tensor_tensor(u_r[:], u_f[:], u_parts[0][:], ALU.subtract))
                own(v.tensor_copy(u_parts[1][:], u_r[:]))
                own(v.tensor_tensor(u_parts[2][:], u_r[:], u_parts[1][:], ALU.subtract))
                for n, part in enumerate(U_PART):
                    last = v.tensor_copy(u_rep[:, :, n, :], u_parts[part][:])
                last.then_inc(s_urep, 1)
                dve.wait_ge(s_bc, 1)
                v.tensor_copy(proj_bc[:], ps[:, 2, :])

            @block.tensor
            def _(pe):
                pe.wait_ge(s_ident, 2)
                for n in range(16):
                    if n >= 8:
                        pe.wait_ge(s_copied, n - 7)
                    bank = ps[:, n % 8, :].bitcast(F16)
                    for m in range(8):
                        if n < 8:
                            d, j = n % 4, 8 * (n // 4) + m
                            pe.wait_ge(s_tern, j + 1)
                            src = fc_n[:, j, d * P:(d + 1) * P]
                        else:
                            j, d = 2 * (n - 8) + m // 4, m % 4
                            pe.wait_ge(s_tern, HCH + DCH)
                            src = pj_n[:, d, j * P:(j + 1) * P]
                        last = nc.tensor.transpose(bank[:, m * P:(m + 1) * P], src, ident16[:])
                    last.then_inc(s_full, 1)
                pe.wait_ge(s_urep, 1)
                for n in range(2):
                    pe.wait_ge(s_copied, 9 + n)
                    bank = ps[:, n, :].bitcast(BF16)
                    for m in range(8):
                        src = u_rep[:, 8 * n + m, :, :].rearrange("p c r -> p (c r)")
                        last = nc.tensor.transpose(bank[:, m * P:(m + 1) * P], src, ident_b[:])
                    last.then_inc(s_full, 1)
                pe.wait_ge(s_diag, 1)
                pe.wait_ge(s_copied, 11)
                for j in range(DCH):
                    last = nc.tensor.matmul(ps[:, 2, j * P:(j + 1) * P], ones[:], diag[:, j, :], start=True, stop=True)
                last.then_inc(s_bc, 1)

        kv_ctx = keep.enter_context(ExitStack())
        wk_s = sb("wk_s", [P, 2, CCH, INNER], F16, kv_ctx)
        wv_s = sb("wv_s", [P, 2, CCH, INNER], F16, kv_ctx)
        q_ctx = keep.enter_context(ExitStack())
        wq_s = sb("wq_s", [P, 2, DCH, INNER], F16, q_ctx)
        with ExitStack() as c:
            wq32 = sb("wq32", [P, DCH, INNER], F32, c)
            wk32 = sb("wk32", [P, CCH, INNER], F32, c)
            wv32 = sb("wv32", [P, CCH, INNER], F32, c)
            wo32 = sb("wo32", [P, ICH, D], F32, c)
            fb32 = sb("fb32", [P, DCH, P], F32, c)
            v32 = sb("v32", [R, D], F32, c)
            fbt = sb("fbt", [R, R], F32, c)
            fbt_rep = sb("fbt_rep", [R, COPIES, R], F32, c)
            amax = sb("amax", [P, 5], F32, c)
            amax_all = sb("amax_all", [P, 5], F32, c)
            field = sb("field", [P, 5], I32, c)
            s_w = [sem(f"w_in{n}", c) for n in range(4)]
            s_lowrank, s_rep = sem("lowrank_in", c), sem("fbt_copies", c)
            s_fb_full, s_own = sem("fb_full", c), sem("dve_own2", c)
            s_amax, s_all, s_scale = sem("w_amax", c), sem("w_amax_all", c), sem("w_scaled", c)
            s_high = sem("w_high", c)
            weights = [(wq32, wq_s, wq, DCH), (wk32, wk_s, wk, CCH), (wv32, wv_s, wv, CCH), (wo32, wo_s, wo, ICH)]
            block = c.enter_context(nc.Block())

            @block.sync
            def _(sp):
                sp.dma_start(v32[:], v_low).then_inc(s_lowrank, 16)
                sp.dma_start(fbt[:], fast_b_t).then_inc(s_lowrank, 16)
                for n, (dst, _, src, _) in enumerate(weights):
                    sp.dma_start(dst[:], src.rearrange("(c p) n -> p c n", p=P)).then_inc(s_w[n], 16)

            @block.tensor
            def _(pe):
                pe.wait_ge(s_rep, 1)
                for j in range(DCH):
                    last = nc.tensor.matmul(ps[:, 0, j * P:(j + 1) * P], v32[:, j * P:(j + 1) * P],
                                            fbt_rep[:].rearrange("p c r -> p (c r)"), start=True, stop=True)
                last.then_inc(s_fb_full, 1)

            @block.gpsimd
            def _(pool):
                pool.wait_ge(s_amax, 5)
                nc.gpsimd.partition_all_reduce(amax_all[:], amax[:], P, ABSMAX).then_inc(s_all, 1)

            @block.scalar
            def _(act):
                act.wait_ge(s_scale, 1)
                for n, (src, dst, _, _) in enumerate(weights):
                    nc.scalar.activation(dst[:, 0], src[:], ACT.Copy, scale=w_scale[:, n:n + 1]).then_inc(s_high, 1)
                nc.scalar.activation(fb_s[:, 0], fb32[:], ACT.Copy, scale=w_scale[:, 4:5]).then_inc(s_high, 1)

            @block.vector
            def _(dve):
                v = nc.vector
                own = Own(dve, s_own)
                dve.wait_ge(s_lowrank, 32)
                for n in range(COPIES):
                    last = v.tensor_copy(fbt_rep[:, n, :], fbt[:])
                last.then_inc(s_rep, 1)
                dve.wait_ge(s_fb_full, 1)
                own(v.tensor_copy(fb32[:].rearrange("p c n -> p (c n)"), ps[:, 0, :]))
                v.tensor_reduce(amax[:, C_FB:C_FB + 1], fb32[:], AX.XY, ALU.max,
                                apply_absolute_value=True).then_inc(s_amax, 1)
                for n, (src, _, _, _) in enumerate(weights):
                    dve.wait_ge(s_w[n], 16)
                    v.tensor_reduce(amax[:, n:n + 1], src[:], AX.XY, ALU.max,
                                    apply_absolute_value=True).then_inc(s_amax, 1)
                dve.wait_ge(s_all, 1)
                pow2_scale(v, own, amax_all[:], field[:], w_scale[:], w_inv[:])
                own(v.tensor_tensor(score_w[:], w_inv[:, C_WQ:C_WQ + 1], w_inv[:, C_WK:C_WK + 1], ALU.mult))
                v.tensor_scalar(score_w[:], score_w[:], 2.0 ** (-Q_EXP - X_EXP - KV_EXP) * DH ** -0.5, None, ALU.mult)
                v.tensor_scalar(out_w[:], w_inv[:, C_WV:C_WV + 1], 2.0 ** (-KV_EXP - P_EXP), None, ALU.mult)
                v.tensor_scalar(z_scale[:], w_inv[:, C_FB:C_FB + 1], 2.0 ** -X_EXP, None, ALU.mult)
                v.tensor_tensor(attn_w[:], w_inv[:, C_WO:C_WO + 1], tanh_g[:, 0:1], ALU.mult).then_inc(s_scale, 1)
                for n, (src, dst, _, _) in enumerate(weights):
                    dve.wait_ge(s_high, n + 1)
                    v.scalar_tensor_tensor(out=dst[:, 1], in0=src[:], scalar=w_scale[:, n:n + 1], in1=dst[:, 0],
                                           op0=ALU.mult, op1=ALU.subtract)
                dve.wait_ge(s_high, 5)
                v.scalar_tensor_tensor(out=fb_s[:, 1], in0=fb32[:], scalar=w_scale[:, 4:5], in1=fb_s[:, 0],
                                       op0=ALU.mult, op1=ALU.subtract)

        with ExitStack() as c:
            xt = [sb(f"xt{n}", [SUB, ST, D], F32, c) for n in range(2)]
            xn = sb("xn", [SUB, ST, D], F32, c)
            stats = sb("q_stats", [SUB, ST, 6], F32, c)
            mean_var = sb("q_mean_var", [SUB, ST, 2], F32, c)
            work = sb("q_work", [SUB, 2, ST], F32, c)
            y_bits = sb("q_y", [SUB, ST], I32, c)
            xT = sb("xT", [P, 2, DCH, TT], F16, c)
            q_out = sb("q_out", [P, 2, ICH, TT], F16, c)
            s_x, s_normed, s_own = [sem(f"x_in{n}", c) for n in range(2)], sem("x_normed", c), sem("dve_own3", c)
            s_full, s_high, s_free = sem("q_full", c), sem("q_high", c), sem("q_free", c)
            s_stored = sem("q_stored", c)
            USES, RING = DCH + ICH, 4
            block = c.enter_context(nc.Block())

            def store_q(sp, i):
                sp.wait_ge(s_free, USES * i + USES)
                for half in range(2):
                    for b in range(2):
                        dst = q_dram[half].rearrange("(i b) (c p) t -> i b p c t", b=2, p=P)[i, b]
                        sp.dma_start(dst, q_out[:, half, :, b * NQ:(b + 1) * NQ]).then_inc(s_stored, 16)

            @block.sync
            def _(sp):
                for i in range(2):
                    sp.dma_start(xt[i][:], x_tiles[i]).then_inc(s_x[i], 16)
                for i in range(NTILES):
                    if i + 2 < NTILES:
                        sp.wait_ge(s_normed, i + 1)
                        sp.dma_start(xt[i % 2][:], x_tiles[i + 2]).then_inc(s_x[i % 2], 16)
                    store_q(sp, i)
                sp.wait_ge(s_stored, 64 * NTILES)

            @block.tensor
            def _(pe):
                for i in range(NTILES):
                    u0 = USES * i
                    pe.wait_ge(s_normed, i + 1)
                    for d in range(DCH):
                        if u0 + d >= RING:
                            pe.wait_ge(s_free, u0 + d - RING + 1)
                        for s in range(ST):
                            last = nc.tensor.transpose(ps[:, (u0 + d) % RING, s * SUB:(s + 1) * SUB],
                                                       xn[:, s, d * P:(d + 1) * P], ident[0:SUB, 0:SUB])
                        last.then_inc(s_full, 1)
                    pe.wait_ge(s_free, u0 + DCH)
                    for n in range(ICH):
                        use = u0 + DCH + n
                        pe.wait_ge(s_free, use - RING + 1)
                        k = 0
                        for wh, xh in ((0, 0), (0, 1), (1, 0)):
                            for d in range(DCH):
                                last = nc.tensor.matmul(ps[:, use % RING, 0:TT], wq_s[:, wh, d, n * P:(n + 1) * P],
                                                        xT[:, xh, d, :], start=(k == 0), stop=(k == 3 * DCH - 1))
                                k += 1
                        last.then_inc(s_full, 1)

            @block.scalar
            def _(act):
                for i in range(NTILES):
                    for n in range(USES):
                        use = USES * i + n
                        act.wait_ge(s_full, use + 1)
                        src = ps[:, use % RING, 0:TT]
                        if n < DCH:
                            nc.scalar.activation(xT[:, 0, n, :], src, ACT.Copy, scale=2.0 ** X_EXP).then_inc(s_high, 1)
                        else:
                            if n == DCH and i >= 1:
                                act.wait_ge(s_stored, 64 * i)
                            nc.scalar.activation(q_out[:, 0, n - DCH, :], src, ACT.Copy,
                                                 scale=2.0 ** Q_EXP).then_inc(s_high, 1)

            @block.vector
            def _(dve):
                v = nc.vector
                for i in range(NTILES):
                    own = Own(dve, s_own, NORM_STEPS * i)
                    dve.wait_ge(s_x[i % 2], 16 * (i // 2 + 1))
                    layer_norm(v, own, xt[i % 2], stats, mean_var, work, y_bits[:], xn).then_inc(s_normed, 1)
                    for n in range(USES):
                        use = USES * i + n
                        dve.wait_ge(s_high, use + 1)
                        src = ps[:, use % RING, 0:TT]
                        dst, exp = (xT[:, :, n, :], X_EXP) if n < DCH else (q_out[:, :, n - DCH, :], Q_EXP)
                        v.scalar_tensor_tensor(out=dst[:, 1, :], in0=src, scalar=2.0 ** exp, in1=dst[:, 0, :],
                                               op0=ALU.mult, op1=ALU.subtract).then_inc(s_free, 1)
        q_ctx.close()

        with ExitStack() as c:
            keys = sb("keys", [P, 2, GH, NK], F16, c)
            vals = sb("vals", [KT, 2, NKT, GH, 2, DH], F16, c)
            q_dup = sb("q_dup", [P, 2, 2, GH, NQ], F16, c)
            ctx32 = sb("ctx32", [P, CCH, NK], F32, c)
            ctx_s = sb("ctx_s", [P, 2, CCH, NK], F16, c)
            probs = sb("probs", [QT, 2, 2, NK], F32, c)
            probs_t = sb("probs_t", [KT, 2, NKT, NQ], F16, c)
            o_low = sb("o_low", [DH, NQ], F32, c)
            o_t = sb("o_t", [P, 2, GH // 2, NQ], F32, c)
            row_max = sb("row_max", [QT, 2], F32, c)
            bias = sb("bias", [QT, 2], F32, c)
            row_sum = sb("row_sum", [QT, 2], F32, c)
            row_inv = sb("row_inv", [QT, 2], F32, c)
            c_amax = sb("c_amax", [P, 1], F32, c)
            c_all = sb("c_all", [P, 1], F32, c)
            c_field = sb("c_field", [P, 1], I32, c)
            c_scale = sb("c_scale", [P, 1], F32, c)
            c_inv = sb("c_inv", [P, 1], F32, c)
            score_scale = sb("score_scale", [P, 2], F32, c)
            out_scale = sb("out_scale", [P, 1], F32, c)

            s_ctx, s_q, s_o = sem("ctx_in", c), [sem(f"q_in{n}", c) for n in range(2)], [sem(f"o_stored{n}", c) for n in range(2)]
            s_amax, s_all = sem("ctx_amax", c), sem("ctx_amax_all", c)
            s_own, s_ctx_scale, s_ctx_high = sem("dve_own4", c), sem("ctx_scale", c), sem("ctx_high", c)
            s_ctx_cut = sem("ctx_cut", c)
            s_scores, s_rowmax, s_bias = sem("scores_full", c), sem("row_max_done", c), sem("bias_ready", c)
            s_exp, s_inv, s_probs = sem("exp_done", c), sem("row_inv_ready", c), sem("probs_ready", c)
            s_full, s_high, s_free = sem("work_full", c), sem("work_high", c), sem("work_free", c)
            s_keys, s_vals = sem("keys_ready", c), sem("vals_ready", c)
            s_set = sem("score_scale_set", c)
            s_pool_passed = sem("pool_passed", c)
            RING = 4
            K_UNITS = [[], [0], [1], [2], [3], [4], [5], [6, 7]]
            V_UNITS = [[], [0], [1], [2], [3], [4], [5], []]
            N_KU, N_VU = GH, NKT
            FIRST_USES = N_KU + N_VU

            def steps(fill):
                out = []
                for h in range(GH):
                    out += [(h, "T", g) for g in range(3)]
                    if fill:
                        out += [(h, "K", n) for n in K_UNITS[h]] + [(h, "V", n) for n in V_UNITS[h]]
                    out.append((h, "A", 0))
                return out

            USES_GROUP = len(steps(True))
            block = c.enter_context(nc.Block())

            def use_base(i, par):
                return FIRST_USES + 2 * USES_GROUP * i + USES_GROUP * par

            def for_groups(eng, group):
                with eng.Fori(0, B - 1) as i:
                    group(i, 0, True, False)
                    group(i, 1, True, False)
                group(B - 1, 0, True, False)
                group(B - 1, 1, False, True)

            def load_q(sp, b, par):
                for half in range(2):
                    for rows in range(2):
                        src = q_dram[half].rearrange("b (g h d) t -> b g d h t", g=2, d=DH)[b, par]
                        sp.dma_start(q_dup[rows * DH:(rows + 1) * DH, par, half, :, :], src).then_inc(s_q[par], 16)

            @block.sync
            def _(sp):
                sp.dma_start(ctx32[:], ctx_v[0]).then_inc(s_ctx, 16)
                for n in range(2):
                    sp.sem_inc(s_o[n], 16)
                load_q(sp, 0, 0)
                load_q(sp, 0, 1)

                def group(i, par, fill, last):
                    if not last and not (par == 0 and isinstance(i, int)):
                        if par == 0:
                            sp.wait_ge(s_ctx_cut, i + 1)
                            sp.dma_start(ctx32[:], ctx_v[i + 1]).then_inc(s_ctx, 16)
                        sp.wait_ge(s_scores, 2 * (2 * GH * i + GH * par + GH))
                        load_q(sp, i + 1, par)
                    sp.wait_ge(s_free, use_base(i, par) + len(steps(fill)))
                    dst = o_dram.rearrange("b (g c p) t -> b g p c t", g=2, p=P)[i, par]
                    sp.dma_start(dst, o_t[:, par]).then_inc(s_o[par], 16)

                for_groups(sp, group)
                for n in range(2):
                    sp.wait_ge(s_o[n], 16 + 16 * B)

            @block.gpsimd
            def _(pool):
                def wait_counted(sem, value):
                    pool.wait_ge(sem, value)
                    pool.sem_inc(s_pool_passed, 1)

                def reduce_ctx(b):
                    wait_counted(s_amax, b + 1)
                    nc.gpsimd.partition_all_reduce(c_all[:], c_amax[:], P, ABSMAX).then_inc(s_all, 1)

                def normalise(head, par_h):
                    for t in range(2):
                        wait_counted(s_inv, 2 * head + t + 1)
                        nc.gpsimd.tensor_scalar(probs[:, par_h, t, :], probs[:, par_h, t, :], row_inv[:, t:t + 1],
                                                2.0 ** P_EXP, ALU.mult, ALU.mult).then_inc(s_probs, 1)

                reduce_ctx(0)
                normalise(0, 0)

                def group(i, par, fill, last):
                    for h in range(GH):
                        if not (last and h == GH - 1):
                            normalise(2 * GH * i + GH * par + h + 1, (h + 1) % 2)
                        if par == 0 and h == 5 and not isinstance(i, int):
                            reduce_ctx(i + 1)

                for_groups(pool, group)

            @block.scalar
            def _(act):
                a = nc.scalar

                def exps(head, par_h, t):
                    act.wait_ge(s_bias, 2 * head + t + 1)
                    a.activation(probs[:, par_h, t, :].rearrange("p (n k) -> p n k", n=2), ps[0:QT, 2 * t:2 * t + 2, 0:KH],
                                 ACT.Exp, bias=bias[:, t:t + 1], scale=score_scale[0:QT, 0:1],
                                 accum_out=row_sum[:, t:t + 1]).then_inc(s_exp, 1)

                def high(use, slot, kind, n, par):
                    bank = ps[:, 4 + slot % RING, :]
                    act.wait_ge(s_full, use + 1)
                    if kind == "T":
                        a.activation(probs_t[:, 0, 2 * n:2 * n + 2, :], bank[0:KT, 0:2 * NQ].rearrange("p (c q) -> p c q", c=2),
                                     ACT.Copy).then_inc(s_high, 1)
                    elif kind == "K":
                        for hh in range(2):
                            last = a.activation(keys[0:DH, par, 2 * (n // 2) + hh, (n % 2) * KH:(n % 2 + 1) * KH],
                                                bank[hh * DH:(hh + 1) * DH, 0:KH], ACT.Copy, scale=2.0 ** KV_EXP)
                        last.then_inc(s_high, 1)
                    elif kind == "V":
                        a.activation(vals[:, par, n, :, 0, :], bank[0:KT, :].rearrange("p (h d) -> p h d", d=DH),
                                     ACT.Copy, scale=2.0 ** KV_EXP).then_inc(s_high, 1)
                    else:
                        a.activation(o_low[:], bank[DH:P, 0:NQ], ACT.Copy, scale=out_scale[0:DH, 0:1]).then_inc(s_high, 1)

                def cut_ctx(b):
                    act.wait_ge(s_ctx_scale, b + 1)
                    a.activation(ctx_s[:, 0], ctx32[:], ACT.Copy, scale=c_scale[:]).then_inc(s_ctx_high, 1)

                cut_ctx(0)
                for use in range(FIRST_USES):
                    kind, n = ("K", use) if use < N_KU else ("V", use - N_KU)
                    high(use, use, kind, n, 0)
                for t in range(2):
                    exps(0, 0, t)

                def group(i, par, fill, last):
                    if par == 1 and fill:
                        act.wait_ge(s_full, use_base(i, par))
                        cut_ctx(i + 1)
                    slot = FIRST_USES + USES_GROUP * par
                    for n, (h, kind, which) in enumerate(steps(fill)):
                        head = 2 * GH * i + GH * par + h
                        more = not (last and h == GH - 1)
                        if kind == "T" and which < 2 and more:
                            exps(head + 1, (h + 1) % 2, which)
                        high(use_base(i, par) + n, slot + n, kind, which, 1 - par)

                for_groups(act, group)

            @block.vector
            def _(dve):
                v = nc.vector

                def maxima(head, t):
                    dve.wait_ge(s_scores, 2 * head + t + 1)
                    v.tensor_reduce(row_max[:, t:t + 1], ps[0:QT, 2 * t:2 * t + 2, 0:KH], AX.XY,
                                    ALU.max).then_inc(s_rowmax, 1)
                    dve.wait_ge(s_rowmax, 2 * head + t + 1)
                    v.tensor_scalar(bias[:, t:t + 1], row_max[:, t:t + 1], score_scale[0:QT, 1:2], None,
                                    ALU.mult).then_inc(s_bias, 1)

                def inverses(head, t):
                    dve.wait_ge(s_exp, 2 * head + t + 1)
                    v.reciprocal(row_inv[:, t:t + 1], row_sum[:, t:t + 1]).then_inc(s_inv, 1)

                def low(use, slot, kind, n, par, h, opar):
                    bank = ps[:, 4 + slot % RING, :]
                    dve.wait_ge(s_high, use + 1)
                    if kind == "T":
                        v.tensor_tensor(probs_t[:, 1, 2 * n:2 * n + 2, :],
                                        bank[0:KT, 0:2 * NQ].rearrange("p (c q) -> p c q", c=2),
                                        probs_t[:, 0, 2 * n:2 * n + 2, :], ALU.subtract).then_inc(s_free, 1)
                    elif kind == "K":
                        for hh in range(2):
                            cols = slice((n % 2) * KH, (n % 2 + 1) * KH)
                            head = 2 * (n // 2) + hh
                            last = v.scalar_tensor_tensor(
                                out=keys[DH:P, par, head, cols], in0=bank[hh * DH:(hh + 1) * DH, 0:KH],
                                scalar=2.0 ** KV_EXP, in1=keys[0:DH, par, head, cols], op0=ALU.mult, op1=ALU.subtract)
                        last.then_inc(s_free, 1)
                    elif kind == "V":
                        v.scalar_tensor_tensor(out=vals[:, par, n, :, 1, :],
                                               in0=bank[0:KT, :].rearrange("p (h d) -> p h d", d=DH),
                                               scalar=2.0 ** KV_EXP, in1=vals[:, par, n, :, 0, :],
                                               op0=ALU.mult, op1=ALU.subtract).then_inc(s_free, 1)
                    else:
                        rows = slice((h % 2) * DH, (h % 2 + 1) * DH)
                        v.scalar_tensor_tensor(out=o_t[rows, opar, h // 2, :], in0=bank[0:DH, 0:NQ],
                                               scalar=out_scale[0:DH, 0:1], in1=o_low[:],
                                               op0=ALU.mult, op1=ALU.add).then_inc(s_free, 1)

                def scale_ctx(b):
                    own = Own(dve, s_own, POW2_STEPS * b)
                    dve.wait_ge(s_all, b + 1)
                    pow2_scale(v, own, c_all[:], c_field[:], c_scale[:], c_inv[:])

                def cut_ctx(b):
                    dve.wait_ge(s_ctx_high, b + 1)
                    v.scalar_tensor_tensor(out=ctx_s[:, 1], in0=ctx32[:], scalar=c_scale[:], in1=ctx_s[:, 0],
                                           op0=ALU.mult, op1=ALU.subtract).then_inc(s_ctx_cut, 1)

                def amax_ctx(b):
                    dve.wait_ge(s_ctx, 16 * (b + 1))
                    v.tensor_reduce(c_amax[:], ctx32[:], AX.XY, ALU.max, apply_absolute_value=True).then_inc(s_amax, 1)

                def set_score_scale():
                    v.tensor_scalar(score_scale[:, 0:1], c_inv[:], score_w[:], None, ALU.mult)
                    v.tensor_scalar(score_scale[:, 1:2], c_inv[:], score_w[:], -1.0, ALU.mult, ALU.mult).then_inc(s_set, 1)

                def set_out_scale():
                    return v.tensor_scalar(out_scale[:], c_inv[:], out_w[:], None, ALU.mult)

                amax_ctx(0)
                scale_ctx(0)
                v.memset(bias[:], 0.0).then_inc(s_ctx_scale, 1)
                cut_ctx(0)
                set_score_scale()
                set_out_scale()
                for use in range(FIRST_USES):
                    kind, n = ("K", use) if use < N_KU else ("V", use - N_KU)
                    low(use, use, kind, n, 0, 0, 0)
                dve.wait_ge(s_set, 1)
                for t in range(2):
                    maxima(0, t)
                for t in range(2):
                    inverses(0, t)

                def group(i, par, fill, last):
                    if par == 1 and fill:
                        scale_ctx(i + 1)
                        v.memset(c_amax[:], 0.0).then_inc(s_ctx_scale, 1)
                        cut_ctx(i + 1)
                    slot = FIRST_USES + USES_GROUP * par
                    for n, (h, kind, which) in enumerate(steps(fill)):
                        head = 2 * GH * i + GH * par + h
                        more = not (last and h == GH - 1)
                        if kind == "T" and which == 0 and more:
                            if par == 1 and h == GH - 1:
                                set_score_scale()
                                dve.wait_ge(s_set, i + 2)
                            maxima(head + 1, 0)
                            maxima(head + 1, 1)
                        if kind == "A" and h == 0:
                            dve.wait_ge(s_o[par], 16 * i + 16)
                        low(use_base(i, par) + n, slot + n, kind, which, 1 - par, h, par)
                        if kind == "T" and which < 2 and more:
                            inverses(head + 1, which)
                        if kind == "A":
                            if par == 0 and h == 3 and fill and not isinstance(i, int):
                                amax_ctx(i + 1)
                    if par == 1 and fill:
                        dve.wait_ge(s_free, use_base(i, par) + USES_GROUP)
                        set_out_scale()

                for_groups(dve, group)

            @block.tensor
            def _(pe):
                mm = nc.tensor.matmul

                def scores(head, par, h, t, first):
                    if not first:
                        pe.wait_ge(s_exp, 2 * head + t - 1)
                    for half in range(2):
                        for n in range(2):
                            last = mm(ps[0:QT, 2 * t + n, 0:KH], q_dup[:, par, half, h, t * QT:(t + 1) * QT],
                                      keys[:, par, h, n * KH:(n + 1) * KH], start=(half == 0), stop=(half == 1))
                    last.then_inc(s_scores, 1)

                def project_keys(use, slot, n, par):
                    bank = ps[:, 4 + slot % RING, 0:KH]
                    col = (par * GH + 2 * (n // 2)) * DH
                    k = 0
                    for wh, xh in ((0, 0), (0, 1), (1, 0)):
                        for d in range(CCH):
                            last = mm(bank, wk_s[:, wh, d, col:col + P], ctx_s[:, xh, d, (n % 2) * KH:(n % 2 + 1) * KH],
                                      start=(k == 0), stop=(k == 3 * CCH - 1))
                            k += 1
                    last.then_inc(s_full, 1)

                def project_values(use, slot, n, par):
                    bank = ps[0:KT, 4 + slot % RING, :]
                    k = 0
                    for wh, xh in ((0, 0), (1, 0), (0, 1)):
                        for d in range(CCH):
                            last = mm(bank, ctx_s[:, xh, d, n * KT:(n + 1) * KT],
                                      wv_s[:, wh, d, par * GH * DH:(par + 1) * GH * DH],
                                      start=(k == 0), stop=(k == 3 * CCH - 1))
                            k += 1
                    last.then_inc(s_full, 1)

                pe.wait_ge(s_ctx_cut, 1)
                for use in range(FIRST_USES):
                    if use >= RING:
                        pe.wait_ge(s_free, use - RING + 1)
                    if use < N_KU:
                        project_keys(use, use, use, 0)
                    else:
                        project_values(use, use, use - N_KU, 0)
                pe.wait_ge(s_q[0], 64)
                pe.wait_ge(s_free, 2)
                for t in range(2):
                    scores(0, 0, 0, t, True)

                def group(i, par, fill, last):
                    slot = FIRST_USES + USES_GROUP * par
                    base = use_base(i, par)
                    k_use = {}
                    for n, (h, kind, which) in enumerate(steps(fill)):
                        head = 2 * GH * i + GH * par + h
                        use = base + n
                        if kind == "T" and which == 0:
                            if h < GH - 1:
                                for t in range(2):
                                    scores(head + 1, par, h + 1, t, False)
                            elif not last:
                                pe.wait_ge(s_free, base + k_use[1] + 1)
                                pe.wait_ge(s_q[1 - par], 64 * (i + 1 + par))
                                for t in range(2):
                                    scores(head + 1, 1 - par, 0, t, False)
                            pe.wait_ge(s_probs, 2 * head + 2)
                            if h == 0:
                                pe.wait_ge(s_free, base - 1)
                        if h == 1 and kind == "K" and which == 0 and par == 1:
                            pe.wait_ge(s_ctx_cut, i + 2)
                        pe.wait_ge(s_free, use - RING + 1)
                        if kind == "K":
                            k_use[which] = n
                            project_keys(use, slot + n, which, 1 - par)
                        elif kind == "V":
                            project_values(use, slot + n, which, 1 - par)
                        elif kind == "T":
                            bank = ps[:, 4 + (slot + n) % RING, :]
                            for k in range(2):
                                for t in range(2):
                                    last_mm = nc.tensor.transpose(
                                        bank[0:KT, k * NQ + t * QT:k * NQ + (t + 1) * QT],
                                        probs[:, h % 2, t, (2 * which + k) * KT:(2 * which + k + 1) * KT],
                                        ident[0:QT, 0:QT])
                            last_mm.then_inc(s_full, 1)
                            t_use = n
                        else:
                            pe.wait_ge(s_free, base + t_use + 1)
                            k = 0
                            for kt in range(NKT):
                                for half in range(2):
                                    last_mm = mm(ps[:, 4 + (slot + n) % RING, 0:NQ],
                                                 vals[:, par, kt, h, :, :].rearrange("p a d -> p (a d)"),
                                                 probs_t[:, half, kt, :], start=(k == 0), stop=(k == 2 * NKT - 1))
                                    k += 1
                            last_mm.then_inc(s_full, 1)

                for_groups(pe, group)
        kv_ctx.close()

        with ExitStack() as c:
            o32 = sb("o32", [P, ICH, TT], F32, c)
            o_s = sb("o_s", [P, 2, ICH, TT], F16, c)
            xr = sb("xr", [SUB, ST, D], F32, c)
            x1 = sb("x1", [SUB, ST, D], F32, c)
            res = sb("res", [SUB, ST, D], F32, c)
            xn = sb("xn2", [SUB, ST, D], F32, c)
            xT = sb("xT2", [P, 2, DCH, TT], F16, c)
            r = sb("r", [P, HCH, TT], F32, c)
            r_s = r[:].bitcast(F16).rearrange("p j (a t) -> p j a t", a=2)
            sq = sb("sq", [P, 3, TT], F32, c)
            z32 = sb("z32", [P, TT], F32, c)
            z_part = [sb(f"z_part{n}", [P, TT], BF16, c) for n in range(2)]
            z_rest = [sb(f"z_rest{n}", [P, TT], F32, c) for n in range(2)]
            z_acc = sb("z_acc", [P, TT], F32, c)
            z = sb("z", [P, TT], BF16, c)
            y_out = sb("y_out", [SUB, ST, D], F32, c)
            stats = sb("f_stats", [SUB, ST, 6], F32, c)
            mean_var = sb("f_mean_var", [SUB, ST, 2], F32, c)
            work = sb("f_work", [SUB, 2, ST], F32, c)
            y_bits = sb("f_y", [SUB, ST], I32, c)
            o_amax = sb("o_amax", [P, 1], F32, c)
            o_all = sb("o_all", [P, 1], F32, c)
            r_amax = sb("r_amax", [P, HCH], F32, c)
            r_amax1 = sb("r_amax1", [P, 1], F32, c)
            r_all = sb("r_all", [P, 1], F32, c)
            fld = sb("fld", [P, 2], I32, c)
            o_scale = sb("o_scale", [P, 1], F32, c)
            o_inv = sb("o_inv", [P, 1], F32, c)
            g_scale = sb("g_scale", [P, 1], F32, c)
            g_inv = sb("g_inv", [P, 1], F32, c)

            s_o, s_x, s_y = sem("o_in", c), sem("xr_in", c), sem("y_stored", c)
            s_oamax, s_oall, s_oscale, s_ohigh = sem("o_amax_s", c), sem("o_all_s", c), sem("o_scale_s", c), sem("o_high", c)
            s_ocut = sem("o_cut", c)
            s_xb, s_res, s_normed = sem("x_plus_bias", c), sem("res_kept", c), sem("x1_normed", c)
            s_own = sem("dve_own5", c)
            s_full, s_free, s_thigh = sem("a_full", c), sem("a_free", c), sem("t_high", c)
            s_zfull, s_z32, s_zready = sem("z_full", c), sem("z32_ready", c), sem("z_ready", c)
            s_fc, s_relu = sem("fc_full", c), sem("relu_done", c)
            s_ramax, s_rall, s_rscale = sem("r_amax_s", c), sem("r_all_s", c), sem("r_scale_s", c)
            s_sq, s_rhigh, s_rlow = sem("squared", c), sem("r_high", c), sem("r_low", c)
            s_part, s_yout = sem("y_part", c), sem("y_ready", c)
            RING_A, RING_B, USES_A = 3, 4, 3 * ST
            SQN = 3
            OWN_STEPS = 1 + POW2_STEPS + NORM_STEPS + 8 + 1 + POW2_STEPS + ST
            block = c.enter_context(nc.Block())

            def a_use(i, kind, n):
                order = {"O": 0, "T": ST} if isinstance(i, int) and i == 0 else None
                if kind != "Y" and order is not None:
                    return order[kind] + n
                if kind == "Y":
                    return 2 * ST + 3 * ST * i + (ST if not (isinstance(i, int) and i == NTILES - 1) else 0) + n
                return 2 * ST + 3 * ST * (i - 1) + (0 if kind == "O" else 2 * ST) + n

            @block.sync
            def _(sp):
                for i in range(NTILES):
                    if i >= 1:
                        sp.wait_ge(s_ocut, i)
                    for b in range(2):
                        src = o_dram.rearrange("(i b) (c p) t -> i b p c t", b=2, p=P)[i, b]
                        sp.dma_start(o32[:, :, b * NQ:(b + 1) * NQ], src).then_inc(s_o, 16)
                    if i >= 1:
                        sp.wait_ge(s_free, a_use(i - 1, "O", ST - 1) + 1)
                    sp.dma_start(xr[:], x_tiles[i]).then_inc(s_x, 16)
                    if i >= 1:
                        sp.wait_ge(s_yout, i)
                        sp.dma_start(out_tiles[i - 1], y_out[:]).then_inc(s_y, 16)
                sp.wait_ge(s_yout, NTILES)
                sp.dma_start(out_tiles[NTILES - 1], y_out[:]).then_inc(s_y, 16)
                sp.wait_ge(s_y, 16 * NTILES)

            @block.gpsimd
            def _(pool):
                g = nc.gpsimd

                def before(i):
                    pool.wait_ge(s_oamax, i + 1)
                    g.partition_all_reduce(o_all[:], o_amax[:], P, ABSMAX).then_inc(s_oall, 1)
                    pool.wait_ge(s_x, 16 * (i + 1))
                    for s in range(ST):
                        last = g.tensor_tensor(xr[:, s, :], xr[:, s, :], bo_bc[0:SUB, :], ALU.add)
                    last.then_inc(s_xb, 1)

                before(0)
                for i in range(NTILES):
                    pool.wait_ge(s_normed, i + 1)
                    if i >= 1:
                        pool.wait_ge(s_yout, i)
                    g.tensor_scalar(res[:], x1[:], 1.0, 1.0, ALU.mult, ALU.mult).then_inc(s_res, 1)
                    pool.wait_ge(s_ramax, i + 1)
                    g.partition_all_reduce(r_all[:], r_amax1[:], P, ABSMAX).then_inc(s_rall, 1)
                    if i + 1 < NTILES:
                        before(i + 1)
                    for j in range(HCH):
                        n = HCH * i + j
                        pool.wait_ge(s_rhigh, n + 1)
                        g.tensor_tensor(r_s[:, j, 1, :], sq[:, n % SQN, :], r_s[:, j, 0, :],
                                        ALU.subtract).then_inc(s_rlow, 1)

            @block.scalar
            def _(act):
                a = nc.scalar

                def before(i):
                    act.wait_ge(s_oscale, i + 1)
                    if i >= 1:
                        act.wait_ge(s_full, a_use(i - 1, "O", ST - 1) + 1)
                    a.activation(o_s[:, 0], o32[:], ACT.Copy, scale=o_scale[:]).then_inc(s_ohigh, 1)

                def transposed(i):
                    for d in range(DCH):
                        use = a_use(i, "T", d)
                        act.wait_ge(s_full, use + 1)
                        if d == 0 and i >= 1:
                            act.wait_ge(s_fc, HCH * i)
                        a.activation(xT[:, 0, d, :], ps[:, use % RING_A, 0:TT], ACT.Copy,
                                     scale=2.0 ** X_EXP).then_inc(s_thigh, 1)
                    act.wait_ge(s_zfull, i + 1)
                    a.activation(z32[:], ps[:, 7, 0:TT], ACT.Copy, scale=z_scale[:]).then_inc(s_z32, 1)

                before(0)
                transposed(0)
                for i in range(NTILES):
                    for j in range(HCH):
                        use = HCH * i + j
                        act.wait_ge(s_fc, use + 1)
                        if j == 0 and i >= 1:
                            act.wait_ge(s_full, a_use(i - 1, "Y", ST - 1) + 1)
                        a.activation(r[:, j, :], ps[:, 3 + use % RING_B, 0:TT], ACT.Relu,
                                     scale=relu_scale[:, j:j + 1]).then_inc(s_relu, 1)
                    if i + 1 < NTILES:
                        before(i + 1)
                    act.wait_ge(s_rscale, i + 1)
                    for j in range(HCH):
                        n = HCH * i + j
                        if n >= SQN:
                            act.wait_ge(s_rlow, n - SQN + 1)
                        a.activation(sq[:, n % SQN, :], r[:, j, :], ACT.Square, scale=g_scale[:]).then_inc(s_sq, 1)
                    if i + 1 < NTILES:
                        transposed(i + 1)

            @block.vector
            def _(dve):
                v = nc.vector
                own = Own(dve, s_own)

                def before(i):
                    dve.wait_ge(s_o, 32 * (i + 1))
                    v.tensor_reduce(o_amax[:], o32[:], AX.XY, ALU.max, apply_absolute_value=True).then_inc(s_oamax, 1)
                    dve.wait_ge(s_oall, i + 1)
                    pow2_scale(v, own, o_all[:], fld[:, 0:1], o_scale[:], o_inv[:])
                    v.tensor_tensor(o_inv[:], o_inv[:], attn_w[:], ALU.mult).then_inc(s_oscale, 1)
                    dve.wait_ge(s_ohigh, i + 1)
                    v.scalar_tensor_tensor(out=o_s[:, 1], in0=o32[:], scalar=o_scale[:], in1=o_s[:, 0],
                                           op0=ALU.mult, op1=ALU.subtract).then_inc(s_ocut, 1)

                def residual(i):
                    dve.wait_ge(s_xb, i + 1)
                    if i >= 1:
                        dve.wait_ge(s_res, i)
                    for s in range(ST):
                        use = a_use(i, "O", s)
                        dve.wait_ge(s_full, use + 1)
                        v.scalar_tensor_tensor(out=x1[:, s, :], in0=ps[0:SUB, use % RING_A, :], scalar=o_inv[0:SUB, :],
                                               in1=xr[:, s, :], op0=ALU.mult, op1=ALU.add).then_inc(s_free, 1)
                    dve.wait_ge(s_free, a_use(i, "O", ST - 1) + 1)
                    layer_norm(v, own, x1, stats, mean_var, work, y_bits[:], xn).then_inc(s_normed, 1)

                def transposed(i):
                    for d in range(DCH):
                        use = a_use(i, "T", d)
                        dve.wait_ge(s_thigh, DCH * i + d + 1)
                        v.scalar_tensor_tensor(out=xT[:, 1, d, :], in0=ps[:, use % RING_A, 0:TT], scalar=2.0 ** X_EXP,
                                               in1=xT[:, 0, d, :], op0=ALU.mult, op1=ALU.subtract).then_inc(s_free, 1)
                    dve.wait_ge(s_z32, i + 1)
                    own(v.tensor_copy(z_part[0][:], z32[:]))
                    own(v.tensor_tensor(z_rest[0][:], z32[:], z_part[0][:], ALU.subtract))
                    own(v.tensor_copy(z_part[1][:], z_rest[0][:]))
                    own(v.tensor_tensor(z_rest[1][:], z_rest[0][:], z_part[1][:], ALU.subtract))
                    own(v.tensor_scalar(z_acc[:], z_part[0][:], masks[:, 0:1], None, ALU.mult))
                    own(v.scalar_tensor_tensor(out=z_acc[:], in0=z_part[1][:], scalar=masks[:, 1:2], in1=z_acc[:],
                                               op0=ALU.mult, op1=ALU.add))
                    v.scalar_tensor_tensor(out=z[:], in0=z_rest[1][:], scalar=masks[:, 2:3], in1=z_acc[:],
                                           op0=ALU.mult, op1=ALU.add).then_inc(s_zready, 1)

                before(0)
                residual(0)
                transposed(0)
                for i in range(NTILES):
                    for j in range(HCH):
                        dve.wait_ge(s_relu, HCH * i + j + 1)
                        last = v.tensor_reduce(r_amax[:, j:j + 1], r[:, j, :], AX.X, ALU.max)
                    own(last)
                    v.tensor_reduce(r_amax1[:], r_amax[:], AX.X, ALU.max).then_inc(s_ramax, 1)
                    if i + 1 < NTILES:
                        before(i + 1)
                    dve.wait_ge(s_rall, i + 1)
                    pow2_scale(v, own, r_all[:], fld[:, 1:2], g_scale[:], g_inv[:], 260)
                    v.tensor_tensor(g_inv[:], g_inv[:], g_inv[:], ALU.mult).then_inc(s_rscale, 1)
                    for j in range(HCH):
                        n = HCH * i + j
                        dve.wait_ge(s_sq, n + 1)
                        v.tensor_copy(r_s[:, j, 0, :], sq[:, n % SQN, :]).then_inc(s_rhigh, 1)
                    if i + 1 < NTILES:
                        residual(i + 1)
                    dve.wait_ge(s_res, i + 1)
                    if i >= 1:
                        dve.wait_ge(s_y, 16 * i)
                    for s in range(ST):
                        use = a_use(i, "Y", s)
                        dve.wait_ge(s_full, use + 1)
                        v.scalar_tensor_tensor(out=y_out[:, s, :], in0=ps[0:SUB, use % RING_A, :], scalar=g_inv[0:SUB, :],
                                               in1=proj_bc[0:SUB, :], op0=ALU.mult, op1=ALU.mult).then_inc(s_free, 1)
                        dve.wait_ge(s_free, use + 1)
                        last = v.tensor_tensor(y_out[:, s, :], y_out[:, s, :], res[:, s, :], ALU.add)
                    last.then_inc(s_yout, 1)
                    if i + 1 < NTILES:
                        transposed(i + 1)

            @block.tensor
            def _(pe):
                mm = nc.tensor.matmul

                def bank_a(use):
                    if use >= RING_A:
                        pe.wait_ge(s_free, use - RING_A + 1)
                    return ps[:, use % RING_A, :]

                def project(i):
                    pe.wait_ge(s_ocut, i + 1)
                    for s in range(ST):
                        bank = bank_a(a_use(i, "O", s))
                        k = 0
                        for oh, wh in ((0, 0), (0, 1), (1, 0)):
                            for d in range(ICH):
                                last = mm(bank[0:SUB, :], o_s[:, oh, d, s * SUB:(s + 1) * SUB], wo_s[:, wh, d, :],
                                          start=(k == 0), stop=(k == 3 * ICH - 1))
                                k += 1
                        last.then_inc(s_full, 1)

                def transposes(i):
                    pe.wait_ge(s_normed, i + 1)
                    for d in range(DCH):
                        bank = bank_a(a_use(i, "T", d))
                        for s in range(ST):
                            last = nc.tensor.transpose(bank[:, s * SUB:(s + 1) * SUB], xn[:, s, d * P:(d + 1) * P],
                                                       ident[0:SUB, 0:SUB])
                        last.then_inc(s_full, 1)
                    pe.wait_ge(s_free, a_use(i, "T", DCH - 1) + 1)
                    if i >= 1:
                        pe.wait_ge(s_z32, i)
                    k = 0
                    for wh, xh in ((0, 0), (0, 1), (1, 0)):
                        for d in range(DCH):
                            last = mm(ps[:, 7, 0:TT], fb_s[:, wh, d, :], xT[:, xh, d, :], start=(k == 0),
                                      stop=(k == 3 * DCH - 1))
                            k += 1
                    last.then_inc(s_zfull, 1)

                def hidden(i):
                    for j in range(HCH):
                        use = HCH * i + j
                        if use >= RING_B:
                            pe.wait_ge(s_relu, use - RING_B + 1)
                        bank = ps[:, 3 + use % RING_B, 0:TT]
                        for k in range(2 * DCH):
                            mm(bank, fc_t[:, k % DCH, j * P:(j + 1) * P], xT[:, k // DCH, k % DCH, :],
                               start=(k == 0), stop=False)
                        if j == 0:
                            pe.wait_ge(s_zready, i + 1)
                        mm(bank, u_t[:, j * P:(j + 1) * P], z[:], start=False, stop=True).then_inc(s_fc, 1)

                def result(i):
                    for s in range(ST):
                        bank = bank_a(a_use(i, "Y", s))
                        for j in range(HCH):
                            if s == 0:
                                pe.wait_ge(s_rlow, HCH * i + j + 1)
                            for half in range(2):
                                last = mm(bank[0:SUB, :], r_s[:, j, half, s * SUB:(s + 1) * SUB], proj_t[:, j, :],
                                          start=(j == 0 and half == 0), stop=(j == HCH - 1 and half == 1))
                        last.then_inc(s_full, 1)

                project(0)
                transposes(0)
                for i in range(NTILES):
                    hidden(i)
                    if i + 1 < NTILES:
                        project(i + 1)
                    result(i)
                    if i + 1 < NTILES:
                        transposes(i + 1)


def kernel(x, ctx_768, g_xattn, g_ffn, L0_xattn_Wq, L0_xattn_Wk, L0_xattn_Wv, L0_xattn_Wo, L0_xattn_bo,
           L0_ffn_fast_b, L0_ffn_w_fc, L0_ffn_w_proj, L0_ffn_u, L0_ffn_v, L0_ffn_gate):
    import concourse.bacc as bacc
    from concourse.bass_utils import run_bass_kernel_spmd

    laid = {
        "x": np.ascontiguousarray(np.asarray(x).reshape(T, D)),
        "ctx_t": np.ascontiguousarray(np.asarray(ctx_768).transpose(0, 2, 1)),
        "g_xattn": np.asarray(g_xattn).reshape(1, 1),
        "g_ffn": np.asarray(g_ffn).reshape(1, 1),
        "wq": np.ascontiguousarray(L0_xattn_Wq),
        "wk": np.ascontiguousarray(L0_xattn_Wk),
        "wv": np.ascontiguousarray(L0_xattn_Wv),
        "wo": np.ascontiguousarray(L0_xattn_Wo),
        "bo": np.asarray(L0_xattn_bo).reshape(1, D),
        "fast_b_t": np.ascontiguousarray(np.asarray(L0_ffn_fast_b).T),
        "w_fc": np.ascontiguousarray(L0_ffn_w_fc),
        "w_proj": np.ascontiguousarray(L0_ffn_w_proj),
        "u": np.ascontiguousarray(L0_ffn_u),
        "v_low": np.ascontiguousarray(L0_ffn_v),
        "gate": np.asarray(L0_ffn_gate).reshape(1, 1),
    }
    nc = bacc.Bacc("TRN2", target_bir_lowering=False, num_devices=1)
    args = {n: nc.dram_tensor(f"in_{n}", a.shape, mybir.dt.from_np(a.dtype), kind="ExternalInput").ap()
            for n, a in laid.items()}
    out = nc.dram_tensor("out", (T, D), F32, kind="ExternalOutput").ap()
    flamingo_block(nc, out=out, **args)
    ran = run_bass_kernel_spmd(nc, [{f"in_{n}": a for n, a in laid.items()}], core_ids=[0])
    return ran.results[0]["out"].reshape(B, NQ, D)
```

```python
from contextlib import ExitStack

import numpy as np

import concourse.bass as bass
from concourse import mybir

F32 = mybir.dt.float32
F16 = mybir.dt.float16
BF16 = mybir.dt.bfloat16
I32 = mybir.dt.int32
ALU = mybir.AluOpType
ACT = mybir.ActivationFunctionType
AX = mybir.AxisListType
ABSMAX = bass.bass_isa.ReduceOp.absmax


P = 128
B, NQ, D = 8, 224, 512
NK, DC = 750, 384
H, DH, HID, R = 16, 64, 2048, 16
INNER = H * DH
T = B * NQ
QT = NQ // 2
KT, NKT = 125, NK // 125
KH = NK // 2
GH = H // 2
DCH, CCH, ICH, HCH = D // P, DC // P, INNER // P, HID // P
TT, ST = 2 * NQ, 4
SUB = TT // ST
NTILES = T // TT
COPIES = P // R
EPS = 1e-5
Z_PART = [0, 0, 0, 1, 1, 1, 2, 2]
U_PART = [0, 1, 2, 0, 1, 2, 0, 1]

X_EXP = 11
Q_EXP, KV_EXP, P_EXP = -20, -24, 14
INV_SQRT_MAGIC = 0x5F3759DF

C_WQ, C_WK, C_WV, C_WO, C_FB = range(5)


def pow2_scale(v, own, amax, field, scale, inverse, exponent_sum=268):
    own(v.tensor_scalar(field, amax.bitcast(I32), 23, None, ALU.logical_shift_right))
    own(v.tensor_scalar(field, field, -1.0, float(exponent_sum), ALU.mult, ALU.add))
    own(v.tensor_scalar(field, field, 253.0, 1.0, ALU.min, ALU.max))
    own(v.tensor_scalar(scale.bitcast(I32), field, 23, None, ALU.logical_shift_left))
    own(v.tensor_scalar(field, field, -1.0, 254.0, ALU.mult, ALU.add))
    own(v.tensor_scalar(inverse.bitcast(I32), field, 23, None, ALU.logical_shift_left))


POW2_STEPS = 6


class Own:

    def __init__(self, eng, sem, start=0):
        self.eng, self.sem, self.start, self.n = eng, sem, start, 0

    def __call__(self, instruction):
        self.n += 1
        instruction.then_inc(self.sem, 1)
        self.eng.wait_ge(self.sem, self.start + self.n)


def layer_norm(v, own, x, stats, mean_var, work, y_bits, out, passed=None):
    for s in range(ST):
        last = v.bn_stats(stats[:, s, :], x[:, s, :])
    own(last)
    if passed is not None:
        own.eng.sem_inc(passed, 1)
    for s in range(ST):
        last = v.bn_aggr(mean_var[:, s, :], stats[:, s, :])
    own(last)
    var, sq = work[:, 0, :], work[:, 1, :]
    y = y_bits.bitcast(F32)
    own(v.tensor_scalar(var, mean_var[:, :, 1], EPS, None, ALU.add))
    own(v.tensor_scalar(y_bits, var.bitcast(I32), 1, None, ALU.logical_shift_right))
    own(v.tensor_scalar(y_bits, y_bits, -1.0, float(INV_SQRT_MAGIC), ALU.mult, ALU.add))
    for _ in range(3):
        own(v.tensor_tensor(sq, y, y, ALU.mult))
        own(v.tensor_tensor(sq, sq, var, ALU.mult))
        own(v.tensor_scalar(sq, sq, -0.5, 1.5, ALU.mult, ALU.add))
        own(v.tensor_tensor(y, y, sq, ALU.mult))
    for s in range(ST):
        last = v.tensor_scalar(out[:, s, :], x[:, s, :], mean_var[:, s, 0:1], y[:, s:s + 1],
                               ALU.subtract, ALU.mult)
    return last


NORM_STEPS = 5 + 12


def flamingo_block(nc, x, ctx_t, g_xattn, g_ffn, wq, wk, wv, wo, bo, fast_b_t, w_fc, w_proj, u, v_low, gate, out):
    x_tiles = x.rearrange("(i s p) d -> i p s d", s=ST, p=SUB)
    out_tiles = out.rearrange("(i s p) d -> i p s d", s=ST, p=SUB)
    ctx_v = ctx_t.rearrange("b (c p) k -> b p c k", p=P)
    q_dram = nc.dram_tensor("q_halves", (2, B, INNER, NQ), F16, kind="Internal").ap()
    o_dram = nc.dram_tensor("o_halves", (2, B, INNER, NQ), F16, kind="Internal").ap()

    with ExitStack() as keep:
        def sb(name, shape, dt, ctx=keep):
            return ctx.enter_context(nc.sbuf_tensor(name, shape, dt))

        def sem(name, ctx=keep):
            return ctx.enter_context(nc.semaphore(name))

        ps = keep.enter_context(nc.psum_tensor("ps", [P, 8, 512], F32))

        ident = sb("ident", [P, P], F32)
        ident16 = sb("ident16", [P, P], F16)
        ident_b = sb("ident_b", [P, P], BF16)
        ones = sb("ones", [P, P], F32)
        masks = sb("masks", [P, 3], F32)
        scal = sb("scal", [P, 3], F32)
        tanh_g = sb("tanh_g", [P, 2], F32)
        bo_bc = sb("bo_bc", [P, D], F32)
        proj_bc = sb("proj_bc", [P, D], F32)
        fc_scale = sb("fc_scale", [P, HCH], F32)
        relu_scale = sb("relu_scale", [P, HCH], F32)
        fc_t = sb("fc_t", [P, DCH, HID], F16)
        proj_t = sb("proj_t", [P, HCH, D], F16)
        u_t = sb("u_t", [P, HID], BF16)
        w_scale = sb("w_scale", [P, 5], F32)
        w_inv = sb("w_inv", [P, 5], F32)
        wo_s = sb("wo_s", [P, 2, ICH, D], F16)
        fb_s = sb("fb_s", [P, 2, DCH, P], F16)
        score_w = sb("score_w", [P, 1], F32)
        z_scale = sb("z_scale", [P, 1], F32)
        attn_w = sb("attn_w", [P, 1], F32)
        attn_scale = sb("attn_scale", [P, B], F32)

        st_ctx = keep.enter_context(ExitStack())
        stage_b = sb("stage_b", [P, ICH * D], F32, st_ctx)
        ctx32 = stage_b[:, 0:CCH * NK].rearrange("p (c k) -> p c k", c=CCH)
        ctx_s = sb("ctx_s", [P, 2, CCH, NK], F16, st_ctx)
        c_amax = sb("c_amax", [P, 1], F32, st_ctx)
        c_all = sb("c_all", [P, 1], F32, st_ctx)
        c_field = sb("c_field", [P, 1], I32, st_ctx)
        c_scale = sb("c_scale", [P, 1], F32, st_ctx)
        c_inv = sb("c_inv", [P, 1], F32, st_ctx)
        kv_ctx = keep.enter_context(ExitStack())
        wk_s = sb("wk_s", [P, 2, CCH, INNER], F16, kv_ctx)
        wv_s = sb("wv_s", [P, 2, CCH, INNER], F16, kv_ctx)

        with ExitStack() as c:
            wq_s = sb("wq_s", [P, 2, DCH, INNER], F16, c)
            stage_a = sb("stage_a", [P, DCH * INNER], F32, c)
            rows32 = sb("rows32", [P, 2, HID], F32, c)
            signs = sb("signs", [P, HID], F16, c)
            tern = sb("tern", [P, HID], F16, c)
            mag = sb("mag", [P, HCH + DCH], F32, c)
            thr = sb("thr", [P, HCH + DCH], F32, c)
            pj_scale = sb("pj_scale", [P, DCH], F32, c)
            rden = sb("rden", [P, HCH], F32, c)
            u32 = sb("u32", [P, HCH, R], F32, c)
            u_f = sb("u_f", [P, HCH, R], F32, c)
            u_parts = [sb(f"u_part{n}", [P, HCH, R], BF16, c) for n in range(3)]
            u_rep = sb("u_rep", [P, HCH, COPIES, R], BF16, c)
            fb32 = sb("fb32", [P, DCH, P], F32, c)
            diag = fb32
            v32 = sb("v32", [R, D], F32, c)
            fbt = sb("fbt", [R, R], F32, c)
            fbt_rep = sb("fbt_rep", [R, COPIES, R], F32, c)
            amax = sb("amax", [P, 5], F32, c)
            amax_all = sb("amax_all", [P, 5], F32, c)
            field = sb("field", [P, 5], I32, c)
            xt = sb("xt", [SUB, ST, D], F32, c)
            xn = sb("xn", [SUB, ST, D], F32, c)
            stats = sb("q_stats", [SUB, ST, 6], F32, c)
            mean_var = sb("q_mean_var", [SUB, ST, 2], F32, c)
            work = sb("q_work", [SUB, 2, ST], F32, c)
            y_bits = sb("q_y", [SUB, ST], I32, c)
            xT = sb("xT", [P, 2, DCH, TT], F16, c)
            QO = 4
            q_out = sb("q_out", [P, QO, 2, TT], F16, c)

            s_x, s_normed, s_own = sem("x_in", c), sem("x_normed", c), sem("dve_own", c)
            s_full, s_high, s_free = sem("q_full", c), sem("q_high", c), sem("q_free", c)
            s_stored = [sem(f"q_stored{n}", c) for n in range(QO)]
            s_const, s_ident = sem("const_made", c), sem("ident_copied", c)
            s_small, s_bo, s_lowrank = sem("small_in", c), sem("bo_in", c), sem("lowrank_in", c)
            s_tanh, s_rep, s_fb_full = sem("tanh_done", c), sem("fbt_copies", c), sem("fb_full", c)
            W = ["wq", "wk", "wv", "wo", "fb"]
            s_win = {n: sem(f"{n}_in", c) for n in W[:4] + ["ctx"]}
            s_amax, s_all, s_scale, s_hi, s_scaled, s_cut = (
                {n: sem(f"{n}_{what}", c) for n in W + ["ctx"]}
                for what in ("amax", "all", "scale", "high", "scaled", "cut"))
            s_rows = [sem(f"rows_in{n}", c) for n in range(2)]
            s_mag, s_thr, s_sign, s_tern = (sem(n, c) for n in ("row_sum", "threshold", "signs_made", "tern_made"))
            s_tfull, s_tcopied = sem("tp_full", c), sem("tp_copied", c)
            s_urep, s_diag, s_bc = sem("u_copies", c), sem("diag_made", c), sem("proj_bc_full", c)

            w32 = {"wq": stage_a[:], "wk": stage_b[:, 0:CCH * INNER], "wv": stage_a[:, 0:CCH * INNER],
                   "wo": stage_b[:], "fb": fb32[:].rearrange("p c n -> p (c n)"), "ctx": stage_b[:, 0:CCH * NK]}
            halves = {n: (t[:, 0].rearrange("p c n -> p (c n)"), t[:, 1].rearrange("p c n -> p (c n)"))
                      for n, t in (("wq", wq_s), ("wk", wk_s), ("wv", wv_s), ("wo", wo_s), ("fb", fb_s), ("ctx", ctx_s))}
            scales = {n: (amax[:, k:k + 1], amax_all[:, k:k + 1], field[:, k:k + 1], w_scale[:, k:k + 1],
                          w_inv[:, k:k + 1]) for k, n in enumerate(W)}
            scales["ctx"] = (c_amax[:], c_all[:], c_field[:], c_scale[:], c_inv[:])

            USES, RING = DCH + ICH, 4
            GROUPS = 2 * DCH
            G_FC = HCH // 4
            side = (["fb.make", "wk.max", "wk.scale", "wv.max", "wk.cut", "wv.scale", "fb.max", "wv.cut", "wo.max",
                     "fb.scale", "fb.cut", "wo.scale", "wo.cut"]
                    + [f"g{n}.{what}" for n in range(GROUPS) for what in ("sum", "sign", "turn")]
                    + ["ctx.max", "u.make", "ctx.scale", "u.turn", "ctx.cut", "last"])
            parts = [("norm", 0)] + [("use", n) for n in range(DCH)]
            parts += [("side", w) for w in ("wq.max", "const", "wq.scale", "wq.cut")]
            spots = NTILES * ICH
            placed = 0
            for i in range(NTILES):
                for n in range(ICH):
                    parts.append(("use", USES * i + DCH + n))
                    upto = len(side) * (i * ICH + n + 1) // spots
                    parts += [("side", w) for w in side[placed:upto]]
                    placed = upto
                    if n == 1 and i + 1 < NTILES:
                        parts.append(("norm", i + 1))
                if i + 1 < NTILES:
                    parts += [("use", USES * (i + 1) + d) for d in range(DCH)]

            block = c.enter_context(nc.Block())

            @block.sync
            def _(sp):
                def load_rows(n):
                    if n < G_FC:
                        src = w_fc.rearrange("(g j p) d -> g p j d", j=4, p=P)[n]
                        dst = rows32[:, n % 2, :].rearrange("p (j d) -> p j d", j=4)
                    else:
                        src = w_proj.rearrange("(g p) h -> g p h", p=P)[n - G_FC]
                        dst = rows32[:, n % 2, :]
                    sp.dma_start(dst, src).then_inc(s_rows[n % 2], 16)

                def load_w(name, src):
                    dst = w32[name].rearrange("p (c n) -> p c n", c=src.shape[0] // P)
                    sp.dma_start(dst, src.rearrange("(c p) n -> p c n", p=P)).then_inc(s_win[name], 16)

                def store(use):
                    i, n = use // USES, use % USES - DCH
                    k = ICH * i + n
                    sp.wait_ge(s_free, use + 1)
                    for b in range(2):
                        dst = q_dram.rearrange("a (i b) (c p) t -> i b c p a t", b=2, p=P)[i, b, n]
                        sp.dma_start(dst, q_out[:, k % QO, :, b * NQ:(b + 1) * NQ]).then_inc(s_stored[k % QO], 16)

                sp.dma_start(xt[:], x_tiles[0]).then_inc(s_x, 16)
                load_w("wq", wq)
                load_w("wk", wk)
                load_rows(0)
                load_rows(1)
                for what, n in parts:
                    if what == "use" and n % USES >= DCH:
                        store(n)
                    elif what == "norm" and n + 1 < NTILES:
                        sp.wait_ge(s_normed, n + 1)
                        sp.dma_start(xt[:], x_tiles[n + 1]).then_inc(s_x, 16)
                    elif n == "wq.cut":
                        sp.wait_ge(s_cut["wq"], 1)
                        load_w("wv", wv)
                    elif n == "wk.cut":
                        sp.wait_ge(s_cut["wk"], 1)
                        load_w("wo", wo)
                    elif n == "wo.cut":
                        sp.wait_ge(s_cut["wo"], 1)
                        sp.dma_start(ctx32, ctx_v[0]).then_inc(s_win["ctx"], 16)
                    elif what == "side" and n[0] == "g" and n.endswith("sign"):
                        g = int(n[1])
                        if g + 2 < GROUPS:
                            sp.wait_ge(s_tern, g + 1)
                            load_rows(g + 2)
                for k in range(QO):
                    sp.wait_ge(s_stored[k], 32 * NTILES * ICH // QO)

            @block.gpsimd
            def _(pool):
                g = nc.gpsimd
                g.memset(ident[:], 0.0).then_inc(s_const, 1)
                g.memset(masks[:], 1.0).then_inc(s_const, 1)
                g.memset(ones[:], 1.0).then_inc(s_const, 1)
                pool.wait_ge(s_const, 3)
                g.affine_select(out=ident[:], in_=ident[:], compare_op=ALU.not_equal, fill=1.0, base=0,
                                pattern=[[-1, P]], channel_multiplier=1).then_inc(s_const, 1)
                for n, first in ((1, R * Z_PART.index(1)), (2, R * Z_PART.index(2))):
                    g.affine_select(out=masks[:, n:n + 1], in_=masks[:, n:n + 1], compare_op=ALU.is_ge, fill=0.0,
                                    base=-first, pattern=[[0, 1]], channel_multiplier=1).then_inc(s_const, 1)
                for what, n in parts:
                    if what != "side" or "." not in n:
                        continue
                    name, does = n.split(".")
                    if does == "max":
                        pool.wait_ge(s_amax[name], 1)
                        g.partition_all_reduce(scales[name][1], scales[name][0], P, ABSMAX).then_inc(s_all[name], 1)
                    elif does == "cut" and name in ("wk", "wv", "wo"):
                        pool.wait_ge(s_hi[name], 1)
                        g.tensor_scalar(w32[name], w32[name], scales[name][3], 1.0, ALU.mult,
                                        ALU.mult).then_inc(s_scaled[name], 1)
                        pool.wait_ge(s_scaled[name], 1)
                        g.tensor_tensor(halves[name][1], w32[name], halves[name][0], ALU.subtract).then_inc(s_cut[name], 1)

            @block.scalar
            def _(act):
                a = nc.scalar
                for n, g in enumerate((g_xattn, g_ffn, gate)):
                    act.dma_start(scal[:, n:n + 1], g.to_broadcast([P, 1])).then_inc(s_small, 16)
                act.dma_start(u32[:], u.rearrange("(j p) r -> p j r", p=P)).then_inc(s_small, 16)
                act.dma_start(v32[:], v_low).then_inc(s_lowrank, 16)
                act.dma_start(fbt[:], fast_b_t).then_inc(s_lowrank, 16)
                act.dma_start(bo_bc[:], bo.to_broadcast([P, D])).then_inc(s_bo, 16)

                def copy_turned(t):
                    act.wait_ge(s_tfull, t + 1)
                    bank = ps[:, 4 + t % RING, :]
                    if t < 2 * G_FC:
                        g, d = t // 2, 2 * (t % 2)
                        dst = fc_t[:, d:d + 2, g * 4 * P:(g + 1) * 4 * P]
                        src = bank.bitcast(F16).rearrange("p (d h) -> p d h", d=2)
                    elif t < 2 * GROUPS:
                        g, j = t // 2 - G_FC, 8 * (t % 2)
                        dst = proj_t[:, j:j + 8, g * P:(g + 1) * P]
                        src = bank.bitcast(F16).rearrange("p (j n) -> p j n", j=8)
                    else:
                        n = t - 2 * GROUPS
                        dst, src = u_t[:, n * 8 * P:(n + 1) * 8 * P], bank.bitcast(BF16)
                    a.activation(dst, src, ACT.Copy).then_inc(s_tcopied, 1)

                for what, n in parts:
                    if what == "use":
                        act.wait_ge(s_full, n + 1)
                        src, m = ps[:, n % RING, 0:TT], n % USES
                        if m < DCH:
                            a.activation(xT[:, 0, m, :], src, ACT.Copy, scale=2.0 ** X_EXP).then_inc(s_high, 1)
                        else:
                            k = ICH * (n // USES) + m - DCH
                            if k >= QO:
                                act.wait_ge(s_stored[k % QO], 32 * (k // QO))
                            a.activation(q_out[:, k % QO, 0, :], src, ACT.Copy, scale=2.0 ** Q_EXP).then_inc(s_high, 1)
                        continue
                    if n == "const":
                        act.wait_ge(s_small, 64)
                        a.activation(tanh_g[:], scal[:, 0:2], ACT.Tanh).then_inc(s_tanh, 1)
                    if what == "norm" or "." not in n:
                        continue
                    name, does = n.split(".")
                    if does == "scale":
                        act.wait_ge(s_scale[name], 1)
                        a.activation(halves[name][0], w32[name], ACT.Copy, scale=scales[name][3]).then_inc(s_hi[name], 1)
                    elif does == "sum":
                        g = int(name[1])
                        act.wait_ge(s_rows[g % 2], 16 * (g // 2 + 1))
                        if g >= 1:
                            act.wait_ge(s_tern, g)
                        if g < G_FC:
                            for j in range(4):
                                cols = slice(j * D, (j + 1) * D)
                                last = a.activation(signs[:, cols], rows32[:, g % 2, cols], ACT.Abs,
                                                    accum_out=mag[:, 4 * g + j:4 * g + j + 1])
                        else:
                            k = HCH + g - G_FC
                            last = a.activation(signs[:], rows32[:, g % 2, :], ACT.Abs, accum_out=mag[:, k:k + 1])
                        last.then_inc(s_mag, 1)
                    elif does == "sign":
                        g = int(name[1])
                        act.wait_ge(s_thr, g + 1)
                        if g < G_FC:
                            for j in range(4):
                                cols = slice(j * D, (j + 1) * D)
                                last = a.activation(signs[:, cols], rows32[:, g % 2, cols], ACT.Sign,
                                                    bias=thr[:, 4 * g + j:4 * g + j + 1])
                        else:
                            k = HCH + g - G_FC
                            last = a.activation(signs[:], rows32[:, g % 2, :], ACT.Sign, bias=thr[:, k:k + 1])
                        last.then_inc(s_sign, 1)
                    elif does == "turn":
                        first = 2 * GROUPS if name == "u" else 2 * int(name[1])
                        copy_turned(first)
                        copy_turned(first + 1)

            @block.vector
            def _(dve):
                v = nc.vector
                own = Own(dve, s_own)

                def side_part(n):
                    if n == "const":
                        dve.wait_ge(s_tanh, 1)
                        dve.wait_ge(s_bo, 16)
                        v.tensor_scalar(bo_bc[:], bo_bc[:], tanh_g[:, 0:1], None, ALU.mult)
                        return
                    if n == "last":
                        own(v.tensor_scalar(pj_scale[:], pj_scale[:], tanh_g[:, 1:2], None, ALU.mult))
                        for j in range(DCH):
                            last = v.tensor_scalar(diag[:, j, :], ident[:], pj_scale[:, j:j + 1], None, ALU.mult)
                        last.then_inc(s_diag, 1)
                        own(v.tensor_tensor(score_w[:], w_inv[:, C_WQ:C_WQ + 1], w_inv[:, C_WK:C_WK + 1], ALU.mult))
                        v.tensor_scalar(score_w[:], score_w[:], 2.0 ** (-Q_EXP - X_EXP - KV_EXP) * DH ** -0.5, None, ALU.mult)
                        v.tensor_scalar(z_scale[:], w_inv[:, C_FB:C_FB + 1], 2.0 ** -X_EXP, None, ALU.mult)
                        own(v.tensor_tensor(attn_w[:], w_inv[:, C_WO:C_WO + 1], w_inv[:, C_WV:C_WV + 1], ALU.mult))
                        own(v.tensor_scalar(attn_w[:], attn_w[:], tanh_g[:, 0:1], 2.0 ** -KV_EXP, ALU.mult, ALU.mult))
                        v.tensor_scalar(relu_scale[:], fc_scale[:], 2.0 ** -X_EXP, None, ALU.mult)
                        dve.wait_ge(s_bc, 1)
                        v.tensor_copy(proj_bc[:], ps[:, 4, :])
                        return
                    name, does = n.split(".")
                    if n == "fb.make":
                        dve.wait_ge(s_lowrank, 32)
                        for k in range(COPIES):
                            last = v.tensor_copy(fbt_rep[:, k, :], fbt[:])
                        last.then_inc(s_rep, 1)
                    elif does == "max":
                        if name == "fb":
                            dve.wait_ge(s_fb_full, 1)
                            own(v.tensor_copy(w32["fb"], ps[:, 4, :]))
                        else:
                            dve.wait_ge(s_win[name], 16)
                        v.tensor_reduce(scales[name][0], w32[name], AX.X, ALU.max,
                                        apply_absolute_value=True).then_inc(s_amax[name], 1)
                    elif does == "scale":
                        _, all_max, f, scale, inverse = scales[name]
                        dve.wait_ge(s_all[name], 1)
                        pow2_scale(v, own, all_max, f, scale, inverse)
                        v.memset(scales[name][0], 0.0).then_inc(s_scale[name], 1)
                    elif does == "cut" and name in ("wq", "fb", "ctx"):
                        dve.wait_ge(s_hi[name], 1)
                        v.scalar_tensor_tensor(out=halves[name][1], in0=w32[name], scalar=scales[name][3],
                                               in1=halves[name][0], op0=ALU.mult, op1=ALU.subtract).then_inc(s_cut[name], 1)
                    elif does == "sum":
                        g = int(name[1])
                        dve.wait_ge(s_mag, g + 1)
                        if g < G_FC:
                            cols, scale, width = slice(4 * g, 4 * g + 4), fc_scale[:, 4 * g:4 * g + 4], D
                        else:
                            cols, scale, width = slice(HCH + g - G_FC, HCH + g - G_FC + 1), \
                                pj_scale[:, g - G_FC:g - G_FC + 1], HID
                        own(v.tensor_scalar(scale, mag[:, cols], 1.0 / width, 1e-5, ALU.mult, ALU.max))
                        v.tensor_scalar(thr[:, cols], scale, 0.5, None, ALU.mult).then_inc(s_thr, 1)
                    elif does == "sign":
                        g = int(name[1])
                        dve.wait_ge(s_sign, g + 1)
                        if g >= 1:
                            dve.wait_ge(s_tfull, 2 * g)
                        if g < G_FC:
                            for j in range(4):
                                cols = slice(j * D, (j + 1) * D)
                                last = v.scalar_tensor_tensor(
                                    out=tern[:, cols], in0=rows32[:, g % 2, cols], scalar=thr[:, 4 * g + j:4 * g + j + 1],
                                    in1=signs[:, cols], op0=ALU.is_gt, op1=ALU.min)
                        else:
                            k = HCH + g - G_FC
                            last = v.scalar_tensor_tensor(out=tern[:], in0=rows32[:, g % 2, :], scalar=thr[:, k:k + 1],
                                                          in1=signs[:], op0=ALU.is_gt, op1=ALU.min)
                        last.then_inc(s_tern, 1)
                    elif n == "u.make":
                        own(v.reciprocal(rden[:], fc_scale[:]))
                        own(v.tensor_scalar(rden[:], rden[:], scal[:, 2:3], 2.0 ** X_EXP, ALU.mult, ALU.mult))
                        for j in range(HCH):
                            last = v.tensor_scalar(u_f[:, j, :], u32[:, j, :], rden[:, j:j + 1], None, ALU.mult)
                        own(last)
                        own(v.tensor_copy(u_parts[0][:], u_f[:]))
                        own(v.tensor_tensor(u_f[:], u_f[:], u_parts[0][:], ALU.subtract))
                        own(v.tensor_copy(u_parts[1][:], u_f[:]))
                        own(v.tensor_tensor(u_parts[2][:], u_f[:], u_parts[1][:], ALU.subtract))
                        for k, part in enumerate(U_PART):
                            last = v.tensor_copy(u_rep[:, :, k, :], u_parts[part][:])
                        last.then_inc(s_urep, 1)

                dve.wait_ge(s_const, 6)
                v.tensor_copy(ident16[:], ident[:]).then_inc(s_ident, 1)
                v.tensor_copy(ident_b[:], ident[:]).then_inc(s_ident, 1)
                own(v.tensor_scalar(masks[:, 0:1], masks[:, 1:2], -1.0, 1.0, ALU.mult, ALU.add))
                own(v.tensor_tensor(masks[:, 1:2], masks[:, 1:2], masks[:, 2:3], ALU.subtract))
                for what, n in parts:
                    if what == "norm":
                        dve.wait_ge(s_x, 16 * (n + 1))
                        if n >= 1:
                            dve.wait_ge(s_full, USES * (n - 1) + DCH)
                        layer_norm(v, own, xt, stats, mean_var, work, y_bits[:], xn).then_inc(s_normed, 1)
                    elif what == "use":
                        dve.wait_ge(s_high, n + 1)
                        m = n % USES
                        k = ICH * (n // USES) + m - DCH
                        dst, exp = (xT[:, :, m, :], X_EXP) if m < DCH else (q_out[:, k % QO, :, :], Q_EXP)
                        v.scalar_tensor_tensor(out=dst[:, 1, :], in0=ps[:, n % RING, 0:TT], scalar=2.0 ** exp,
                                               in1=dst[:, 0, :], op0=ALU.mult, op1=ALU.subtract).then_inc(s_free, 1)
                    else:
                        side_part(n)

            @block.tensor
            def _(pe):
                def turn(t, square):
                    if t >= RING:
                        pe.wait_ge(s_tcopied, t - RING + 1)
                    for m in range(8):
                        last = square(m, ps[:, 4 + t % RING, :])
                    last.then_inc(s_tfull, 1)

                pe.wait_ge(s_ident, 2)
                for what, n in parts:
                    if what == "use":
                        i, m = n // USES, n % USES
                        bank = ps[:, n % RING, 0:TT]
                        if n >= RING:
                            pe.wait_ge(s_free, n - RING + 1)
                        if m < DCH:
                            pe.wait_ge(s_normed, i + 1)
                            for s in range(ST):
                                last = nc.tensor.transpose(bank[:, s * SUB:(s + 1) * SUB], xn[:, s, m * P:(m + 1) * P],
                                                           ident[0:SUB, 0:SUB])
                            last.then_inc(s_full, 1)
                            continue
                        q = m - DCH
                        if q == 0:
                            pe.wait_ge(s_free, n)
                            pe.wait_ge(s_cut["wq"], 1)
                        k = 0
                        for wh, xh in ((0, 0), (0, 1), (1, 0)):
                            for d in range(DCH):
                                last = nc.tensor.matmul(bank, wq_s[:, wh, d, q * P:(q + 1) * P], xT[:, xh, d, :],
                                                        start=(k == 0), stop=(k == 3 * DCH - 1))
                                k += 1
                        last.then_inc(s_full, 1)
                    elif n == "fb.make":
                        pe.wait_ge(s_rep, 1)
                        for j in range(DCH):
                            last = nc.tensor.matmul(ps[:, 4, j * P:(j + 1) * P], v32[:, j * P:(j + 1) * P],
                                                    fbt_rep[:].rearrange("p c r -> p (c r)"), start=True, stop=True)
                        last.then_inc(s_fb_full, 1)
                    elif n == "u.turn":
                        pe.wait_ge(s_urep, 1)
                        for k in range(2):
                            turn(2 * GROUPS + k, lambda m, bank: nc.tensor.transpose(
                                bank.bitcast(BF16)[:, m * P:(m + 1) * P],
                                u_rep[:, 8 * k + m, :, :].rearrange("p c r -> p (c r)"), ident_b[:]))
                    elif what == "side" and n.endswith("turn"):
                        g = int(n[1])
                        if g == 0:
                            pe.wait_ge(s_amax["fb"], 1)
                        pe.wait_ge(s_tern, g + 1)
                        for k in range(2):
                            def square(m, bank):
                                if g < G_FC:
                                    col = (m % 4) * D + (2 * k + m // 4) * P
                                else:
                                    col = (8 * k + m) * P
                                return nc.tensor.transpose(bank.bitcast(F16)[:, m * P:(m + 1) * P],
                                                           tern[:, col:col + P], ident16[:])
                            turn(2 * g + k, square)
                    elif n == "last":
                        pe.wait_ge(s_diag, 1)
                        pe.wait_ge(s_tcopied, 2 * GROUPS + 2)
                        for j in range(DCH):
                            last = nc.tensor.matmul(ps[:, 4, j * P:(j + 1) * P], ones[:], diag[:, j, :], start=True,
                                                    stop=True)
                        last.then_inc(s_bc, 1)

        with ExitStack() as c:
            keys = sb("keys", [P, 2, GH, NK], F16, c)
            vals = sb("vals", [KT, 2, NKT, GH, 2, DH], F16, c)
            q_dup = sb("q_dup", [P, 2, 2, GH, NQ], F16, c)
            probs = sb("probs", [QT, 2, 2, NK], F32, c)
            probs_t = sb("probs_t", [KT, 2, NKT, NQ], F16, c)
            o_low = sb("o_low", [DH, NQ], F32, c)
            o_sum = sb("o_sum", [P, 2, NQ], F32, c)
            o_t = sb("o_t", [P, 2, 2, GH // 2, NQ], F16, c)
            row_max = sb("row_max", [QT, 2], F32, c)
            bias = sb("bias", [QT, 2], F32, c)
            row_sum = sb("row_sum", [QT, 2], F32, c)
            row_inv = sb("row_inv", [QT, 2], F32, c)
            score_scale = sb("score_scale", [P, 2], F32, c)
            c_peaks = sb("c_peaks", [P, CCH], F32, c)
            ctx_s1 = sb("ctx_s1", [P, 2, CCH, NK], F16, c)
            ctx_buf = [ctx_s, ctx_s1]

            s_ctx, s_q, s_o = sem("ctx_in", c), [sem(f"q_in{n}", c) for n in range(2)], [sem(f"o_stored{n}", c) for n in range(2)]
            s_amax, s_all = sem("ctx_amax", c), sem("ctx_amax_all", c)
            s_own, s_ctx_scale, s_ctx_high = sem("dve_own4", c), sem("ctx_scale", c), sem("ctx_high", c)
            s_ctx_cut, s_peaks = sem("ctx_cut", c), sem("ctx_peaks", c)
            s_scores, s_rowmax, s_bias = sem("scores_full", c), sem("row_max_done", c), sem("bias_ready", c)
            s_exp, s_inv, s_probs = sem("exp_done", c), sem("row_inv_ready", c), sem("probs_ready", c)
            s_full, s_high, s_free = sem("work_full", c), sem("work_high", c), sem("work_free", c)
            s_keys, s_vals = sem("keys_ready", c), sem("vals_ready", c)
            s_set = sem("score_scale_set", c)
            s_ohigh = sem("o_high", c)
            s_pool_passed, s_ocut = sem("pool_passed", c), sem("o_cut", c)
            RING = 4
            K_UNITS = [[n] for n in range(GH)]
            V_UNITS = [[0], [1], [2], [], [3], [4], [5], []]
            CTX_MAX, SCALE_STEP, CTX_CUT = {0: 0, 1: 1, 2: 2}, 3, {4: 0, 5: 1, 6: 2}
            N_KU, N_VU = GH, NKT
            PAIRS = GH // 2
            FIRST_USES = N_KU + N_VU

            def steps(fill):
                out = []
                for h in range(GH):
                    out += [(h, "T", g) for g in range(3)]
                    if fill:
                        out += [(h, "K", n) for n in K_UNITS[h]] + [(h, "V", n) for n in V_UNITS[h]]
                    out.append((h, "A", 0))
                return out

            USES_GROUP = len(steps(True))
            block = c.enter_context(nc.Block())

            def use_base(i, par):
                return FIRST_USES + 2 * USES_GROUP * i + USES_GROUP * par

            def for_groups(eng, group):
                with eng.Fori(0, B // 2 - 1) as pair:
                    for buf in range(2):
                        for par in range(2):
                            group(2 * pair + buf, par, buf, False)
                for buf in range(2):
                    for par in range(2):
                        group(B - 2 + buf, par, buf, buf == 1)

            def load_q(sp, b, par):
                for half in range(2):
                    for rows in range(2):
                        src = q_dram.rearrange("a b (g h d) t -> b g a d h t", g=2, d=DH)[b, par, half]
                        sp.dma_start(q_dup[rows * DH:(rows + 1) * DH, par, half, :, :], src).then_inc(s_q[par], 16)

            @block.sync
            def _(sp):
                for n in range(2):
                    sp.sem_inc(s_o[n], 32)
                load_q(sp, 0, 0)
                load_q(sp, 0, 1)
                sp.dma_start(ctx32[:], ctx_v[1]).then_inc(s_ctx, 16)

                def group(i, par, buf, final):
                    if par == 1 and not isinstance(i, int):
                        sp.wait_ge(s_ctx_cut, i + 2)
                        sp.dma_start(ctx32[:], ctx_v[i + 2]).then_inc(s_ctx, 16)
                    if not final:
                        sp.wait_ge(s_scores, 2 * (2 * GH * i + GH * par + GH))
                        load_q(sp, i + 1, par)
                    sp.wait_ge(s_ocut, PAIRS * (2 * i + par + 1) + 2)
                    for half in range(2):
                        dst = o_dram.rearrange("a b (g c p) t -> b g a p c t", g=2, p=P)[i, par, half]
                        sp.dma_start(dst, o_t[:, par, half]).then_inc(s_o[par], 16)

                for_groups(sp, group)
                for n in range(2):
                    sp.wait_ge(s_o[n], 32 + 32 * B)

            @block.gpsimd
            def _(pool):
                def wait_counted(sem, value):
                    pool.wait_ge(sem, value)
                    pool.sem_inc(s_pool_passed, 1)

                def reduce_ctx(b):
                    wait_counted(s_amax, b)
                    nc.gpsimd.partition_all_reduce(c_all[:], c_amax[:], P, ABSMAX).then_inc(s_all, 1)

                def normalise(head, par_h):
                    wait_counted(s_inv, head + 1)
                    for t in range(2):
                        nc.gpsimd.tensor_scalar(probs[:, par_h, t, :], probs[:, par_h, t, :], row_inv[:, t:t + 1],
                                                2.0 ** P_EXP, ALU.mult, ALU.mult).then_inc(s_probs, 1)

                def cut_outputs(i, par, c, use):
                    pair = 2 * PAIRS * i + PAIRS * par + c
                    wait_counted(s_free, use)
                    if c == 0:
                        wait_counted(s_o[par], 32 * i + 32)
                    g = nc.gpsimd
                    g.tensor_scalar(o_t[:, par, 0, c, :], o_sum[:, c % 2, :], 1.0, 1.0, ALU.mult,
                                    ALU.mult).then_inc(s_ohigh, 1)
                    wait_counted(s_ohigh, pair + 1)
                    g.tensor_tensor(o_t[:, par, 1, c, :], o_sum[:, c % 2, :], o_t[:, par, 0, c, :],
                                    ALU.subtract).then_inc(s_ocut, 1)

                pool.sem_inc(s_ocut, 2)
                normalise(0, 0)

                def group(i, par, buf, final):
                    fill = not (final and par == 1)
                    for h in range(GH):
                        if fill or h < GH - 1:
                            normalise(2 * GH * i + GH * par + h + 1, (h + 1) % 2)
                        if par == 0 and h == len(CTX_MAX) - 1 and not final:
                            reduce_ctx(i + 1)
                        if h % 2 == 1:
                            of_head = [n for n, (hh, kind, _) in enumerate(steps(fill)) if hh == h and kind == "A"][0]
                            cut_outputs(i, par, h // 2, use_base(i, par) + of_head + 1)

                for_groups(pool, group)

            @block.scalar
            def _(act):
                a = nc.scalar

                def exps(head, par_h, t):
                    act.wait_ge(s_bias, 2 * head + t + 1)
                    a.activation(probs[:, par_h, t, :].rearrange("p (n k) -> p n k", n=2), ps[0:QT, 2 * t:2 * t + 2, 0:KH],
                                 ACT.Exp, bias=bias[:, t:t + 1], scale=score_scale[0:QT, 0:1],
                                 accum_out=row_sum[:, t:t + 1]).then_inc(s_exp, 1)

                def high(use, slot, kind, n, par):
                    bank = ps[:, 4 + slot % RING, :]
                    act.wait_ge(s_full, use + 1)
                    if kind == "T":
                        a.activation(probs_t[:, 0, 2 * n:2 * n + 2, :], bank[0:KT, 0:2 * NQ].rearrange("p (c q) -> p c q", c=2),
                                     ACT.Copy).then_inc(s_high, 1)
                    elif kind == "K":
                        for hh in range(2):
                            last = a.activation(keys[0:DH, par, 2 * (n // 2) + hh, (n % 2) * KH:(n % 2 + 1) * KH],
                                                bank[hh * DH:(hh + 1) * DH, 0:KH], ACT.Copy, scale=2.0 ** KV_EXP)
                        last.then_inc(s_high, 1)
                    elif kind == "V":
                        a.activation(vals[:, par, n, :, 0, :], bank[0:KT, :].rearrange("p (h d) -> p h d", d=DH),
                                     ACT.Copy, scale=2.0 ** KV_EXP).then_inc(s_high, 1)
                    else:
                        a.activation(o_low[:], bank[DH:P, 0:NQ], ACT.Copy, scale=2.0 ** -P_EXP).then_inc(s_high, 1)

                def cut_ctx(b, part, buf):
                    if part == 0:
                        act.wait_ge(s_ctx_scale, b)
                    a.activation(ctx_buf[buf][:, 0, part], ctx32[:, part], ACT.Copy,
                                 scale=c_scale[:]).then_inc(s_ctx_high, 1)

                for use in range(FIRST_USES):
                    kind, n = ("K", use) if use < N_KU else ("V", use - N_KU)
                    high(use, use, kind, n, 0)
                for t in range(2):
                    exps(0, 0, t)

                def group(i, par, buf, final):
                    fill = not (final and par == 1)
                    slot = FIRST_USES + USES_GROUP * par
                    for n, (h, kind, which) in enumerate(steps(fill)):
                        head = 2 * GH * i + GH * par + h
                        more = fill or h < GH - 1
                        if kind == "T" and which == 0 and par == 0 and h in CTX_CUT and not final:
                            cut_ctx(i + 1, CTX_CUT[h], 1 - buf)
                        high(use_base(i, par) + n, slot + n, kind, which, 1 - par)
                        if kind == "T" and which != 1 and more:
                            exps(head + 1, (h + 1) % 2, which // 2)

                for_groups(act, group)

            @block.vector
            def _(dve):
                v = nc.vector

                def maxima(head, t):
                    dve.wait_ge(s_scores, 2 * head + t + 1)
                    v.tensor_reduce(row_max[:, t:t + 1], ps[0:QT, 2 * t:2 * t + 2, 0:KH], AX.XY,
                                    ALU.max).then_inc(s_rowmax, 1)
                    dve.wait_ge(s_rowmax, 2 * head + t + 1)
                    v.tensor_scalar(bias[:, t:t + 1], row_max[:, t:t + 1], score_scale[0:QT, 1:2], None,
                                    ALU.mult).then_inc(s_bias, 1)

                def inverses(head):
                    dve.wait_ge(s_exp, 2 * head + 2)
                    v.reciprocal(row_inv[:], row_sum[:]).then_inc(s_inv, 1)

                def low(use, slot, kind, n, par, h, opar):
                    bank = ps[:, 4 + slot % RING, :]
                    dve.wait_ge(s_high, use + 1)
                    if kind == "T":
                        v.tensor_tensor(probs_t[:, 1, 2 * n:2 * n + 2, :],
                                        bank[0:KT, 0:2 * NQ].rearrange("p (c q) -> p c q", c=2),
                                        probs_t[:, 0, 2 * n:2 * n + 2, :], ALU.subtract).then_inc(s_free, 1)
                    elif kind == "K":
                        for hh in range(2):
                            cols = slice((n % 2) * KH, (n % 2 + 1) * KH)
                            head = 2 * (n // 2) + hh
                            last = v.scalar_tensor_tensor(
                                out=keys[DH:P, par, head, cols], in0=bank[hh * DH:(hh + 1) * DH, 0:KH],
                                scalar=2.0 ** KV_EXP, in1=keys[0:DH, par, head, cols], op0=ALU.mult, op1=ALU.subtract)
                        last.then_inc(s_free, 1)
                    elif kind == "V":
                        v.scalar_tensor_tensor(out=vals[:, par, n, :, 1, :],
                                               in0=bank[0:KT, :].rearrange("p (h d) -> p h d", d=DH),
                                               scalar=2.0 ** KV_EXP, in1=vals[:, par, n, :, 0, :],
                                               op0=ALU.mult, op1=ALU.subtract).then_inc(s_free, 1)
                    else:
                        rows = slice((h % 2) * DH, (h % 2 + 1) * DH)
                        v.scalar_tensor_tensor(out=o_sum[rows, (h // 2) % 2, :], in0=bank[0:DH, 0:NQ],
                                               scalar=2.0 ** -P_EXP, in1=o_low[:],
                                               op0=ALU.mult, op1=ALU.add).then_inc(s_free, 1)

                def scale_ctx(b):
                    own = Own(dve, s_own, POW2_STEPS * (b - 1))
                    dve.wait_ge(s_all, b)
                    pow2_scale(v, own, c_all[:], c_field[:], c_scale[:], c_inv[:])

                def cut_ctx(b, part, buf):
                    dve.wait_ge(s_ctx_high, CCH * (b - 1) + part + 1)
                    cut = v.scalar_tensor_tensor(out=ctx_buf[buf][:, 1, part], in0=ctx32[:, part], scalar=c_scale[:],
                                                 in1=ctx_buf[buf][:, 0, part], op0=ALU.mult, op1=ALU.subtract)
                    if part == CCH - 1:
                        cut.then_inc(s_ctx_cut, 1)

                def amax_ctx(b, part):
                    if part == 0:
                        dve.wait_ge(s_ctx, 16 * b)
                    peak = v.tensor_reduce(c_peaks[:, part:part + 1], ctx32[:, part], AX.X, ALU.max,
                                           apply_absolute_value=True)
                    if part == CCH - 1:
                        peak.then_inc(s_peaks, 1)
                        dve.wait_ge(s_peaks, b)
                        v.tensor_reduce(c_amax[:], c_peaks[:], AX.X, ALU.max).then_inc(s_amax, 1)

                def set_score_scale():
                    v.tensor_scalar(score_scale[:, 0:1], c_inv[:], score_w[:], None, ALU.mult)
                    v.tensor_scalar(score_scale[:, 1:2], c_inv[:], score_w[:], -1.0, ALU.mult, ALU.mult).then_inc(s_set, 1)

                def set_attn_scale(b):
                    v.tensor_scalar(attn_scale[:, bass.ds(b, 1)], c_inv[:], attn_w[:], None, ALU.mult)

                v.memset(bias[:], 0.0).then_inc(s_ctx_cut, 1)
                set_score_scale()
                set_attn_scale(0)
                for use in range(FIRST_USES):
                    kind, n = ("K", use) if use < N_KU else ("V", use - N_KU)
                    low(use, use, kind, n, 0, 0, 0)
                dve.wait_ge(s_set, 1)
                for t in range(2):
                    maxima(0, t)
                inverses(0)

                def group(i, par, buf, final):
                    fill = not (final and par == 1)
                    slot = FIRST_USES + USES_GROUP * par
                    for n, (h, kind, which) in enumerate(steps(fill)):
                        head = 2 * GH * i + GH * par + h
                        more = fill or h < GH - 1
                        if kind == "T" and which == 0 and more:
                            if par == 1 and h == GH - 1:
                                set_score_scale()
                                dve.wait_ge(s_set, i + 2)
                            for t in range(2):
                                maxima(head + 1, t)
                        if kind == "A":
                            if h % 2 == 0:
                                dve.wait_ge(s_ocut, 2 * PAIRS * i + PAIRS * par + h // 2 + 1)
                        low(use_base(i, par) + n, slot + n, kind, which, 1 - par, h, par)
                        if kind == "T" and which == 2 and more:
                            inverses(head + 1)
                        if kind == "T" and which == 2 and par == 0 and not final:
                            if h in CTX_MAX:
                                amax_ctx(i + 1, CTX_MAX[h])
                            elif h == SCALE_STEP:
                                scale_ctx(i + 1)
                                set_attn_scale(i + 1)
                                v.memset(c_amax[:], 0.0).then_inc(s_ctx_scale, 1)
                            elif h in CTX_CUT:
                                cut_ctx(i + 1, CTX_CUT[h], 1 - buf)

                for_groups(dve, group)

            @block.tensor
            def _(pe):
                mm = nc.tensor.matmul

                def scores(head, par, h, t, first):
                    if not first:
                        pe.wait_ge(s_exp, 2 * head + t - 1)
                    for half in range(2):
                        for n in range(2):
                            last = mm(ps[0:QT, 2 * t + n, 0:KH], q_dup[:, par, half, h, t * QT:(t + 1) * QT],
                                      keys[:, par, h, n * KH:(n + 1) * KH], start=(half == 0), stop=(half == 1))
                    last.then_inc(s_scores, 1)

                def project_keys(slot, n, par, buf):
                    bank = ps[:, 4 + slot % RING, 0:KH]
                    col = (par * GH + 2 * (n // 2)) * DH
                    k = 0
                    for wh, xh in ((0, 0), (0, 1), (1, 0)):
                        for d in range(CCH):
                            last = mm(bank, wk_s[:, wh, d, col:col + P],
                                      ctx_buf[buf][:, xh, d, (n % 2) * KH:(n % 2 + 1) * KH],
                                      start=(k == 0), stop=(k == 3 * CCH - 1))
                            k += 1
                    last.then_inc(s_full, 1)

                def project_values(slot, n, par, buf):
                    bank = ps[0:KT, 4 + slot % RING, :]
                    k = 0
                    for wh, xh in ((0, 0), (1, 0), (0, 1)):
                        for d in range(CCH):
                            last = mm(bank, ctx_buf[buf][:, xh, d, n * KT:(n + 1) * KT],
                                      wv_s[:, wh, d, par * GH * DH:(par + 1) * GH * DH],
                                      start=(k == 0), stop=(k == 3 * CCH - 1))
                            k += 1
                    last.then_inc(s_full, 1)

                for use in range(FIRST_USES):
                    if use >= RING:
                        pe.wait_ge(s_free, use - RING + 1)
                    if use < N_KU:
                        project_keys(use, use, 0, 0)
                    else:
                        project_values(use, use - N_KU, 0, 0)
                pe.wait_ge(s_q[0], 64)
                pe.wait_ge(s_free, 2)
                for t in range(2):
                    scores(0, 0, 0, t, True)

                def group(i, par, buf, final):
                    fill = not (final and par == 1)
                    slot = FIRST_USES + USES_GROUP * par
                    base = use_base(i, par)
                    k_use = {}
                    for n, (h, kind, which) in enumerate(steps(fill)):
                        head = 2 * GH * i + GH * par + h
                        use = base + n
                        if kind == "T" and which == 0:
                            if h < GH - 1:
                                for t in range(2):
                                    scores(head + 1, par, h + 1, t, False)
                            elif fill:
                                pe.wait_ge(s_free, base + k_use[1] + 1)
                                pe.wait_ge(s_q[1 - par], 64 * (i + 1 + par))
                                for t in range(2):
                                    scores(head + 1, 1 - par, 0, t, False)
                            pe.wait_ge(s_probs, 2 * head + 2)
                        if h == 0 and kind == "K" and par == 1:
                            pe.wait_ge(s_ctx_cut, i + 2)
                        pe.wait_ge(s_free, use - RING + 1)
                        if kind == "K":
                            k_use[which] = n
                            project_keys(slot + n, which, 1 - par, (buf + par) % 2)
                        elif kind == "V":
                            project_values(slot + n, which, 1 - par, (buf + par) % 2)
                        elif kind == "T":
                            bank = ps[:, 4 + (slot + n) % RING, :]
                            for k in range(2):
                                for t in range(2):
                                    last_mm = nc.tensor.transpose(
                                        bank[0:KT, k * NQ + t * QT:k * NQ + (t + 1) * QT],
                                        probs[:, h % 2, t, (2 * which + k) * KT:(2 * which + k + 1) * KT],
                                        ident[0:QT, 0:QT])
                            last_mm.then_inc(s_full, 1)
                            t_use = n
                        else:
                            pe.wait_ge(s_free, base + t_use + 1)
                            k = 0
                            for kt in range(NKT):
                                for half in range(2):
                                    last_mm = mm(ps[:, 4 + (slot + n) % RING, 0:NQ],
                                                 vals[:, par, kt, h, :, :].rearrange("p a d -> p (a d)"),
                                                 probs_t[:, half, kt, :], start=(k == 0), stop=(k == 2 * NKT - 1))
                                    k += 1
                            last_mm.then_inc(s_full, 1)

                for_groups(pe, group)
        kv_ctx.close()
        st_ctx.close()

        with ExitStack() as c:
            o_s = sb("o_s", [P, 2, ICH, TT], F16, c)
            xr = sb("xr", [SUB, ST, D], F32, c)
            x1 = sb("x1", [SUB, ST, D], F32, c)
            res = sb("res", [SUB, ST, D], F32, c)
            xn = sb("xn2", [SUB, ST, D], F32, c)
            xT = sb("xT2", [P, 2, DCH, TT], F16, c)
            r = sb("r", [P, HCH, TT], F32, c)
            r_s = r[:].bitcast(F16).rearrange("p j (a t) -> p j a t", a=2)
            SQN = 4
            sq = sb("sq", [P, SQN, TT], F32, c)
            z32 = sb("z32", [P, TT], F32, c)
            z_part = [sb(f"z_part{n}", [P, TT], BF16, c) for n in range(2)]
            z_rest = [sb(f"z_rest{n}", [P, TT], F32, c) for n in range(2)]
            z_acc = sb("z_acc", [P, TT], F32, c)
            z = sb("z", [P, TT], BF16, c)
            y_out = sb("y_out", [SUB, ST, D], F32, c)
            stats = sb("f_stats", [SUB, ST, 6], F32, c)
            mean_var = sb("f_mean_var", [SUB, ST, 2], F32, c)
            work = sb("f_work", [SUB, 2, ST], F32, c)
            y_bits = sb("f_y", [SUB, ST], I32, c)
            r_amax = sb("r_amax", [P, HCH], F32, c)
            r_amax1 = sb("r_amax1", [P, 1], F32, c)
            r_all = sb("r_all", [P, 1], F32, c)
            fld = sb("fld", [P, 1], I32, c)
            g_scale = sb("g_scale", [P, 1], F32, c)
            g_inv = sb("g_inv", [P, 1], F32, c)

            s_o, s_x, s_y = sem("o_in", c), sem("xr_in", c), sem("y_stored", c)
            s_xb, s_res, s_normed = sem("x_plus_bias", c), sem("res_kept", c), sem("x1_normed", c)
            s_own_t, s_own_z, s_own_r = sem("dve_own_norm", c), sem("dve_own_z", c), sem("dve_own_r", c)
            s_full, s_free, s_thigh = sem("a_full", c), sem("a_free", c), sem("t_high", c)
            s_zfull, s_z32, s_zready = sem("z_full", c), sem("z32_ready", c), sem("z_ready", c)
            s_fc, s_relu = sem("fc_full", c), sem("relu_done", c)
            s_ramax, s_rall, s_rscale = sem("r_amax_s", c), sem("r_all_s", c), sem("r_scale_s", c)
            s_sq, s_rhigh, s_rlow = sem("squared", c), sem("r_high", c), sem("r_low", c)
            s_norm_passed = sem("norm_passed", c)
            s_yout, s_pool_passed = sem("y_ready", c), sem("pool_passed3", c)
            RING_A, RING_B, USES_A, Z_STEPS = 3, 4, 3 * ST, 6
            block = c.enter_context(nc.Block())

            def use_o(i, n):
                return (n, n) if isinstance(i, int) and i == 0 else (2 * ST + n, 2 * ST + USES_A * (i - 1) + n)

            def use_t(i, n):
                return (ST + n, ST + n) if isinstance(i, int) and i == 0 else (4 * ST + n, 4 * ST + USES_A * (i - 1) + n)

            def use_y(i, n, last):
                first = 2 * ST if last else 3 * ST
                return (first + n, first + USES_A * i + n)

            def for_tiles(eng, tile):
                with eng.Fori(0, NTILES - 1) as i:
                    tile(i, False)
                tile(NTILES - 1, True)

            @block.sync
            def _(sp):
                def loads(i):
                    for half in range(2):
                        for b in range(2):
                            src = o_dram.rearrange("a (i b) (c p) t -> i b a p c t", b=2, p=P)[i, b, half]
                            sp.dma_start(o_s[:, half, :, b * NQ:(b + 1) * NQ], src).then_inc(s_o, 16)
                    sp.dma_start(xr[:], x_tiles[i]).then_inc(s_x, 16)

                loads(0)
                sp.sem_inc(s_y, 16)

                def tile(i, last):
                    if not last:
                        sp.wait_ge(s_normed, i + 1)
                        loads(i + 1)
                    sp.wait_ge(s_yout, i + 2)
                    sp.dma_start(out_tiles[i], y_out[:]).then_inc(s_y, 16)

                for_tiles(sp, tile)
                sp.wait_ge(s_y, 16 + 16 * NTILES)

            @block.gpsimd
            def _(pool):
                g = nc.gpsimd

                def wait_counted(sem, value):
                    pool.wait_ge(sem, value)
                    pool.sem_inc(s_pool_passed, 1)

                def add_bias(i):
                    wait_counted(s_x, 16 * (i + 1))
                    for s in range(ST):
                        last = g.tensor_tensor(xr[:, s, :], xr[:, s, :], bo_bc[0:SUB, :], ALU.add)
                    last.then_inc(s_xb, 1)

                add_bias(0)
                pool.sem_inc(s_rlow, SQN)

                def tile(i, last):
                    wait_counted(s_normed, i + 1)
                    wait_counted(s_yout, i + 1)
                    g.tensor_scalar(res[:], x1[:], 1.0, 1.0, ALU.mult, ALU.mult).then_inc(s_res, 1)
                    wait_counted(s_ramax, i + 1)
                    g.partition_all_reduce(r_all[:], r_amax1[:], P, ABSMAX).then_inc(s_rall, 1)
                    if not last:
                        add_bias(i + 1)
                    for j in range(HCH):
                        wait_counted(s_rhigh, HCH * i + j + 1)
                        g.tensor_tensor(r_s[:, j, 1, :], sq[:, j % SQN, :], r_s[:, j, 0, :],
                                        ALU.subtract).then_inc(s_rlow, 1)

                for_tiles(pool, tile)

            @block.scalar
            def _(act):
                a = nc.scalar

                def transposed(i):
                    for d in range(DCH):
                        turn, use = use_t(i, d)
                        act.wait_ge(s_full, use + 1)
                        a.activation(xT[:, 0, d, :], ps[:, turn % RING_A, 0:TT], ACT.Copy,
                                     scale=2.0 ** X_EXP).then_inc(s_thigh, 1)
                    act.wait_ge(s_zfull, i + 1)
                    a.activation(z32[:], ps[:, 7, 0:TT], ACT.Copy, scale=z_scale[:]).then_inc(s_z32, 1)

                transposed(0)
                act.sem_inc(s_relu, RING_B)

                def tile(i, last):
                    for j in range(HCH):
                        act.wait_ge(s_fc, HCH * i + j + 1)
                        a.activation(r[:, j, :], ps[:, 3 + j % RING_B, 0:TT], ACT.Relu,
                                     scale=relu_scale[:, j:j + 1]).then_inc(s_relu, 1)
                    act.wait_ge(s_rscale, i + 1)
                    for j in range(HCH):
                        act.wait_ge(s_rlow, HCH * i + j + 1)
                        a.activation(sq[:, j % SQN, :], r[:, j, :], ACT.Square, scale=g_scale[:]).then_inc(s_sq, 1)
                    if not last:
                        transposed(i + 1)

                for_tiles(act, tile)

            @block.vector
            def _(dve):
                v = nc.vector

                def residual(i):
                    dve.wait_ge(s_xb, i + 1)
                    if not (isinstance(i, int) and i == 0):
                        dve.wait_ge(s_res, i)
                    for s in range(ST):
                        turn, use = use_o(i, s)
                        dve.wait_ge(s_full, use + 1)
                        v.scalar_tensor_tensor(out=x1[:, s, :], in0=ps[0:SUB, turn % RING_A, :],
                                               scalar=attn_scale[0:SUB, bass.ds(2 * i + s // 2, 1)],
                                               in1=xr[:, s, :], op0=ALU.mult, op1=ALU.add).then_inc(s_free, 1)
                    dve.wait_ge(s_free, use_o(i, ST - 1)[1] + 1)
                    own = Own(dve, s_own_t, NORM_STEPS * i)
                    layer_norm(v, own, x1, stats, mean_var, work, y_bits[:], xn,
                               s_norm_passed).then_inc(s_normed, 1)

                def transposed(i):
                    for d in range(DCH):
                        turn, use = use_t(i, d)
                        dve.wait_ge(s_thigh, DCH * i + d + 1)
                        v.scalar_tensor_tensor(out=xT[:, 1, d, :], in0=ps[:, turn % RING_A, 0:TT], scalar=2.0 ** X_EXP,
                                               in1=xT[:, 0, d, :], op0=ALU.mult, op1=ALU.subtract).then_inc(s_free, 1)
                    own = Own(dve, s_own_z, Z_STEPS * i)
                    dve.wait_ge(s_z32, i + 1)
                    own(v.tensor_copy(z_part[0][:], z32[:]))
                    own(v.tensor_tensor(z_rest[0][:], z32[:], z_part[0][:], ALU.subtract))
                    own(v.tensor_copy(z_part[1][:], z_rest[0][:]))
                    own(v.tensor_tensor(z_rest[1][:], z_rest[0][:], z_part[1][:], ALU.subtract))
                    own(v.tensor_scalar(z_acc[:], z_part[0][:], masks[:, 0:1], None, ALU.mult))
                    own(v.scalar_tensor_tensor(out=z_acc[:], in0=z_part[1][:], scalar=masks[:, 1:2], in1=z_acc[:],
                                               op0=ALU.mult, op1=ALU.add))
                    v.scalar_tensor_tensor(out=z[:], in0=z_rest[1][:], scalar=masks[:, 2:3], in1=z_acc[:],
                                           op0=ALU.mult, op1=ALU.add).then_inc(s_zready, 1)

                residual(0)
                transposed(0)
                v.memset(r_amax1[:], 0.0).then_inc(s_yout, 1)

                def tile(i, last):
                    for j in range(HCH):
                        dve.wait_ge(s_relu, HCH * i + j + 1 + RING_B)
                        peak = v.tensor_reduce(r_amax[:, j:j + 1], r[:, j, :], AX.X, ALU.max)
                    own = Own(dve, s_own_r, (1 + POW2_STEPS) * i)
                    own(peak)
                    v.tensor_reduce(r_amax1[:], r_amax[:], AX.X, ALU.max).then_inc(s_ramax, 1)
                    dve.wait_ge(s_rall, i + 1)
                    pow2_scale(v, own, r_all[:], fld[:], g_scale[:], g_inv[:], 260)
                    v.tensor_tensor(g_inv[:], g_inv[:], g_inv[:], ALU.mult).then_inc(s_rscale, 1)
                    for j in range(HCH):
                        dve.wait_ge(s_sq, HCH * i + j + 1)
                        v.tensor_copy(r_s[:, j, 0, :], sq[:, j % SQN, :]).then_inc(s_rhigh, 1)
                    if not last:
                        residual(i + 1)
                    dve.wait_ge(s_res, i + 1)
                    dve.wait_ge(s_y, 16 * i + 16)
                    for s in range(ST):
                        turn, use = use_y(i, s, last)
                        dve.wait_ge(s_full, use + 1)
                        v.scalar_tensor_tensor(out=y_out[:, s, :], in0=ps[0:SUB, turn % RING_A, :], scalar=g_inv[0:SUB, :],
                                               in1=proj_bc[0:SUB, :], op0=ALU.mult, op1=ALU.mult).then_inc(s_free, 1)
                        dve.wait_ge(s_free, use + 1)
                        total = v.tensor_tensor(y_out[:, s, :], y_out[:, s, :], res[:, s, :], ALU.add)
                    total.then_inc(s_yout, 1)
                    if not last:
                        transposed(i + 1)

                for_tiles(dve, tile)

            @block.tensor
            def _(pe):
                mm = nc.tensor.matmul

                def bank_a(turn_use):
                    turn, use = turn_use
                    if turn >= RING_A:
                        pe.wait_ge(s_free, use - RING_A + 1)
                    return ps[:, turn % RING_A, :]

                def project(i):
                    pe.wait_ge(s_o, 64 * (i + 1))
                    for s in range(ST):
                        bank = bank_a(use_o(i, s))
                        k = 0
                        for oh, wh in ((0, 0), (0, 1), (1, 0)):
                            for d in range(ICH):
                                last = mm(bank[0:SUB, :], o_s[:, oh, d, s * SUB:(s + 1) * SUB], wo_s[:, wh, d, :],
                                          start=(k == 0), stop=(k == 3 * ICH - 1))
                                k += 1
                        last.then_inc(s_full, 1)

                def transposes(i):
                    pe.wait_ge(s_normed, i + 1)
                    for d in range(DCH):
                        bank = bank_a(use_t(i, d))
                        for s in range(ST):
                            last = nc.tensor.transpose(bank[:, s * SUB:(s + 1) * SUB], xn[:, s, d * P:(d + 1) * P],
                                                       ident[0:SUB, 0:SUB])
                        last.then_inc(s_full, 1)
                    pe.wait_ge(s_free, use_t(i, DCH - 1)[1] + 1)
                    if not (isinstance(i, int) and i == 0):
                        pe.wait_ge(s_z32, i)
                    k = 0
                    for wh, xh in ((0, 0), (0, 1), (1, 0)):
                        for d in range(DCH):
                            last = mm(ps[:, 7, 0:TT], fb_s[:, wh, d, :], xT[:, xh, d, :], start=(k == 0),
                                      stop=(k == 3 * DCH - 1))
                            k += 1
                    last.then_inc(s_zfull, 1)

                def hidden(i):
                    for j in range(HCH):
                        pe.wait_ge(s_relu, HCH * i + j + 1)
                        bank = ps[:, 3 + j % RING_B, 0:TT]
                        for k in range(2 * DCH):
                            mm(bank, fc_t[:, k % DCH, j * P:(j + 1) * P], xT[:, k // DCH, k % DCH, :],
                               start=(k == 0), stop=False)
                        if j == 0:
                            pe.wait_ge(s_zready, i + 1)
                        mm(bank, u_t[:, j * P:(j + 1) * P], z[:], start=False, stop=True).then_inc(s_fc, 1)

                def result(i, last_tile):
                    for s in range(ST):
                        bank = bank_a(use_y(i, s, last_tile))
                        for j in range(HCH):
                            if s == 0:
                                pe.wait_ge(s_rlow, HCH * i + j + 1 + SQN)
                            for half in range(2):
                                last = mm(bank[0:SUB, :], r_s[:, j, half, s * SUB:(s + 1) * SUB], proj_t[:, j, :],
                                          start=(j == 0 and half == 0), stop=(j == HCH - 1 and half == 1))
                        last.then_inc(s_full, 1)

                project(0)
                transposes(0)

                def tile(i, last):
                    hidden(i)
                    if not last:
                        project(i + 1)
                    result(i, last)
                    if not last:
                        transposes(i + 1)

                for_tiles(pe, tile)


def kernel(x, ctx_768, g_xattn, g_ffn, L0_xattn_Wq, L0_xattn_Wk, L0_xattn_Wv, L0_xattn_Wo, L0_xattn_bo,
           L0_ffn_fast_b, L0_ffn_w_fc, L0_ffn_w_proj, L0_ffn_u, L0_ffn_v, L0_ffn_gate):
    import concourse.bacc as bacc
    from concourse.bass_utils import run_bass_kernel_spmd

    laid = {
        "x": np.ascontiguousarray(np.asarray(x).reshape(T, D)),
        "ctx_t": np.ascontiguousarray(np.asarray(ctx_768).transpose(0, 2, 1)),
        "g_xattn": np.asarray(g_xattn).reshape(1, 1),
        "g_ffn": np.asarray(g_ffn).reshape(1, 1),
        "wq": np.ascontiguousarray(L0_xattn_Wq),
        "wk": np.ascontiguousarray(L0_xattn_Wk),
        "wv": np.ascontiguousarray(L0_xattn_Wv),
        "wo": np.ascontiguousarray(L0_xattn_Wo),
        "bo": np.asarray(L0_xattn_bo).reshape(1, D),
        "fast_b_t": np.ascontiguousarray(np.asarray(L0_ffn_fast_b).T),
        "w_fc": np.ascontiguousarray(L0_ffn_w_fc),
        "w_proj": np.ascontiguousarray(L0_ffn_w_proj),
        "u": np.ascontiguousarray(L0_ffn_u),
        "v_low": np.ascontiguousarray(L0_ffn_v),
        "gate": np.asarray(L0_ffn_gate).reshape(1, 1),
    }
    nc = bacc.Bacc("TRN2", target_bir_lowering=False, num_devices=1)
    args = {n: nc.dram_tensor(f"in_{n}", a.shape, mybir.dt.from_np(a.dtype), kind="ExternalInput").ap()
            for n, a in laid.items()}
    out = nc.dram_tensor("out", (T, D), F32, kind="ExternalOutput").ap()
    flamingo_block(nc, out=out, **args)
    ran = run_bass_kernel_spmd(nc, [{f"in_{n}": a for n, a in laid.items()}], core_ids=[0])
    return ran.results[0]["out"].reshape(B, NQ, D)
```

```python
from contextlib import ExitStack

import numpy as np

import concourse.bass as bass
from concourse import mybir

F32 = mybir.dt.float32
F16 = mybir.dt.float16
BF16 = mybir.dt.bfloat16
I32 = mybir.dt.int32
ALU = mybir.AluOpType
ACT = mybir.ActivationFunctionType
AX = mybir.AxisListType
ABSMAX = bass.bass_isa.ReduceOp.absmax


P = 128
B, NQ, D = 8, 224, 512
NK, DC = 750, 384
H, DH, HID, R = 16, 64, 2048, 16
INNER = H * DH
T = B * NQ
QT = NQ // 2
KT, NKT = 125, NK // 125
KH = NK // 2
GH = H // 2
DCH, CCH, ICH, HCH = D // P, DC // P, INNER // P, HID // P
TT, ST = 2 * NQ, 4
SUB = TT // ST
NTILES = T // TT
COPIES = P // R
EPS = 1e-5
Z_PART = [0, 0, 0, 1, 1, 1, 2, 2]
U_PART = [0, 1, 2, 0, 1, 2, 0, 1]

X_EXP = 11
Q_EXP, KV_EXP, P_EXP = -20, -24, 14
INV_SQRT_MAGIC = 0x5F3759DF

C_WQ, C_WK, C_WV, C_WO, C_FB = range(5)


def pow2_scale(v, own, amax, field, scale, inverse, exponent_sum=268):
    own(v.tensor_scalar(field, amax.bitcast(I32), 23, None, ALU.logical_shift_right))
    own(v.tensor_scalar(field, field, -1.0, float(exponent_sum), ALU.mult, ALU.add))
    own(v.tensor_scalar(field, field, 253.0, 1.0, ALU.min, ALU.max))
    own(v.tensor_scalar(scale.bitcast(I32), field, 23, None, ALU.logical_shift_left))
    own(v.tensor_scalar(field, field, -1.0, 254.0, ALU.mult, ALU.add))
    own(v.tensor_scalar(inverse.bitcast(I32), field, 23, None, ALU.logical_shift_left))


POW2_STEPS = 6


class Own:

    def __init__(self, eng, sem, start=0):
        self.eng, self.sem, self.start, self.n = eng, sem, start, 0

    def __call__(self, instruction):
        self.n += 1
        instruction.then_inc(self.sem, 1)
        self.eng.wait_ge(self.sem, self.start + self.n)


def row_factors(v, own, last, stats, mean_var, work, y_bits, passed=None):
    if last is not None:
        own(last)
    if passed is not None:
        own.eng.sem_inc(passed, 1)
    for s in range(ST):
        last = v.bn_aggr(mean_var[:, s, :], stats[:, s, :])
    own(last)
    var, sq = work[:, 0, :], work[:, 1, :]
    y = y_bits.bitcast(F32)
    v.tensor_scalar(work[:, 2, :], mean_var[:, :, 0], -1.0, None, ALU.mult)
    own(v.tensor_scalar(var, mean_var[:, :, 1], EPS, None, ALU.add))
    own(v.tensor_scalar(y_bits, var.bitcast(I32), 1, None, ALU.logical_shift_right))
    own(v.tensor_scalar(y_bits, y_bits, -1.0, float(INV_SQRT_MAGIC), ALU.mult, ALU.add))
    for step in range(3):
        own(v.tensor_tensor(sq, y, y, ALU.mult))
        own(v.tensor_tensor(sq, sq, var, ALU.mult))
        own(v.tensor_scalar(sq, sq, -0.5, 1.5, ALU.mult, ALU.add))
        last = v.tensor_tensor(y, y, sq, ALU.mult)
        if step < 2:
            own(last)
    return last


NORM_STEPS = 5 + 11


def normalise_rows(eng, x, work, y_bits, out, subtiles):
    for s in subtiles:
        last = eng.tensor_scalar(out[:, s, :], x[:, s, :], work[:, 2, s:s + 1], y_bits.bitcast(F32)[:, s:s + 1],
                                 ALU.add, ALU.mult)
    return last


def flamingo_block(nc, x, ctx_t, g_xattn, g_ffn, wq, wk, wv, wo, bo, fast_b_t, w_fc, w_proj, u, v_low, gate, out):
    x_tiles = x.rearrange("(i s p) d -> i p s d", s=ST, p=SUB)
    out_tiles = out.rearrange("(i s p) d -> i p s d", s=ST, p=SUB)
    ctx_v = ctx_t.rearrange("b (c p) k -> b p c k", p=P)
    q_dram = nc.dram_tensor("q_halves", (NTILES, ICH, P, 2, TT), F16, kind="Internal").ap()
    o_dram = nc.dram_tensor("o_halves", (NTILES, ICH, P, 2, TT), F16, kind="Internal").ap()

    with ExitStack() as keep:
        def sb(name, shape, dt, ctx=keep):
            return ctx.enter_context(nc.sbuf_tensor(name, shape, dt))

        def sem(name, ctx=keep):
            return ctx.enter_context(nc.semaphore(name))

        ps = keep.enter_context(nc.psum_tensor("ps", [P, 8, 512], F32))

        ident = sb("ident", [P, P], F32)
        ident16 = sb("ident16", [P, P], F16)
        ident_b = sb("ident_b", [P, P], BF16)
        ones = sb("ones", [P, P], F32)
        masks = sb("masks", [P, 3], F32)
        scal = sb("scal", [P, 3], F32)
        tanh_g = sb("tanh_g", [P, 2], F32)
        bo_bc = sb("bo_bc", [P, D], F32)
        proj_bc = sb("proj_bc", [P, D], F32)
        fc_scale = sb("fc_scale", [P, HCH], F32)
        relu_scale = sb("relu_scale", [P, HCH], F32)
        fc_t = sb("fc_t", [P, DCH, HID], F16)
        proj_t = sb("proj_t", [P, HCH, D], F16)
        u_t = sb("u_t", [P, HID], BF16)
        w_scale = sb("w_scale", [P, 5], F32)
        w_inv = sb("w_inv", [P, 5], F32)
        wo_s = sb("wo_s", [P, 2, ICH, D], F16)
        fb_s = sb("fb_s", [P, 2, DCH, P], F16)
        score_w = sb("score_w", [P, 1], F32)
        z_scale = sb("z_scale", [P, 1], F32)
        attn_w = sb("attn_w", [P, 1], F32)
        attn_scale = sb("attn_scale", [P, B], F32)

        st_ctx = keep.enter_context(ExitStack())
        stage_b = sb("stage_b", [P, ICH * D], F32, st_ctx)
        ctx32 = stage_b[:, 0:CCH * NK].rearrange("p (c k) -> p c k", c=CCH)
        ctx_s = sb("ctx_s", [P, 2, CCH, NK], F16, st_ctx)
        c_amax = sb("c_amax", [P, 1], F32, st_ctx)
        c_all = sb("c_all", [P, 1], F32, st_ctx)
        c_field = sb("c_field", [P, 1], I32, st_ctx)
        c_scale = sb("c_scale", [P, 1], F32, st_ctx)
        c_inv = sb("c_inv", [P, 1], F32, st_ctx)
        kv_w = sb("kv_w", [P, 2, 2, CCH, INNER], F16)
        wk_s, wv_s = kv_w[:, 0], kv_w[:, 1]

        with ExitStack() as c:
            wq_s = sb("wq_s", [P, 2, DCH, INNER], F16, c)
            stage_a = sb("stage_a", [P, DCH * INNER], F32, c)
            rows32 = sb("rows32", [P, 2, HID], F32, c)
            sign_bufs = sb("signs", [P, 2, HID], F16, c)
            tern = sb("tern", [P, HID], F16, c)
            mag = sb("mag", [P, HCH + DCH], F32, c)
            thr = sb("thr", [P, HCH + DCH], F32, c)
            pj_scale = sb("pj_scale", [P, DCH], F32, c)
            rden = sb("rden", [P, HCH], F32, c)
            u32 = sb("u32", [P, HCH, R], F32, c)
            u_f = sb("u_f", [P, HCH, R], F32, c)
            u_parts = [sb(f"u_part{n}", [P, HCH, R], BF16, c) for n in range(3)]
            u_rep = sb("u_rep", [P, HCH, COPIES, R], BF16, c)
            fb32 = sb("fb32", [P, DCH, P], F32, c)
            diag = fb32
            v32 = tern[0:R, 0:2 * D].bitcast(F32)
            fbt = sb("fbt", [R, R], F32, c)
            fbt_rep = sb("fbt_rep", [R, COPIES, R], F32, c)
            amax = sb("amax", [P, 5], F32, c)
            q_peaks = sb("q_peaks", [P, DCH], F32, c)
            amax_all = sb("amax_all", [P, 5], F32, c)
            field = sb("field", [P, 5], I32, c)
            xt = sb("xt", [SUB, ST, D], F32, c)
            xn = sb("xn", [SUB, ST, D], F32, c)
            stats = sb("q_stats", [SUB, ST, 6], F32, c)
            mean_var = sb("q_mean_var", [SUB, ST, 2], F32, c)
            work = sb("q_work", [SUB, 3, ST], F32, c)
            y_bits = sb("q_y", [SUB, ST], I32, c)
            xT = sb("xT", [P, 2, DCH, TT], F16, c)
            QO, ROW_BUFS, WQ_CUTS = 3, 4, 4
            ROWS_AT = [0, 1, 0, 1, 2, 3, 0, 1]
            q_out = sb("q_out", [P, QO, 2, TT], F16, c)

            s_x, s_normed, s_own = sem("x_in", c), sem("x_normed", c), sem("dve_own", c)
            s_factors = sem("row_factors_ready", c)
            s_full, s_high, s_free = sem("q_full", c), sem("q_high", c), sem("q_free", c)
            s_stored = [sem(f"q_stored{n}", c) for n in range(QO)]
            s_const, s_ident = sem("const_made", c), sem("ident_copied", c)
            s_small, s_bo, s_lowrank = sem("small_in", c), sem("bo_in", c), sem("lowrank_in", c)
            s_tanh, s_rep, s_fb_full = sem("tanh_done", c), sem("fbt_copies", c), sem("fb_full", c)
            W = ["wq", "wk", "wv", "wo", "fb"]
            s_wq_in = [sem(f"wq_in{n}", c) for n in range(DCH)]
            s_win = {n: sem(f"{n}_in", c) for n in W[1:4] + ["ctx"]}
            s_amax, s_all, s_scale, s_hi, s_scaled, s_cut = (
                {n: sem(f"{n}_{what}", c) for n in W + ["ctx"]}
                for what in ("amax", "all", "scale", "high", "scaled", "cut"))
            s_rows = [sem(f"rows_in{n}", c) for n in range(ROW_BUFS)]
            s_mag, s_thr, s_sign, s_tern = (sem(n, c) for n in ("row_sum", "threshold", "signs_made", "tern_made"))
            s_tfull, s_tcopied = sem("tp_full", c), sem("tp_copied", c)
            s_urep, s_diag, s_bc = sem("u_copies", c), sem("diag_made", c), sem("proj_bc_full", c)

            w32 = {"wq": stage_a[:], "wk": stage_b[:, 0:CCH * INNER], "wv": stage_a[:, 0:CCH * INNER],
                   "wo": stage_b[:], "fb": fb32[:].rearrange("p c n -> p (c n)"), "ctx": stage_b[:, 0:CCH * NK]}
            halves = {n: (t[:, 0].rearrange("p c n -> p (c n)"), t[:, 1].rearrange("p c n -> p (c n)"))
                      for n, t in (("wq", wq_s), ("wk", wk_s), ("wv", wv_s), ("wo", wo_s), ("fb", fb_s), ("ctx", ctx_s))}
            scales = {n: (amax[:, k:k + 1], amax_all[:, k:k + 1], field[:, k:k + 1], w_scale[:, k:k + 1],
                          w_inv[:, k:k + 1]) for k, n in enumerate(W)}
            scales["ctx"] = (c_amax[:], c_all[:], c_field[:], c_scale[:], c_inv[:])

            USES, RING = DCH + ICH, 4
            GROUPS = 2 * DCH
            G_FC = HCH // 4
            beside = {
                0: ["wk.max"], 1: ["fb.copies"],
                2: ["wk.scale", "fb.make", "wk.high", "wk.cut", "norm", "g0.sum"], 4: ["fb.max", "wk.cut"],
                5: ["g0.sign", "wv.max", "const"], 6: ["g0.tern"], 7: ["wv.scale", "fb.scale"],
                8: ["g0.turn", "wv.high", "wk.cut", "norm", "g1.sum"], 9: ["fb.high"],
                10: ["wo.load", "g1.sign"], 11: ["wv.cut", "g1.tern", "g2.sum", "wv.cut"],
                12: ["g0.copy", "g2.sign", "fb.cut"], 13: ["g1.turn", "g2.tern"],
                14: ["g2.turn", "g1.copy", "g3.sum", "wo.max", "wo.scale"], 15: ["wv.cut", "g2.copy"],
                16: ["rows.load", "wo.high", "g3.sign", "wo.cut", "norm"], 18: ["g4.sum", "g3.tern"],
                19: ["wo.cut", "wo.cut", "g4.sign"], 20: ["g3.turn", "g5.sum", "wo.cut"],
                22: ["ctx.load", "g5.sign", "g4.tern"], 23: ["g4.turn", "g6.sum"],
                24: ["g3.copy", "g6.sign", "g5.tern", "u.make", "g7.sum"],
                25: ["g5.turn", "g6.tern", "g4.copy", "g5.copy"], 26: ["g7.sign", "ctx.max"],
                28: ["g6.turn", "ctx.scale"], 29: ["g7.tern", "g6.copy"], 30: ["ctx.high", "ctx.cut"],
                31: ["g7.turn", "g7.copy"],
            }
            for spot, step in ((31, "u.turn"), (31, "u.copy"), (31, "last")):
                beside.setdefault(spot, []).append(step)
            parts = [("norm", 0), ("apply", 0), ("side", "wq.max"), ("side", "wq.scale")]
            parts += [("use", n) for n in range(DCH)]
            parts += [("side", "wq.high"), ("side", "wq.cut")]
            for i in range(NTILES):
                for n in range(ICH):
                    parts.append(("use", USES * i + DCH + n))
                    for step in beside.get(ICH * i + n, []):
                        parts += [("norm", i + 1), ("apply", i + 1)] if step == "norm" else [("side", step)]
                if i + 1 < NTILES:
                    parts += [("use", USES * (i + 1) + d) for d in range(DCH)]

            def wq_block(k):
                cols = slice(k * INNER // WQ_CUTS, (k + 1) * INNER // WQ_CUTS)
                return wq_s[:, 0, :, cols], wq_s[:, 1, :, cols], stage_a[:].rearrange("p (c n) -> p c n", c=DCH)[:, :, cols]

            def rows_of(g):
                k = ROWS_AT[g]
                return rows32[:, k, :] if k < 2 else stage_a[:, (k - 2) * HID:(k - 1) * HID]

            block = c.enter_context(nc.Block())

            @block.sync
            def _(sp):
                def load_rows(n):
                    if n < G_FC:
                        src = w_fc.rearrange("(g j p) d -> g p j d", j=4, p=P)[n]
                        dst = rows_of(n).rearrange("p (j d) -> p j d", j=4)
                    else:
                        src = w_proj.rearrange("(g p) h -> g p h", p=P)[n - G_FC]
                        dst = rows_of(n)
                    sp.dma_start(dst, src).then_inc(s_rows[ROWS_AT[n]], 16)

                def load_w(name, src):
                    dst = w32[name].rearrange("p (c n) -> p c n", c=src.shape[0] // P)
                    sp.dma_start(dst, src.rearrange("(c p) n -> p c n", p=P)).then_inc(s_win[name], 16)

                sp.dma_start(xt[:], x_tiles[0]).then_inc(s_x, 16)
                for d in range(DCH):
                    sp.dma_start(stage_a[:, d * INNER:(d + 1) * INNER], wq[d * P:(d + 1) * P, :]).then_inc(s_wq_in[d], 16)
                load_w("wk", wk)
                for what, n in parts:
                    if what == "apply" and n + 1 < NTILES:
                        sp.wait_ge(s_normed, n + 1)
                        sp.dma_start(xt[:], x_tiles[n + 1]).then_inc(s_x, 16)
                    elif n == "wq.cut":
                        sp.wait_ge(s_cut["wq"], WQ_CUTS)
                        load_w("wv", wv)
                        load_rows(0)
                        load_rows(1)
                    elif n == "wo.load":
                        sp.wait_ge(s_cut["wk"], CCH)
                        load_w("wo", wo)
                    elif n == "rows.load":
                        sp.wait_ge(s_cut["wv"], CCH)
                        load_rows(4)
                        load_rows(5)
                    elif n == "ctx.load":
                        sp.wait_ge(s_cut["wo"], DCH)
                        sp.dma_start(ctx32, ctx_v[0]).then_inc(s_win["ctx"], 16)
                    elif what == "side" and n[0] == "g" and n.endswith("turn"):
                        g = int(n[1])
                        if ROWS_AT[g] in ROWS_AT[g + 1:]:
                            sp.wait_ge(s_tern, g + 1)
                            load_rows(ROWS_AT.index(ROWS_AT[g], g + 1))

            @block.gpsimd
            def _(pool):
                g = nc.gpsimd
                g.memset(ident[:], 0.0).then_inc(s_const, 1)
                g.memset(masks[:], 1.0).then_inc(s_const, 1)
                g.memset(ones[:], 1.0).then_inc(s_const, 1)
                pool.wait_ge(s_const, 3)
                g.affine_select(out=ident[:], in_=ident[:], compare_op=ALU.not_equal, fill=1.0, base=0,
                                pattern=[[-1, P]], channel_multiplier=1).then_inc(s_const, 1)
                for n, first in ((1, R * Z_PART.index(1)), (2, R * Z_PART.index(2))):
                    g.affine_select(out=masks[:, n:n + 1], in_=masks[:, n:n + 1], compare_op=ALU.is_ge, fill=0.0,
                                    base=-first, pattern=[[0, 1]], channel_multiplier=1).then_inc(s_const, 1)
                cuts_made = {}
                for what, n in parts:
                    if what == "apply":
                        pool.wait_ge(s_factors, n + 1)
                        if n >= 1:
                            pool.wait_ge(s_full, USES * (n - 1) + DCH)
                        normalise_rows(g, xt, work, y_bits[:], xn, range(ST)).then_inc(s_normed, 1)
                    if what != "side" or "." not in n:
                        continue
                    name, does = n.split(".")
                    if does == "max":
                        pool.wait_ge(s_amax[name], 1)
                        g.partition_all_reduce(scales[name][1], scales[name][0], P, ABSMAX).then_inc(s_all[name], 1)
                    elif does == "cut" and name in ("wk", "wv", "wo"):
                        k = cuts_made[name] = cuts_made.get(name, 0) + 1
                        cols = slice((k - 1) * INNER, k * INNER)
                        pool.wait_ge(s_hi[name], 1)
                        g.tensor_scalar(w32[name][:, cols], w32[name][:, cols], scales[name][3], 1.0, ALU.mult,
                                        ALU.mult).then_inc(s_scaled[name], 1)
                        pool.wait_ge(s_scaled[name], k)
                        g.tensor_tensor(halves[name][1][:, cols], w32[name][:, cols], halves[name][0][:, cols],
                                        ALU.subtract).then_inc(s_cut[name], 1)

            @block.scalar
            def _(act):
                a = nc.scalar
                for n, g in enumerate((g_xattn, g_ffn, gate)):
                    act.dma_start(scal[:, n:n + 1], g.to_broadcast([P, 1])).then_inc(s_small, 16)
                act.dma_start(u32[:], u.rearrange("(j p) r -> p j r", p=P)).then_inc(s_small, 16)
                act.dma_start(v32, v_low).then_inc(s_lowrank, 16)
                act.dma_start(fbt[:], fast_b_t).then_inc(s_lowrank, 16)
                act.dma_start(bo_bc[:], bo.to_broadcast([P, D])).then_inc(s_bo, 16)

                def copy_turned(t):
                    act.wait_ge(s_tfull, t + 1)
                    bank = ps[:, 4 + t % RING, :]
                    if t < 2 * G_FC:
                        g, d = t // 2, 2 * (t % 2)
                        dst = fc_t[:, d:d + 2, g * 4 * P:(g + 1) * 4 * P]
                        src = bank.bitcast(F16).rearrange("p (d h) -> p d h", d=2)
                    elif t < 2 * GROUPS:
                        g, j = t // 2 - G_FC, 8 * (t % 2)
                        dst = proj_t[:, j:j + 8, g * P:(g + 1) * P]
                        src = bank.bitcast(F16).rearrange("p (j n) -> p j n", j=8)
                    else:
                        n = t - 2 * GROUPS
                        dst, src = u_t[:, n * 8 * P:(n + 1) * 8 * P], bank.bitcast(BF16)
                    a.activation(dst, src, ACT.Copy).then_inc(s_tcopied, 1)

                def store(n):
                    tile, q = n // USES, n % USES - DCH
                    k = ICH * tile + q
                    act.wait_ge(s_free, n + 1)
                    act.dma_start(q_dram[tile, q], q_out[:, k % QO]).then_inc(s_stored[k % QO], 16)

                unstored = []
                for what, n in parts:
                    if what == "use":
                        act.wait_ge(s_full, n + 1)
                        src, m = ps[:, n % RING, 0:TT], n % USES
                        if m < DCH:
                            a.activation(xT[:, 0, m, :], src, ACT.Copy, scale=2.0 ** X_EXP).then_inc(s_high, 1)
                        else:
                            k = ICH * (n // USES) + m - DCH
                            if k >= QO:
                                act.wait_ge(s_stored[k % QO], 16 * (k // QO))
                            a.activation(q_out[:, k % QO, 0, :], src, ACT.Copy, scale=2.0 ** Q_EXP).then_inc(s_high, 1)
                        if unstored:
                            store(unstored.pop())
                        if m >= DCH:
                            unstored.append(n)
                        continue
                    if n == "const":
                        act.wait_ge(s_small, 64)
                        a.activation(tanh_g[:], scal[:, 0:2], ACT.Tanh).then_inc(s_tanh, 1)
                    if what != "side" or "." not in n:
                        continue
                    name, does = n.split(".")
                    if n == "wq.high":
                        act.wait_ge(s_scale[name], 1)
                        for k in range(WQ_CUTS):
                            high, _, w = wq_block(k)
                            a.activation(high, w, ACT.Copy, scale=scales[name][3]).then_inc(s_hi[name], 1)
                    elif does == "high":
                        act.wait_ge(s_scale[name], 1)
                        a.activation(halves[name][0], w32[name], ACT.Copy, scale=scales[name][3]).then_inc(s_hi[name], 1)
                    elif does == "sum":
                        g = int(name[1])
                        act.wait_ge(s_rows[ROWS_AT[g]], 16 * ROWS_AT[:g + 1].count(ROWS_AT[g]))
                        signs = sign_bufs[:, g % 2, :]
                        if g >= 2:
                            act.wait_ge(s_tern, g - 1)
                        if g < G_FC:
                            for j in range(4):
                                cols = slice(j * D, (j + 1) * D)
                                last = a.activation(signs[:, cols], rows_of(g)[:, cols], ACT.Abs,
                                                    accum_out=mag[:, 4 * g + j:4 * g + j + 1])
                        else:
                            k = HCH + g - G_FC
                            last = a.activation(signs, rows_of(g), ACT.Abs, accum_out=mag[:, k:k + 1])
                        last.then_inc(s_mag, 1)
                    elif does == "sign":
                        g = int(name[1])
                        signs = sign_bufs[:, g % 2, :]
                        act.wait_ge(s_thr, g + 1)
                        if g < G_FC:
                            for j in range(4):
                                cols = slice(j * D, (j + 1) * D)
                                last = a.activation(signs[:, cols], rows_of(g)[:, cols], ACT.Sign,
                                                    bias=thr[:, 4 * g + j:4 * g + j + 1])
                        else:
                            k = HCH + g - G_FC
                            last = a.activation(signs, rows_of(g), ACT.Sign, bias=thr[:, k:k + 1])
                        last.then_inc(s_sign, 1)
                    elif does == "copy":
                        first = 2 * GROUPS if name == "u" else 2 * int(name[1])
                        copy_turned(first)
                        copy_turned(first + 1)
                store(unstored.pop())
                for k in range(QO):
                    act.wait_ge(s_stored[k], 16 * len(range(k, NTILES * ICH, QO)))

            @block.vector
            def _(dve):
                v = nc.vector
                own = Own(dve, s_own)

                def side_part(n):
                    if n == "const":
                        dve.wait_ge(s_tanh, 1)
                        dve.wait_ge(s_bo, 16)
                        v.tensor_scalar(bo_bc[:], bo_bc[:], tanh_g[:, 0:1], None, ALU.mult)
                        return
                    if n == "last":
                        own(v.tensor_scalar(pj_scale[:], pj_scale[:], tanh_g[:, 1:2], None, ALU.mult))
                        for j in range(DCH):
                            last = v.tensor_scalar(diag[:, j, :], ident[:], pj_scale[:, j:j + 1], None, ALU.mult)
                        last.then_inc(s_diag, 1)
                        own(v.tensor_tensor(score_w[:], w_inv[:, C_WQ:C_WQ + 1], w_inv[:, C_WK:C_WK + 1], ALU.mult))
                        v.tensor_scalar(score_w[:], score_w[:], 2.0 ** (-Q_EXP - X_EXP - KV_EXP) * DH ** -0.5, None, ALU.mult)
                        v.tensor_scalar(z_scale[:], w_inv[:, C_FB:C_FB + 1], 2.0 ** -X_EXP, None, ALU.mult)
                        own(v.tensor_tensor(attn_w[:], w_inv[:, C_WO:C_WO + 1], w_inv[:, C_WV:C_WV + 1], ALU.mult))
                        own(v.tensor_scalar(attn_w[:], attn_w[:], tanh_g[:, 0:1], 2.0 ** -KV_EXP, ALU.mult, ALU.mult))
                        v.tensor_scalar(relu_scale[:], fc_scale[:], 2.0 ** -X_EXP, None, ALU.mult)
                        dve.wait_ge(s_bc, 1)
                        v.tensor_copy(proj_bc[:], ps[:, 4, :])
                        return
                    name, does = n.split(".")
                    if n == "fb.copies":
                        dve.wait_ge(s_lowrank, 32)
                        for k in range(COPIES):
                            last = v.tensor_copy(fbt_rep[:, k, :], fbt[:])
                        last.then_inc(s_rep, 1)
                    elif n == "wq.max":
                        for d in range(DCH):
                            dve.wait_ge(s_wq_in[d], 16)
                            last = v.tensor_reduce(q_peaks[:, d:d + 1], stage_a[:, d * INNER:(d + 1) * INNER], AX.X,
                                                   ALU.max, apply_absolute_value=True)
                        own(last)
                        v.tensor_reduce(scales[name][0], q_peaks[:], AX.X, ALU.max).then_inc(s_amax[name], 1)
                    elif does == "max":
                        if name == "fb":
                            dve.wait_ge(s_fb_full, 1)
                            own(v.tensor_copy(w32["fb"], ps[:, 4, :]))
                        else:
                            dve.wait_ge(s_win[name], 16)
                        v.tensor_reduce(scales[name][0], w32[name], AX.X, ALU.max,
                                        apply_absolute_value=True).then_inc(s_amax[name], 1)
                    elif does == "scale":
                        _, all_max, f, scale, inverse = scales[name]
                        dve.wait_ge(s_all[name], 1)
                        pow2_scale(v, own, all_max, f, scale, inverse)
                        v.memset(scales[name][0], 0.0).then_inc(s_scale[name], 1)
                    elif n == "wq.cut":
                        for k in range(WQ_CUTS):
                            high, low, w = wq_block(k)
                            dve.wait_ge(s_hi[name], k + 1)
                            v.scalar_tensor_tensor(out=low, in0=w, scalar=scales[name][3], in1=high, op0=ALU.mult,
                                                   op1=ALU.subtract).then_inc(s_cut[name], 1)
                    elif does == "cut" and name in ("fb", "ctx"):
                        dve.wait_ge(s_hi[name], 1)
                        v.scalar_tensor_tensor(out=halves[name][1], in0=w32[name], scalar=scales[name][3],
                                               in1=halves[name][0], op0=ALU.mult, op1=ALU.subtract).then_inc(s_cut[name], 1)
                    elif does == "sign":
                        g = int(name[1])
                        dve.wait_ge(s_mag, g + 1)
                        if g < G_FC:
                            cols, scale, width = slice(4 * g, 4 * g + 4), fc_scale[:, 4 * g:4 * g + 4], D
                        else:
                            cols, scale, width = slice(HCH + g - G_FC, HCH + g - G_FC + 1), \
                                pj_scale[:, g - G_FC:g - G_FC + 1], HID
                        own(v.tensor_scalar(scale, mag[:, cols], 1.0 / width, 1e-5, ALU.mult, ALU.max))
                        v.tensor_scalar(thr[:, cols], scale, 0.5, None, ALU.mult).then_inc(s_thr, 1)
                    elif does == "tern":
                        g = int(name[1])
                        signs = sign_bufs[:, g % 2, :]
                        dve.wait_ge(s_sign, g + 1)
                        if g >= 1:
                            dve.wait_ge(s_tfull, 2 * g)
                        if g < G_FC:
                            for j in range(4):
                                cols = slice(j * D, (j + 1) * D)
                                last = v.scalar_tensor_tensor(
                                    out=tern[:, cols], in0=rows_of(g)[:, cols], scalar=thr[:, 4 * g + j:4 * g + j + 1],
                                    in1=signs[:, cols], op0=ALU.is_gt, op1=ALU.min)
                        else:
                            k = HCH + g - G_FC
                            last = v.scalar_tensor_tensor(out=tern[:], in0=rows_of(g), scalar=thr[:, k:k + 1],
                                                          in1=signs, op0=ALU.is_gt, op1=ALU.min)
                        last.then_inc(s_tern, 1)
                    elif n == "u.make":
                        own(v.reciprocal(rden[:], fc_scale[:]))
                        own(v.tensor_scalar(rden[:], rden[:], scal[:, 2:3], 2.0 ** X_EXP, ALU.mult, ALU.mult))
                        for j in range(HCH):
                            last = v.tensor_scalar(u_f[:, j, :], u32[:, j, :], rden[:, j:j + 1], None, ALU.mult)
                        own(last)
                        own(v.tensor_copy(u_parts[0][:], u_f[:]))
                        own(v.tensor_tensor(u_f[:], u_f[:], u_parts[0][:], ALU.subtract))
                        own(v.tensor_copy(u_parts[1][:], u_f[:]))
                        own(v.tensor_tensor(u_parts[2][:], u_f[:], u_parts[1][:], ALU.subtract))
                        for k, part in enumerate(U_PART):
                            last = v.tensor_copy(u_rep[:, :, k, :], u_parts[part][:])
                        last.then_inc(s_urep, 1)

                dve.wait_ge(s_const, 6)
                v.tensor_copy(ident16[:], ident[:]).then_inc(s_ident, 1)
                v.tensor_copy(ident_b[:], ident[:]).then_inc(s_ident, 1)
                own(v.tensor_scalar(masks[:, 0:1], masks[:, 1:2], -1.0, 1.0, ALU.mult, ALU.add))
                own(v.tensor_tensor(masks[:, 1:2], masks[:, 1:2], masks[:, 2:3], ALU.subtract))
                for what, n in parts:
                    if what == "norm":
                        dve.wait_ge(s_x, 16 * (n + 1))
                        if n >= 1:
                            dve.wait_ge(s_normed, n)
                        for s in range(ST):
                            last = v.bn_stats(stats[:, s, :], xt[:, s, :])
                        row_factors(v, own, last, stats, mean_var, work, y_bits[:]).then_inc(s_factors, 1)
                    elif what == "use":
                        dve.wait_ge(s_high, n + 1)
                        m = n % USES
                        k = ICH * (n // USES) + m - DCH
                        dst, exp = (xT[:, :, m, :], X_EXP) if m < DCH else (q_out[:, k % QO, :, :], Q_EXP)
                        v.scalar_tensor_tensor(out=dst[:, 1, :], in0=ps[:, n % RING, 0:TT], scalar=2.0 ** exp,
                                               in1=dst[:, 0, :], op0=ALU.mult, op1=ALU.subtract).then_inc(s_free, 1)
                    elif what == "side":
                        side_part(n)

            @block.tensor
            def _(pe):
                def turn(t, square):
                    if t >= RING:
                        pe.wait_ge(s_tcopied, t - RING + 1)
                    for m in range(8):
                        last = square(m, ps[:, 4 + t % RING, :])
                    last.then_inc(s_tfull, 1)

                pe.wait_ge(s_ident, 2)
                for what, n in parts:
                    if what == "use":
                        i, m = n // USES, n % USES
                        bank = ps[:, n % RING, 0:TT]
                        if n >= RING:
                            pe.wait_ge(s_free, n - RING + 1)
                        if m < DCH:
                            pe.wait_ge(s_normed, i + 1)
                            for s in range(ST):
                                last = nc.tensor.transpose(bank[:, s * SUB:(s + 1) * SUB], xn[:, s, m * P:(m + 1) * P],
                                                           ident[0:SUB, 0:SUB])
                            last.then_inc(s_full, 1)
                            continue
                        q = m - DCH
                        if q == 0:
                            pe.wait_ge(s_free, n)
                        if i == 0:
                            pe.wait_ge(s_cut["wq"], q * WQ_CUTS // ICH + 1)
                        k = 0
                        for wh, xh in ((0, 0), (0, 1), (1, 0)):
                            for d in range(DCH):
                                last = nc.tensor.matmul(bank, wq_s[:, wh, d, q * P:(q + 1) * P], xT[:, xh, d, :],
                                                        start=(k == 0), stop=(k == 3 * DCH - 1))
                                k += 1
                        last.then_inc(s_full, 1)
                    elif n == "fb.make":
                        pe.wait_ge(s_rep, 1)
                        for j in range(DCH):
                            last = nc.tensor.matmul(ps[:, 4, j * P:(j + 1) * P], v32[:, j * P:(j + 1) * P],
                                                    fbt_rep[:].rearrange("p c r -> p (c r)"), start=True, stop=True)
                        last.then_inc(s_fb_full, 1)
                    elif n == "u.turn":
                        pe.wait_ge(s_urep, 1)
                        for k in range(2):
                            turn(2 * GROUPS + k, lambda m, bank: nc.tensor.transpose(
                                bank.bitcast(BF16)[:, m * P:(m + 1) * P],
                                u_rep[:, 8 * k + m, :, :].rearrange("p c r -> p (c r)"), ident_b[:]))
                    elif what == "side" and n.endswith("turn"):
                        g = int(n[1])
                        if g == 0:
                            pe.wait_ge(s_amax["fb"], 1)
                        pe.wait_ge(s_tern, g + 1)
                        for k in range(2):
                            def square(m, bank):
                                if g < G_FC:
                                    col = (m % 4) * D + (2 * k + m // 4) * P
                                else:
                                    col = (8 * k + m) * P
                                return nc.tensor.transpose(bank.bitcast(F16)[:, m * P:(m + 1) * P],
                                                           tern[:, col:col + P], ident16[:])
                            turn(2 * g + k, square)
                    elif n == "last":
                        pe.wait_ge(s_diag, 1)
                        pe.wait_ge(s_tcopied, 2 * GROUPS + 2)
                        for j in range(DCH):
                            last = nc.tensor.matmul(ps[:, 4, j * P:(j + 1) * P], ones[:], diag[:, j, :], start=True,
                                                    stop=True)
                        last.then_inc(s_bc, 1)

        o_s = kv_w[:].rearrange("p w a c n -> p (w a c n)")[:, 0:2 * ICH * TT].rearrange("p (a c t) -> p a c t", a=2, t=TT)
        xr = stage_b[0:SUB, 0:ST * D].rearrange("p (s d) -> p s d", s=ST)
        x1 = stage_b[0:SUB, ST * D:2 * ST * D].rearrange("p (s d) -> p s d", s=ST)
        xn = ctx_s[0:SUB].rearrange("p a c k -> p (a c k)")[:, 0:2 * ST * D].bitcast(F32).rearrange("p (s d) -> p s d", s=ST)
        s_o_in, s_x, s_xb, s_normed = sem("o_in"), sem("xr_in"), sem("x_plus_bias"), sem("x1_normed")
        s_o = [sem(f"o_stored{n}") for n in range(2)]

        def load_o(sp, i):
            for half in range(2):
                src = o_dram.rearrange("i c p a t -> i a p c t")[i, half]
                sp.dma_start(o_s[:, half, :, :], src).then_inc(s_o_in, 16)

        with ExitStack() as c:
            keys = sb("keys", [P, 2, GH, NK], F16, c)
            vals = sb("vals", [KT, 2, NKT, GH, 2, DH], F16, c)
            q_dup = sb("q_dup", [P, 2, 2, GH, NQ], F16, c)
            probs = sb("probs", [QT, 2, 2, NK], F32, c)
            probs_t = sb("probs_t", [KT, 2, NKT, NQ], F16, c)
            o_low = sb("o_low", [DH, NQ], F32, c)
            o_sum = sb("o_sum", [P, 2, NQ], F32, c)
            o_t = sb("o_t", [P, 2, 2, GH // 2, NQ], F16, c)
            row_max = sb("row_max", [QT, 2], F32, c)
            bias = sb("bias", [QT, 2], F32, c)
            row_sum = sb("row_sum", [QT, 2], F32, c)
            row_inv = sb("row_inv", [QT, 2], F32, c)
            score_scale = sb("score_scale", [P, 2], F32, c)
            c_peaks = sb("c_peaks", [P, CCH], F32, c)
            stats = sb("a_stats", [SUB, ST, 6], F32, c)
            mean_var = sb("a_mean_var", [SUB, ST, 2], F32, c)
            work = sb("a_work", [SUB, 3, ST], F32, c)
            y_bits = sb("a_y", [SUB, ST], I32, c)
            ctx_s1 = sb("ctx_s1", [P, 2, CCH, NK], F16, c)
            ctx_buf = [ctx_s, ctx_s1]

            s_ctx, s_q = sem("ctx_in", c), [sem(f"q_in{n}", c) for n in range(2)]
            s_amax, s_all = sem("ctx_amax", c), sem("ctx_amax_all", c)
            s_own, s_ctx_scale, s_ctx_high = sem("dve_own4", c), sem("ctx_scale", c), sem("ctx_high", c)
            s_ctx_cut, s_peaks = sem("ctx_cut", c), sem("ctx_peaks", c)
            s_scores, s_rowmax, s_bias = sem("scores_full", c), sem("row_max_done", c), sem("bias_ready", c)
            s_exp, s_inv, s_probs = sem("exp_done", c), sem("row_inv_ready", c), sem("probs_ready", c)
            s_full, s_high, s_free = sem("work_full", c), sem("work_high", c), sem("work_free", c)
            s_keys, s_vals = sem("keys_ready", c), sem("vals_ready", c)
            s_set = sem("score_scale_set", c)
            s_ohigh = sem("o_high", c)
            s_pool_passed, s_sp_passed, s_ocut = sem("pool_passed", c), sem("sp_passed", c), sem("o_cut", c)
            s_own_n, s_x1 = sem("dve_own_first_norm", c), sem("x1_half", c)
            RING = 4
            K_UNITS = [[0], [1], [], [2, 3], [4], [], [5], [6, 7]]
            V_UNITS = [[0], [1], [2], [], [3], [4], [5], []]
            CTX_MAX, SCALE_STEP, CTX_CUT = {0: 0, 1: 1, 2: 2}, 3, {4: 0, 5: 1, 6: 2}
            O_UNITS = [[], [0], [1], [2], [3, 4], [5, 6], [7], []]
            NORM_STEP = GH - 1
            N_KU, N_VU = GH, NKT
            PAIRS = GH // 2
            FIRST_USES = N_KU + N_VU

            def steps(fill):
                out = []
                for h in range(GH):
                    out += [(h, "T", g) for g in range(3)]
                    if fill:
                        out += [(h, "K", n) for n in K_UNITS[h]] + [(h, "V", n) for n in V_UNITS[h]]
                    else:
                        out += [(h, "O", n) for n in O_UNITS[h]]
                    out.append((h, "A", 0))
                return out

            USES_GROUP = len(steps(True))
            block = c.enter_context(nc.Block())

            def use_base(i, par):
                return FIRST_USES + 2 * USES_GROUP * i + USES_GROUP * par

            def for_groups(eng, group):
                with eng.Fori(0, B // 2 - 1) as pair:
                    for buf in range(2):
                        for par in range(2):
                            group(pair, buf, par, False)
                for buf in range(2):
                    for par in range(2):
                        group(B // 2 - 1, buf, par, buf == 1)

            def load_q(sp, tile, which, par):
                for half in range(2):
                    for rows in range(2):
                        src = q_dram.rearrange("i (g c) (m d) a (s t) -> i s g a d c m t", g=2, d=DH, s=2)[tile, which, par, half]
                        dst = q_dup[rows * DH:(rows + 1) * DH, par, half, :, :].rearrange("d (c m) t -> d c m t", m=2)
                        for m in range(2):
                            sp.dma_start(dst[:, :, m], src[:, :, m]).then_inc(s_q[par], 16)

            @block.sync
            def _(sp):
                for n in range(2):
                    sp.sem_inc(s_o[n], 32)
                load_q(sp, 0, 0, 0)
                load_q(sp, 0, 0, 1)
                sp.dma_start(ctx32[:], ctx_v[1]).then_inc(s_ctx, 16)

                def group(pair, buf, par, final):
                    i = 2 * pair + buf
                    if par == 1 and not isinstance(i, int):
                        sp.wait_ge(s_ctx_cut, i + 2)
                        sp.dma_start(ctx32[:], ctx_v[i + 2]).then_inc(s_ctx, 16)
                    if not final:
                        sp.wait_ge(s_scores, 2 * (2 * GH * i + GH * par + GH))
                        load_q(sp, pair + buf, 1 - buf, par)
                    if final and par == 0:
                        sp.wait_ge(s_ctx_cut, B)
                        sp.dma_start(xr, x_tiles[0]).then_inc(s_x, 16)
                        sp.wait_ge(s_full, use_base(i, 1))
                        for n in range(2):
                            sp.wait_ge(s_o[n], 32 + 32 * i)
                        load_o(sp, 0)
                    sp.wait_ge(s_ocut, PAIRS * (2 * i + par + 1) + 2)
                    sp.sem_inc(s_sp_passed, 1)
                    for half in range(2):
                        dst = o_dram.rearrange("i (g c) p a (b t) -> i b g a p c t", g=2, b=2)[pair, buf, par, half]
                        sp.dma_start(dst, o_t[:, par, half]).then_inc(s_o[par], 16)

                for_groups(sp, group)

            @block.gpsimd
            def _(pool):
                def wait_counted(sem, value):
                    pool.wait_ge(sem, value)
                    pool.sem_inc(s_pool_passed, 1)

                def reduce_ctx(b):
                    wait_counted(s_amax, b)
                    nc.gpsimd.partition_all_reduce(c_all[:], c_amax[:], P, ABSMAX).then_inc(s_all, 1)

                def normalise(head, par_h):
                    wait_counted(s_inv, head + 1)
                    for t in range(2):
                        nc.gpsimd.tensor_scalar(probs[:, par_h, t, :], probs[:, par_h, t, :], row_inv[:, t:t + 1],
                                                2.0 ** P_EXP, ALU.mult, ALU.mult).then_inc(s_probs, 1)

                def cut_outputs(i, par, c, use):
                    pair = 2 * PAIRS * i + PAIRS * par + c
                    wait_counted(s_free, use)
                    if c == 0:
                        wait_counted(s_o[par], 32 * i + 32)
                    g = nc.gpsimd
                    g.tensor_scalar(o_t[:, par, 0, c, :], o_sum[:, c % 2, :], 1.0, 1.0, ALU.mult,
                                    ALU.mult).then_inc(s_ohigh, 1)
                    wait_counted(s_ohigh, pair + 1)
                    g.tensor_tensor(o_t[:, par, 1, c, :], o_sum[:, c % 2, :], o_t[:, par, 0, c, :],
                                    ALU.subtract).then_inc(s_ocut, 1)

                pool.sem_inc(s_ocut, 2)
                normalise(0, 0)

                def group(pair, buf, par, final):
                    i = 2 * pair + buf
                    fill = not (final and par == 1)
                    for h in range(GH):
                        if fill or h < GH - 1:
                            normalise(2 * GH * i + GH * par + h + 1, (h + 1) % 2)
                        if par == 0 and h == len(CTX_MAX) - 1 and not final:
                            reduce_ctx(i + 1)
                        if final and par == 0 and h >= GH - ST:
                            s = h - (GH - ST)
                            pool.wait_ge(s_x, 16)
                            nc.gpsimd.tensor_tensor(xr[:, s, :], xr[:, s, :], bo_bc[0:SUB, :], ALU.add).then_inc(s_xb, 1)
                        if h % 2 == 1:
                            of_head = [n for n, (hh, kind, _) in enumerate(steps(fill)) if hh == h and kind == "A"][0]
                            cut_outputs(i, par, h // 2, use_base(i, par) + of_head + 1)

                for_groups(pool, group)

            @block.scalar
            def _(act):
                a = nc.scalar

                def exps(head, par_h, t):
                    act.wait_ge(s_bias, head + 1)
                    a.activation(probs[:, par_h, t, :].rearrange("p (n k) -> p n k", n=2), ps[0:QT, 2 * t:2 * t + 2, 0:KH],
                                 ACT.Exp, bias=bias[:, t:t + 1], scale=score_scale[0:QT, 0:1],
                                 accum_out=row_sum[:, t:t + 1]).then_inc(s_exp, 1)

                def high(use, slot, kind, n, par):
                    bank = ps[:, 4 + slot % RING, :]
                    act.wait_ge(s_full, use + 1)
                    if kind == "O":
                        s, cols = n // 2, slice(n % 2 * D // 2, (n % 2 + 1) * D // 2)
                        a.activation(x1[:, s, cols], bank[0:SUB, 0:D // 2], ACT.Copy,
                                     scale=attn_scale[0:SUB, s // 2:s // 2 + 1]).then_inc(s_high, 1)
                    elif kind == "T":
                        a.activation(probs_t[:, 0, 2 * n:2 * n + 2, :], bank[0:KT, 0:2 * NQ].rearrange("p (c q) -> p c q", c=2),
                                     ACT.Copy).then_inc(s_high, 1)
                    elif kind == "K":
                        for hh in range(2):
                            last = a.activation(keys[0:DH, par, 2 * (n // 2) + hh, (n % 2) * KH:(n % 2 + 1) * KH],
                                                bank[hh * DH:(hh + 1) * DH, 0:KH], ACT.Copy, scale=2.0 ** KV_EXP)
                        last.then_inc(s_high, 1)
                    elif kind == "V":
                        a.activation(vals[:, par, n, :, 0, :], bank[0:KT, :].rearrange("p (h d) -> p h d", d=DH),
                                     ACT.Copy, scale=2.0 ** KV_EXP).then_inc(s_high, 1)
                    else:
                        a.activation(o_low[:], bank[DH:P, 0:NQ], ACT.Copy, scale=2.0 ** -P_EXP).then_inc(s_high, 1)

                def cut_ctx(b, part, buf):
                    if part == 0:
                        act.wait_ge(s_ctx_scale, b)
                    a.activation(ctx_buf[buf][:, 0, part], ctx32[:, part], ACT.Copy,
                                 scale=c_scale[:]).then_inc(s_ctx_high, 1)

                for use in range(FIRST_USES):
                    kind, n = ("K", use) if use < N_KU else ("V", use - N_KU)
                    high(use, use, kind, n, 0)
                for t in range(2):
                    exps(0, 0, t)

                def group(pair, buf, par, final):
                    i = 2 * pair + buf
                    fill = not (final and par == 1)
                    slot = FIRST_USES + USES_GROUP * par
                    for n, (h, kind, which) in enumerate(steps(fill)):
                        head = 2 * GH * i + GH * par + h
                        more = fill or h < GH - 1
                        if kind == "T" and which == 0 and par == 0 and h in CTX_CUT and not final:
                            cut_ctx(i + 1, CTX_CUT[h], 1 - buf)
                        high(use_base(i, par) + n, slot + n, kind, which, 1 - par)
                        if kind == "T" and which == 2 and more:
                            for t in range(2):
                                exps(head + 1, (h + 1) % 2, t)

                for_groups(act, group)

            @block.vector
            def _(dve):
                v = nc.vector

                def maxima(head):
                    for t in range(2):
                        dve.wait_ge(s_scores, 2 * head + t + 1)
                        last = v.tensor_reduce(row_max[:, t:t + 1], ps[0:QT, 2 * t:2 * t + 2, 0:KH], AX.XY, ALU.max)
                    last.then_inc(s_rowmax, 1)
                    dve.wait_ge(s_rowmax, head + 1)
                    v.tensor_scalar(bias[:], row_max[:], score_scale[0:QT, 1:2], None, ALU.mult).then_inc(s_bias, 1)

                def inverses(head):
                    dve.wait_ge(s_exp, 2 * head + 2)
                    v.reciprocal(row_inv[:], row_sum[:]).then_inc(s_inv, 1)

                def low(use, slot, kind, n, par, h, opar):
                    bank = ps[:, 4 + slot % RING, :]
                    dve.wait_ge(s_high, use + 1)
                    if kind == "O":
                        s, cols = n // 2, slice(n % 2 * D // 2, (n % 2 + 1) * D // 2)
                        dve.wait_ge(s_xb, s + 1)
                        v.tensor_tensor(x1[:, s, cols], x1[:, s, cols], xr[:, s, cols], ALU.add).then_inc(s_free, 1)
                    elif kind == "T":
                        v.tensor_tensor(probs_t[:, 1, 2 * n:2 * n + 2, :],
                                        bank[0:KT, 0:2 * NQ].rearrange("p (c q) -> p c q", c=2),
                                        probs_t[:, 0, 2 * n:2 * n + 2, :], ALU.subtract).then_inc(s_free, 1)
                    elif kind == "K":
                        for hh in range(2):
                            cols = slice((n % 2) * KH, (n % 2 + 1) * KH)
                            head = 2 * (n // 2) + hh
                            last = v.scalar_tensor_tensor(
                                out=keys[DH:P, par, head, cols], in0=bank[hh * DH:(hh + 1) * DH, 0:KH],
                                scalar=2.0 ** KV_EXP, in1=keys[0:DH, par, head, cols], op0=ALU.mult, op1=ALU.subtract)
                        last.then_inc(s_free, 1)
                    elif kind == "V":
                        v.scalar_tensor_tensor(out=vals[:, par, n, :, 1, :],
                                               in0=bank[0:KT, :].rearrange("p (h d) -> p h d", d=DH),
                                               scalar=2.0 ** KV_EXP, in1=vals[:, par, n, :, 0, :],
                                               op0=ALU.mult, op1=ALU.subtract).then_inc(s_free, 1)
                    else:
                        rows = slice((h % 2) * DH, (h % 2 + 1) * DH)
                        v.scalar_tensor_tensor(out=o_sum[rows, (h // 2) % 2, :], in0=bank[0:DH, 0:NQ],
                                               scalar=2.0 ** -P_EXP, in1=o_low[:],
                                               op0=ALU.mult, op1=ALU.add).then_inc(s_free, 1)

                def scale_ctx(b):
                    own = Own(dve, s_own, POW2_STEPS * (b - 1))
                    dve.wait_ge(s_all, b)
                    pow2_scale(v, own, c_all[:], c_field[:], c_scale[:], c_inv[:])

                def cut_ctx(b, part, buf):
                    dve.wait_ge(s_ctx_high, CCH * (b - 1) + part + 1)
                    cut = v.scalar_tensor_tensor(out=ctx_buf[buf][:, 1, part], in0=ctx32[:, part], scalar=c_scale[:],
                                                 in1=ctx_buf[buf][:, 0, part], op0=ALU.mult, op1=ALU.subtract)
                    if part == CCH - 1:
                        cut.then_inc(s_ctx_cut, 1)

                def amax_ctx(b, part):
                    if part == 0:
                        dve.wait_ge(s_ctx, 16 * b)
                    peak = v.tensor_reduce(c_peaks[:, part:part + 1], ctx32[:, part], AX.X, ALU.max,
                                           apply_absolute_value=True)
                    if part == CCH - 1:
                        peak.then_inc(s_peaks, 1)
                        dve.wait_ge(s_peaks, b)
                        v.tensor_reduce(c_amax[:], c_peaks[:], AX.X, ALU.max).then_inc(s_amax, 1)

                def set_score_scale():
                    v.tensor_scalar(score_scale[:, 0:1], c_inv[:], score_w[:], None, ALU.mult)
                    v.tensor_scalar(score_scale[:, 1:2], c_inv[:], score_w[:], -1.0, ALU.mult, ALU.mult).then_inc(s_set, 1)

                def set_attn_scale(b):
                    v.tensor_scalar(attn_scale[:, bass.ds(b, 1)], c_inv[:], attn_w[:], None, ALU.mult)

                v.memset(bias[:], 0.0).then_inc(s_ctx_cut, 1)
                set_score_scale()
                set_attn_scale(0)
                for use in range(FIRST_USES):
                    kind, n = ("K", use) if use < N_KU else ("V", use - N_KU)
                    low(use, use, kind, n, 0, 0, 0)
                dve.wait_ge(s_set, 1)
                maxima(0)
                inverses(0)

                def group(pair, buf, par, final):
                    i = 2 * pair + buf
                    fill = not (final and par == 1)
                    slot = FIRST_USES + USES_GROUP * par
                    for n, (h, kind, which) in enumerate(steps(fill)):
                        head = 2 * GH * i + GH * par + h
                        more = fill or h < GH - 1
                        if kind == "T" and which == 0 and more:
                            if par == 1 and h == GH - 1:
                                set_score_scale()
                                dve.wait_ge(s_set, i + 2)
                            maxima(head + 1)
                        if kind == "A":
                            if h % 2 == 0:
                                dve.wait_ge(s_ocut, 2 * PAIRS * i + PAIRS * par + h // 2 + 1)
                        low(use_base(i, par) + n, slot + n, kind, which, 1 - par, h, par)
                        if kind == "O" and which % 2 == 1:
                            dve.wait_ge(s_free, use_base(i, par) + n + 1)
                            v.bn_stats(stats[:, which // 2, :], x1[:, which // 2, :]).then_inc(s_x1, 1)
                        if kind == "T" and which == 2 and not fill and h == NORM_STEP:
                            dve.wait_ge(s_x1, ST)
                            own = Own(dve, s_own_n)
                            own(row_factors(v, own, None, stats, mean_var, work, y_bits[:]))
                            normalise_rows(v, x1, work, y_bits[:], xn, range(ST)).then_inc(s_normed, 1)
                        if kind == "T" and which == 2 and more:
                            inverses(head + 1)
                        if kind == "T" and which == 2 and par == 0 and not final:
                            if h in CTX_MAX:
                                amax_ctx(i + 1, CTX_MAX[h])
                            elif h == SCALE_STEP:
                                scale_ctx(i + 1)
                                set_attn_scale(i + 1)
                                v.memset(c_amax[:], 0.0).then_inc(s_ctx_scale, 1)
                            elif h in CTX_CUT:
                                cut_ctx(i + 1, CTX_CUT[h], 1 - buf)

                for_groups(dve, group)

            @block.tensor
            def _(pe):
                mm = nc.tensor.matmul

                def scores(head, par, h, t, first):
                    if not first:
                        pe.wait_ge(s_exp, 2 * head + t - 1)
                    for half in range(2):
                        for n in range(2):
                            last = mm(ps[0:QT, 2 * t + n, 0:KH], q_dup[:, par, half, h, t * QT:(t + 1) * QT],
                                      keys[:, par, h, n * KH:(n + 1) * KH], start=(half == 0), stop=(half == 1))
                    last.then_inc(s_scores, 1)

                def project_keys(slot, n, par, buf):
                    bank = ps[:, 4 + slot % RING, 0:KH]
                    col = (par * GH + 2 * (n // 2)) * DH
                    k = 0
                    for wh, xh in ((0, 0), (0, 1), (1, 0)):
                        for d in range(CCH):
                            last = mm(bank, wk_s[:, wh, d, col:col + P],
                                      ctx_buf[buf][:, xh, d, (n % 2) * KH:(n % 2 + 1) * KH],
                                      start=(k == 0), stop=(k == 3 * CCH - 1))
                            k += 1
                    last.then_inc(s_full, 1)

                def project_values(slot, n, par, buf):
                    bank = ps[0:KT, 4 + slot % RING, :]
                    k = 0
                    for wh, xh in ((0, 0), (1, 0), (0, 1)):
                        for d in range(CCH):
                            last = mm(bank, ctx_buf[buf][:, xh, d, n * KT:(n + 1) * KT],
                                      wv_s[:, wh, d, par * GH * DH:(par + 1) * GH * DH],
                                      start=(k == 0), stop=(k == 3 * CCH - 1))
                            k += 1
                    last.then_inc(s_full, 1)

                for use in range(FIRST_USES):
                    if use >= RING:
                        pe.wait_ge(s_free, use - RING + 1)
                    if use < N_KU:
                        project_keys(use, use, 0, 0)
                    else:
                        project_values(use, use - N_KU, 0, 0)
                pe.wait_ge(s_q[0], 128)
                pe.wait_ge(s_free, 2)
                for t in range(2):
                    scores(0, 0, 0, t, True)

                def group(pair, buf, par, final):
                    i = 2 * pair + buf
                    fill = not (final and par == 1)
                    slot = FIRST_USES + USES_GROUP * par
                    base = use_base(i, par)
                    k_use = {}
                    for n, (h, kind, which) in enumerate(steps(fill)):
                        head = 2 * GH * i + GH * par + h
                        use = base + n
                        if kind == "T" and which == 0:
                            if h < GH - 1:
                                for t in range(2):
                                    scores(head + 1, par, h + 1, t, False)
                            elif fill:
                                pe.wait_ge(s_free, base + k_use[1] + 1)
                                pe.wait_ge(s_q[1 - par], 128 * (i + 1 + par))
                                for t in range(2):
                                    scores(head + 1, 1 - par, 0, t, False)
                            pe.wait_ge(s_probs, 2 * head + 2)
                        if h == 0 and kind == "K" and par == 1:
                            pe.wait_ge(s_ctx_cut, i + 2)
                        pe.wait_ge(s_free, use - RING + 1)
                        if kind == "K":
                            k_use[which] = n
                            project_keys(slot + n, which, 1 - par, (buf + par) % 2)
                        elif kind == "V":
                            project_values(slot + n, which, 1 - par, (buf + par) % 2)
                        elif kind == "O":
                            if which == 0:
                                pe.wait_ge(s_o_in, 32)
                            s, cols = which // 2, slice(which % 2 * D // 2, (which % 2 + 1) * D // 2)
                            k = 0
                            for oh, wh in ((0, 0), (0, 1), (1, 0)):
                                for d in range(ICH):
                                    last_mm = mm(ps[0:SUB, 4 + (slot + n) % RING, 0:D // 2],
                                                 o_s[:, oh, d, s * SUB:(s + 1) * SUB], wo_s[:, wh, d, cols],
                                                 start=(k == 0), stop=(k == 3 * ICH - 1))
                                    k += 1
                            last_mm.then_inc(s_full, 1)
                        elif kind == "T":
                            bank = ps[:, 4 + (slot + n) % RING, :]
                            for k in range(2):
                                for t in range(2):
                                    last_mm = nc.tensor.transpose(
                                        bank[0:KT, k * NQ + t * QT:k * NQ + (t + 1) * QT],
                                        probs[:, h % 2, t, (2 * which + k) * KT:(2 * which + k + 1) * KT],
                                        ident[0:QT, 0:QT])
                            last_mm.then_inc(s_full, 1)
                            t_use = n
                        else:
                            pe.wait_ge(s_free, base + t_use + 1)
                            k = 0
                            for kt in range(NKT):
                                for half in range(2):
                                    last_mm = mm(ps[:, 4 + (slot + n) % RING, 0:NQ],
                                                 vals[:, par, kt, h, :, :].rearrange("p a d -> p (a d)"),
                                                 probs_t[:, half, kt, :], start=(k == 0), stop=(k == 2 * NKT - 1))
                                    k += 1
                            last_mm.then_inc(s_full, 1)

                for_groups(pe, group)

        with ExitStack() as c:
            res = sb("res", [SUB, ST, D], F32, c)
            xT = sb("xT2", [P, 2, DCH, TT], F16, c)
            r = sb("r", [P, HCH, TT], F32, c)
            r_s = r[:].bitcast(F16).rearrange("p j (a t) -> p j a t", a=2)
            SQN = 4
            sq = sb("sq", [P, SQN, TT], F32, c)
            z32 = sb("z32", [P, TT], F32, c)
            z_part = [sb(f"z_part{n}", [P, TT], BF16, c) for n in range(2)]
            z_rest = [sb(f"z_rest{n}", [P, TT], F32, c) for n in range(2)]
            z_acc = sb("z_acc", [P, TT], F32, c)
            z = sb("z", [P, TT], BF16, c)
            y_out = sb("y_out", [SUB, ST, D], F32, c)
            stats = sb("f_stats", [SUB, ST, 6], F32, c)
            mean_var = sb("f_mean_var", [SUB, ST, 2], F32, c)
            work = sb("f_work", [SUB, 3, ST], F32, c)
            y_bits = sb("f_y", [SUB, ST], I32, c)
            r_amax = sb("r_amax", [P, HCH], F32, c)
            r_amax1 = sb("r_amax1", [P, 1], F32, c)
            r_all = sb("r_all", [P, 1], F32, c)
            fld = sb("fld", [P, 1], I32, c)
            g_scale = sb("g_scale", [P, 1], F32, c)
            g_inv = sb("g_inv", [P, 1], F32, c)

            s_ysub = sem("y_subtile_ready", c)
            s_y, s_res = sem("y_stored", c), sem("res_kept", c)
            s_own_t, s_own_z, s_own_r = sem("dve_own_norm", c), sem("dve_own_z", c), sem("dve_own_r", c)
            s_full, s_free, s_thigh = sem("a_full", c), sem("a_free", c), sem("t_high", c)
            s_zfull, s_z32, s_zready = sem("z_full", c), sem("z32_ready", c), sem("z_ready", c)
            s_fc, s_relu = sem("fc_full", c), sem("relu_done", c)
            s_ramax, s_rall, s_rscale = sem("r_amax_s", c), sem("r_all_s", c), sem("r_scale_s", c)
            s_sq, s_rhigh, s_rlow = sem("squared", c), sem("r_high", c), sem("r_low", c)
            s_norm_passed = sem("norm_passed", c)
            s_yout, s_pool_passed = sem("y_ready", c), sem("pool_passed3", c)
            RING_A, RING_B, USES_A, Z_STEPS = 3, 4, 3 * ST, 6
            Z_LATE = 3
            RESIDUAL_FROM = 5
            block = c.enter_context(nc.Block())

            def use_o(i, n):
                return (ST + n, ST + USES_A * (i - 1) + n)

            def use_t(i, n):
                return (n, n) if isinstance(i, int) and i == 0 else (3 * ST + n, 3 * ST + USES_A * (i - 1) + n)

            def use_y(i, n, last):
                first = ST if last else 2 * ST
                return (first + n, first + USES_A * i + n)

            def for_tiles(eng, tile):
                with eng.Fori(0, NTILES - 1) as i:
                    tile(i, False)
                tile(NTILES - 1, True)

            @block.sync
            def _(sp):
                for n in range(2):
                    sp.wait_ge(s_o[n], 32 + 32 * B)
                sp.sem_inc(s_y, 16)

                def tile(i, last):
                    if not last:
                        sp.wait_ge(s_normed, i + 1)
                        load_o(sp, i + 1)
                        sp.dma_start(xr, x_tiles[i + 1]).then_inc(s_x, 16)
                    if last:
                        for s in range(ST):
                            sp.wait_ge(s_ysub, s + 1)
                            sp.dma_start(out_tiles[i][:, s, :], y_out[:, s, :]).then_inc(s_y, 16)
                    else:
                        sp.wait_ge(s_yout, i + 2)
                        sp.dma_start(out_tiles[i], y_out[:]).then_inc(s_y, 16)

                for_tiles(sp, tile)
                sp.wait_ge(s_y, 16 * NTILES + 16 * ST)

            @block.gpsimd
            def _(pool):
                g = nc.gpsimd

                def wait_counted(sem, value):
                    pool.wait_ge(sem, value)
                    pool.sem_inc(s_pool_passed, 1)

                def add_bias(i):
                    wait_counted(s_x, 16 * (i + 1))
                    for s in range(ST):
                        last = g.tensor_tensor(xr[:, s, :], xr[:, s, :], bo_bc[0:SUB, :], ALU.add)
                    last.then_inc(s_xb, 1)

                pool.sem_inc(s_rlow, SQN)

                def tile(i, last):
                    wait_counted(s_normed, i + 1)
                    wait_counted(s_yout, i + 1)
                    g.tensor_scalar(res[:], x1[:], 1.0, 1.0, ALU.mult, ALU.mult).then_inc(s_res, 1)
                    wait_counted(s_ramax, i + 1)
                    g.partition_all_reduce(r_all[:], r_amax1[:], P, ABSMAX).then_inc(s_rall, 1)
                    if not last:
                        add_bias(i + 1)
                    for j in range(HCH):
                        wait_counted(s_rhigh, HCH * i + j + 1)
                        g.tensor_tensor(r_s[:, j, 1, :], sq[:, j % SQN, :], r_s[:, j, 0, :],
                                        ALU.subtract).then_inc(s_rlow, 1)

                for_tiles(pool, tile)

            @block.scalar
            def _(act):
                a = nc.scalar

                def transposed(i):
                    for d in range(DCH):
                        turn, use = use_t(i, d)
                        act.wait_ge(s_full, use + 1)
                        a.activation(xT[:, 0, d, :], ps[:, turn % RING_A, 0:TT], ACT.Copy,
                                     scale=2.0 ** X_EXP).then_inc(s_thigh, 1)
                    act.wait_ge(s_zfull, i + 1)
                    a.activation(z32[:], ps[:, 7, 0:TT], ACT.Copy, scale=z_scale[:]).then_inc(s_z32, 1)

                transposed(0)
                act.sem_inc(s_relu, RING_B)

                def tile(i, last):
                    for j in range(HCH):
                        act.wait_ge(s_fc, HCH * i + j + 1)
                        a.activation(r[:, j, :], ps[:, 3 + j % RING_B, 0:TT], ACT.Relu,
                                     scale=relu_scale[:, j:j + 1]).then_inc(s_relu, 1)
                    act.wait_ge(s_rscale, i + 1)
                    for j in range(HCH):
                        act.wait_ge(s_rlow, HCH * i + j + 1)
                        a.activation(sq[:, j % SQN, :], r[:, j, :], ACT.Square, scale=g_scale[:]).then_inc(s_sq, 1)
                    if not last:
                        transposed(i + 1)

                for_tiles(act, tile)

            @block.vector
            def _(dve):
                v = nc.vector

                def residual(i, s):
                    if s == 0:
                        dve.wait_ge(s_xb, ST + i)
                        dve.wait_ge(s_res, i)
                    turn, use = use_o(i, s)
                    dve.wait_ge(s_full, use + 1)
                    v.scalar_tensor_tensor(out=x1[:, s, :], in0=ps[0:SUB, turn % RING_A, :],
                                           scalar=attn_scale[0:SUB, bass.ds(2 * i + s // 2, 1)],
                                           in1=xr[:, s, :], op0=ALU.mult, op1=ALU.add).then_inc(s_free, 1)
                    dve.wait_ge(s_free, use + 1)
                    return v.bn_stats(stats[:, s, :], x1[:, s, :])

                def normalise(i, last):
                    own = Own(dve, s_own_t, (NORM_STEPS + 1) * (i - 1))
                    own(row_factors(v, own, last, stats, mean_var, work, y_bits[:], s_norm_passed))
                    normalise_rows(v, x1, work, y_bits[:], xn, range(ST)).then_inc(s_normed, 1)

                def transposed(i):
                    for d in range(DCH):
                        turn, use = use_t(i, d)
                        dve.wait_ge(s_thigh, DCH * i + d + 1)
                        v.scalar_tensor_tensor(out=xT[:, 1, d, :], in0=ps[:, turn % RING_A, 0:TT], scalar=2.0 ** X_EXP,
                                               in1=xT[:, 0, d, :], op0=ALU.mult, op1=ALU.subtract).then_inc(s_free, 1)
                    own = Own(dve, s_own_z, Z_STEPS * i)
                    dve.wait_ge(s_z32, i + 1)
                    own(v.tensor_copy(z_part[0][:], z32[:]))
                    own(v.tensor_tensor(z_rest[0][:], z32[:], z_part[0][:], ALU.subtract))
                    own(v.tensor_copy(z_part[1][:], z_rest[0][:]))
                    own(v.tensor_tensor(z_rest[1][:], z_rest[0][:], z_part[1][:], ALU.subtract))
                    own(v.tensor_scalar(z_acc[:], z_part[0][:], masks[:, 0:1], None, ALU.mult))
                    own(v.scalar_tensor_tensor(out=z_acc[:], in0=z_part[1][:], scalar=masks[:, 1:2], in1=z_acc[:],
                                               op0=ALU.mult, op1=ALU.add))
                    v.scalar_tensor_tensor(out=z[:], in0=z_rest[1][:], scalar=masks[:, 2:3], in1=z_acc[:],
                                           op0=ALU.mult, op1=ALU.add).then_inc(s_zready, 1)

                transposed(0)
                v.memset(r_amax1[:], 0.0).then_inc(s_yout, 1)

                def tile(i, last):
                    for j in range(HCH):
                        dve.wait_ge(s_relu, HCH * i + j + 1 + RING_B)
                        peak = v.tensor_reduce(r_amax[:, j:j + 1], r[:, j, :], AX.X, ALU.max)
                    own = Own(dve, s_own_r, (1 + POW2_STEPS) * i)
                    own(peak)
                    v.tensor_reduce(r_amax1[:], r_amax[:], AX.X, ALU.max).then_inc(s_ramax, 1)
                    dve.wait_ge(s_rall, i + 1)
                    pow2_scale(v, own, r_all[:], fld[:], g_scale[:], g_inv[:], 260)
                    v.tensor_tensor(g_inv[:], g_inv[:], g_inv[:], ALU.mult).then_inc(s_rscale, 1)
                    for j in range(HCH):
                        dve.wait_ge(s_sq, HCH * i + j + 1)
                        v.tensor_copy(r_s[:, j, 0, :], sq[:, j % SQN, :]).then_inc(s_rhigh, 1)
                        if not last and j >= RESIDUAL_FROM and (j - RESIDUAL_FROM) % 4 == 0:
                            stats_of = residual(i + 1, (j - RESIDUAL_FROM) // 4)
                    if not last:
                        stats_of = residual(i + 1, ST - 1)
                        normalise(i + 1, stats_of)
                    dve.wait_ge(s_res, i + 1)
                    dve.wait_ge(s_y, 16 * i + 16)
                    for s in range(ST):
                        turn, use = use_y(i, s, last)
                        dve.wait_ge(s_full, use + 1)
                        v.scalar_tensor_tensor(out=y_out[:, s, :], in0=ps[0:SUB, turn % RING_A, :], scalar=g_inv[0:SUB, :],
                                               in1=proj_bc[0:SUB, :], op0=ALU.mult, op1=ALU.mult).then_inc(s_free, 1)
                        dve.wait_ge(s_free, use + 1)
                        total = v.tensor_tensor(y_out[:, s, :], y_out[:, s, :], res[:, s, :], ALU.add)
                        if last:
                            total.then_inc(s_ysub, 1)
                    if not last:
                        total.then_inc(s_yout, 1)
                    if not last:
                        transposed(i + 1)

                for_tiles(dve, tile)

            @block.tensor
            def _(pe):
                mm = nc.tensor.matmul

                def bank_a(turn_use):
                    turn, use = turn_use
                    if turn >= RING_A:
                        pe.wait_ge(s_free, use - RING_A + 1)
                    return ps[:, turn % RING_A, :]

                def project(i):
                    pe.wait_ge(s_o_in, 32 * (i + 1))
                    for s in range(ST):
                        bank = bank_a(use_o(i, s))
                        k = 0
                        for oh, wh in ((0, 0), (0, 1), (1, 0)):
                            for d in range(ICH):
                                last = mm(bank[0:SUB, :], o_s[:, oh, d, s * SUB:(s + 1) * SUB], wo_s[:, wh, d, :],
                                          start=(k == 0), stop=(k == 3 * ICH - 1))
                                k += 1
                        last.then_inc(s_full, 1)

                def transposes(i):
                    pe.wait_ge(s_normed, i + 1)
                    for d in range(DCH):
                        bank = bank_a(use_t(i, d))
                        for s in range(ST):
                            last = nc.tensor.transpose(bank[:, s * SUB:(s + 1) * SUB], xn[:, s, d * P:(d + 1) * P],
                                                       ident[0:SUB, 0:SUB])
                        last.then_inc(s_full, 1)
                    pe.wait_ge(s_thigh, DCH * (i + 1))
                    if not (isinstance(i, int) and i == 0):
                        pe.wait_ge(s_z32, i)
                    k = 0
                    for wh, xh in ((0, 0), (1, 0), (0, 1)):
                        if xh == 1:
                            pe.wait_ge(s_free, use_t(i, DCH - 1)[1] + 1)
                        for d in range(DCH):
                            last = mm(ps[:, 7, 0:TT], fb_s[:, wh, d, :], xT[:, xh, d, :], start=(k == 0),
                                      stop=(k == 3 * DCH - 1))
                            k += 1
                    last.then_inc(s_zfull, 1)

                def hidden(i):
                    def bank_b(j):
                        return ps[:, 3 + j % RING_B, 0:TT]

                    def slow(j):
                        pe.wait_ge(s_relu, HCH * i + j + 1)
                        for k in range(2 * DCH):
                            mm(bank_b(j), fc_t[:, k % DCH, j * P:(j + 1) * P], xT[:, k // DCH, k % DCH, :],
                               start=(k == 0), stop=False)

                    def fast(j):
                        mm(bank_b(j), u_t[:, j * P:(j + 1) * P], z[:], start=False, stop=True).then_inc(s_fc, 1)

                    for j in range(Z_LATE):
                        slow(j)
                    pe.wait_ge(s_zready, i + 1)
                    for j in range(Z_LATE):
                        fast(j)
                    for j in range(Z_LATE, HCH):
                        slow(j)
                        fast(j)

                def result(i, last_tile):
                    for s in range(ST):
                        bank = bank_a(use_y(i, s, last_tile))
                        for j in range(HCH):
                            if s == 0:
                                pe.wait_ge(s_rlow, HCH * i + j + 1 + SQN)
                            for half in range(2):
                                last = mm(bank[0:SUB, :], r_s[:, j, half, s * SUB:(s + 1) * SUB], proj_t[:, j, :],
                                          start=(j == 0 and half == 0), stop=(j == HCH - 1 and half == 1))
                        last.then_inc(s_full, 1)

                transposes(0)

                def tile(i, last):
                    hidden(i)
                    if not last:
                        project(i + 1)
                    result(i, last)
                    if not last:
                        transposes(i + 1)

                for_tiles(pe, tile)


def kernel(x, ctx_768, g_xattn, g_ffn, L0_xattn_Wq, L0_xattn_Wk, L0_xattn_Wv, L0_xattn_Wo, L0_xattn_bo,
           L0_ffn_fast_b, L0_ffn_w_fc, L0_ffn_w_proj, L0_ffn_u, L0_ffn_v, L0_ffn_gate):
    import concourse.bacc as bacc
    from concourse.bass_utils import run_bass_kernel_spmd

    laid = {
        "x": np.ascontiguousarray(np.asarray(x).reshape(T, D)),
        "ctx_t": np.ascontiguousarray(np.asarray(ctx_768).transpose(0, 2, 1)),
        "g_xattn": np.asarray(g_xattn).reshape(1, 1),
        "g_ffn": np.asarray(g_ffn).reshape(1, 1),
        "wq": np.ascontiguousarray(L0_xattn_Wq),
        "wk": np.ascontiguousarray(L0_xattn_Wk),
        "wv": np.ascontiguousarray(L0_xattn_Wv),
        "wo": np.ascontiguousarray(L0_xattn_Wo),
        "bo": np.asarray(L0_xattn_bo).reshape(1, D),
        "fast_b_t": np.ascontiguousarray(np.asarray(L0_ffn_fast_b).T),
        "w_fc": np.ascontiguousarray(L0_ffn_w_fc),
        "w_proj": np.ascontiguousarray(L0_ffn_w_proj),
        "u": np.ascontiguousarray(L0_ffn_u),
        "v_low": np.ascontiguousarray(L0_ffn_v),
        "gate": np.asarray(L0_ffn_gate).reshape(1, 1),
    }
    nc = bacc.Bacc("TRN2", target_bir_lowering=False, num_devices=1)
    args = {n: nc.dram_tensor(f"in_{n}", a.shape, mybir.dt.from_np(a.dtype), kind="ExternalInput").ap()
            for n, a in laid.items()}
    out = nc.dram_tensor("out", (T, D), F32, kind="ExternalOutput").ap()
    flamingo_block(nc, out=out, **args)
    ran = run_bass_kernel_spmd(nc, [{f"in_{n}": a for n, a in laid.items()}], core_ids=[0])
    return ran.results[0]["out"].reshape(B, NQ, D)
```
